# Optimizing a Trainium2 kernel written in Bass

```python
import numpy as np
import jax
import jax.numpy as jnp

def _softmax(x, axis=-1):
    return jax.nn.softmax(x, axis=axis)

def _gelu(x):
    return jax.nn.gelu(x, approximate=True)

def _silu(x):
    return jax.nn.silu(x)

def _sigmoid(x):
    return jax.nn.sigmoid(x)

def _layernorm(x, axis=-1, eps=1e-05):
    m = jnp.mean(x, axis=axis, keepdims=True)
    v = jnp.var(x, axis=axis, keepdims=True)
    return (x - m) / jnp.sqrt(v + eps)

def _scatter_add(tgt, idx, src, axis=0):
    return tgt.at[idx].add(src)

def _segment_sum(src, seg, n):
    return jax.ops.segment_sum(src, seg, n)
kernel_name = 'mk_macaron_d2_jaxref_r8_228135'

def setup_inputs(seed: int=0):
    np.random.seed(seed)
    _w = jnp.asarray

    def _L0_attn_setup():
        import jax, jax.numpy as jnp
        import numpy as np
        from math import log2, floor
        HEADS = 16
        DIM_HEAD = 64
        SCALE = DIM_HEAD ** (-0.5)

        def _get_slopes(heads):

            def pow2_slopes(n):
                start = 2 ** (-2 ** (-(log2(n) - 3)))
                return [start * start ** i for i in range(n)]
            if log2(heads).is_integer():
                return pow2_slopes(heads)
            c = 2 ** floor(log2(heads))
            return pow2_slopes(c) + pow2_slopes(2 * c)[0::2][:heads - c]
        key = jax.random.key(seed)
        k1, k2, k3 = jax.random.split(key, 3)
        b, n, dim = (2, 256, 128)
        inner = HEADS * DIM_HEAD
        x = jax.random.normal(k1, (b, n, dim), dtype=jnp.float32)
        w_qkv = jax.random.normal(k2, (dim, 3 * inner), dtype=jnp.float32) * dim ** (-0.5)
        w_out = jax.random.normal(k3, (inner, dim), dtype=jnp.float32) * inner ** (-0.5)
        b_out = jnp.zeros((dim,), dtype=jnp.float32)
        return {'x': x, 'w_qkv': w_qkv, 'w_out': w_out, 'b_out': b_out}
    _L0_attn_in = _L0_attn_setup()

    def _L0_ffn_setup():
        import jax, jax.numpy as jnp
        import numpy as np
        B, SEQ, DIM = (2, 512, 128)
        E, S = (8, 64)
        HID = 4 * DIM
        SCALE = DIM ** 0.5

        def rmsnorm(x, gamma):
            n = jnp.linalg.norm(x, axis=-1, keepdims=True)
            return x / jnp.maximum(n, 1e-12) * SCALE * gamma
        key = jax.random.key(seed)
        ks = jax.random.split(key, 4)
        w_init = lambda k, shape: jax.random.normal(k, shape, dtype=jnp.float32) * 0.02
        return {'x': jax.random.normal(ks[0], (B, SEQ, DIM), dtype=jnp.float32), 'norm_gamma': jnp.ones((DIM,), jnp.float32), 'slot_norm_gamma': jnp.ones((DIM,), jnp.float32), 'slot_embeds': jax.random.normal(ks[1], (E, S, DIM), dtype=jnp.float32), 'w1': w_init(ks[2], (E, DIM, HID)), 'b1': jnp.zeros((E, HID), jnp.float32), 'w2': w_init(ks[3], (E, HID, DIM)), 'b2': jnp.zeros((E, DIM), jnp.float32)}
    _L0_ffn_in = _L0_ffn_setup()

    def _L1_attn_setup():
        import jax, jax.numpy as jnp
        import numpy as np
        B, T, C = (64, 32, 128)
        N_HEAD, HEAD_SIZE, KV_RANK = (16, 64, 128)
        BLOCK_SIZE = 32
        key = jax.random.key(seed)
        ks = jax.random.split(key, 5)
        HD = N_HEAD * HEAD_SIZE

        def init(k, shape):
            fan_in = shape[0]
            bound = 1.0 / np.sqrt(fan_in)
            return jax.random.uniform(k, shape, jnp.float32, -bound, bound)
        return {'x': jax.random.normal(ks[0], (B, T, C), jnp.float32), 'w_kv_down': init(ks[1], (C, KV_RANK)), 'w_kv_up': init(ks[2], (KV_RANK, 2 * HD)), 'w_q': init(ks[3], (C, HD)), 'w_out': init(ks[4], (HD, C))}
    _L1_attn_in = _L1_attn_setup()

    def _L1_ffn_setup():
        import jax, jax.numpy as jnp
        import numpy as np
        B, T, H = (8, 256, 128)
        F = 512
        E = 8
        TOP_K = 2
        key = jax.random.key(seed)
        ks = jax.random.split(key, 6)
        s_h = 1.0 / np.sqrt(H)
        s_f = 1.0 / np.sqrt(F)
        return {'hidden_states': jax.random.normal(ks[0], (B, T, H), dtype=jnp.float32), 'gate_w': jax.random.uniform(ks[1], (H, E), minval=-s_h, maxval=s_h, dtype=jnp.float32), 'w1': jax.random.uniform(ks[2], (E, H, F), minval=-s_h, maxval=s_h, dtype=jnp.float32), 'b1': jax.random.uniform(ks[3], (E, F), minval=-s_h, maxval=s_h, dtype=jnp.float32), 'w2': jax.random.uniform(ks[4], (E, F, H), minval=-s_f, maxval=s_f, dtype=jnp.float32), 'b2': jax.random.uniform(ks[5], (E, H), minval=-s_f, maxval=s_f, dtype=jnp.float32)}
    _L1_ffn_in = _L1_ffn_setup()
    _d = {'L0_attn_x': _L0_attn_in['x'], 'L0_attn_w_qkv': _L0_attn_in['w_qkv'], 'L0_attn_w_out': _L0_attn_in['w_out'], 'L0_attn_b_out': _L0_attn_in['b_out'], 'L0_ffn_norm_gamma': _L0_ffn_in['norm_gamma'], 'L0_ffn_slot_norm_gamma': _L0_ffn_in['slot_norm_gamma'], 'L0_ffn_slot_embeds': _L0_ffn_in['slot_embeds'], 'L0_ffn_w1': _L0_ffn_in['w1'], 'L0_ffn_b1': _L0_ffn_in['b1'], 'L0_ffn_w2': _L0_ffn_in['w2'], 'L0_ffn_b2': _L0_ffn_in['b2'], 'L1_attn_w_kv_down': _L1_attn_in['w_kv_down'], 'L1_attn_w_kv_up': _L1_attn_in['w_kv_up'], 'L1_attn_w_q': _L1_attn_in['w_q'], 'L1_attn_w_out': _L1_attn_in['w_out'], 'L1_ffn_gate_w': _L1_ffn_in['gate_w'], 'L1_ffn_w1': _L1_ffn_in['w1'], 'L1_ffn_b1': _L1_ffn_in['b1'], 'L1_ffn_w2': _L1_ffn_in['w2'], 'L1_ffn_b2': _L1_ffn_in['b2']}
    _x0 = _d['L0_attn_x']
    _d['L0_attn_x'] = jax.random.normal(jax.random.fold_in(jax.random.key(seed), 1), (8, 512, 128), dtype=_x0.dtype)
    del _x0
    return _d

def reference(L0_attn_x, L0_attn_w_qkv, L0_attn_w_out, L0_attn_b_out, L0_ffn_norm_gamma, L0_ffn_slot_norm_gamma, L0_ffn_slot_embeds, L0_ffn_w1, L0_ffn_b1, L0_ffn_w2, L0_ffn_b2, L1_attn_w_kv_down, L1_attn_w_kv_up, L1_attn_w_q, L1_attn_w_out, L1_ffn_gate_w, L1_ffn_w1, L1_ffn_b1, L1_ffn_w2, L1_ffn_b2):

    def _L0_attn_ref(x, w_qkv, w_out, b_out):
        import jax, jax.numpy as jnp
        import numpy as np
        from math import log2, floor
        HEADS = 16
        DIM_HEAD = 64
        SCALE = DIM_HEAD ** (-0.5)

        def _get_slopes(heads):

            def pow2_slopes(n):
                start = 2 ** (-2 ** (-(log2(n) - 3)))
                return [start * start ** i for i in range(n)]
            if log2(heads).is_integer():
                return pow2_slopes(heads)
            c = 2 ** floor(log2(heads))
            return pow2_slopes(c) + pow2_slopes(2 * c)[0::2][:heads - c]
        b, n, _ = x.shape
        qkv = x @ w_qkv
        q, k, v = jnp.split(qkv, 3, axis=-1)

        def to_heads(t):
            return t.reshape(b, n, HEADS, DIM_HEAD).transpose(0, 2, 1, 3)
        q, k, v = map(to_heads, (q, k, v))
        q = q * SCALE
        sim = jnp.einsum('bhid,bhjd->bhij', q, k)
        slopes = jnp.asarray(_get_slopes(HEADS), dtype=sim.dtype)[:, None, None]
        i = jnp.arange(n)
        rel = -jnp.abs(i[None, :] - i[:, None]).astype(sim.dtype)
        sim = sim + rel[None, :, :] * slopes
        causal = jnp.triu(jnp.ones((n, n), dtype=bool), 1)
        mask_value = -jnp.finfo(sim.dtype).max
        sim = jnp.where(causal, mask_value, sim)
        attn = jax.nn.softmax(sim, axis=-1)
        out = jnp.einsum('bhij,bhjd->bhid', attn, v)
        out = out.transpose(0, 2, 1, 3).reshape(b, n, HEADS * DIM_HEAD)
        return out @ w_out + b_out

    def _L0_ffn_ref(x, norm_gamma, slot_norm_gamma, slot_embeds, w1, b1, w2, b2):
        import jax, jax.numpy as jnp
        import numpy as np
        B, SEQ, DIM = (2, 512, 128)
        E, S = (8, 64)
        HID = 4 * DIM
        SCALE = DIM ** 0.5

        def rmsnorm(x, gamma):
            n = jnp.linalg.norm(x, axis=-1, keepdims=True)
            return x / jnp.maximum(n, 1e-12) * SCALE * gamma
        xn = rmsnorm(x, norm_gamma)
        sn = rmsnorm(slot_embeds, slot_norm_gamma)
        logits = jnp.einsum('bnd,esd->bnes', xn, sn)
        dispatch = jax.nn.softmax(logits, axis=1)
        b, n, e, s = logits.shape
        combine = jax.nn.softmax(logits.reshape(b, n, e * s), axis=-1)
        slots = jnp.einsum('bnd,bnes->besd', xn, dispatch)
        h = jnp.einsum('besd,edh->besh', slots, w1) + b1[None, :, None, :]
        h = jax.nn.gelu(h, approximate=False)
        eo = jnp.einsum('besh,ehd->besd', h, w2) + b2[None, :, None, :]
        eo = eo.reshape(b, e * s, DIM)
        out = jnp.einsum('bmd,bnm->bnd', eo, combine)
        return out

    def _L1_attn_ref(x, w_kv_down, w_kv_up, w_q, w_out):
        import jax, jax.numpy as jnp
        import numpy as np
        B, T, C = (64, 32, 128)
        N_HEAD, HEAD_SIZE, KV_RANK = (16, 64, 128)
        BLOCK_SIZE = 32
        Bx, Tx, Cx = x.shape
        HD = N_HEAD * HEAD_SIZE
        latent_kv = x @ w_kv_down
        kv = latent_kv @ w_kv_up
        k, v = (kv[..., :HD], kv[..., HD:])
        k = k.reshape(Bx, Tx, N_HEAD, HEAD_SIZE)
        v = v.reshape(Bx, Tx, N_HEAD, HEAD_SIZE)
        q = (x @ w_q).reshape(Bx, Tx, N_HEAD, HEAD_SIZE)
        scale = HEAD_SIZE ** (-0.5)
        att = jnp.einsum('bqhd,bkhd->bhqk', q, k) * scale
        causal = jnp.tril(jnp.ones((Tx, Tx), dtype=bool))
        att = jnp.where(causal, att, -jnp.inf)
        att = jax.nn.softmax(att, axis=-1)
        y = jnp.einsum('bhqk,bkhd->bqhd', att, v)
        y = y.reshape(Bx, Tx, HD)
        return y @ w_out

    def _L1_ffn_ref(hidden_states, gate_w, w1, b1, w2, b2):
        import jax, jax.numpy as jnp
        import numpy as np
        B, T, H = (8, 256, 128)
        F = 512
        E = 8
        TOP_K = 2
        b, t, h = hidden_states.shape
        seq_rep = hidden_states.mean(axis=1)
        router_logits = seq_rep @ gate_w
        probs = jax.nn.softmax(router_logits.astype(jnp.float32), axis=-1)
        top_w, top_i = jax.lax.top_k(probs, TOP_K)
        top_w = top_w / top_w.sum(axis=-1, keepdims=True)
        top_w = top_w.astype(hidden_states.dtype)
        combine = jnp.zeros((b, E), dtype=hidden_states.dtype)
        combine = combine.at[jnp.arange(b)[:, None], top_i].set(top_w)
        out = jnp.zeros_like(hidden_states)
        for e in range(E):
            hmid = jax.nn.gelu(jnp.einsum('bth,hf->btf', hidden_states, w1[e]) + b1[e], approximate=False)
            y = jnp.einsum('btf,fh->bth', hmid, w2[e]) + b2[e]
            out = out + combine[:, e][:, None, None] * y
        return out
    x = L0_attn_x
    x = x + 0.5 * _L0_ffn_ref(_layernorm(x, axis=-1), L0_ffn_norm_gamma, L0_ffn_slot_norm_gamma, L0_ffn_slot_embeds, L0_ffn_w1, L0_ffn_b1, L0_ffn_w2, L0_ffn_b2)
    x = x + _L0_attn_ref(_layernorm(x, axis=-1), L0_attn_w_qkv, L0_attn_w_out, L0_attn_b_out)
    x = x + 0.5 * _L0_ffn_ref(_layernorm(x, axis=-1), L0_ffn_norm_gamma, L0_ffn_slot_norm_gamma, L0_ffn_slot_embeds, L0_ffn_w1, L0_ffn_b1, L0_ffn_w2, L0_ffn_b2)
    x = x + 0.5 * _L1_ffn_ref(_layernorm(x, axis=-1), L1_ffn_gate_w, L1_ffn_w1, L1_ffn_b1, L1_ffn_w2, L1_ffn_b2)
    x = x + _L1_attn_ref(_layernorm(x, axis=-1), L1_attn_w_kv_down, L1_attn_w_kv_up, L1_attn_w_q, L1_attn_w_out)
    x = x + 0.5 * _L1_ffn_ref(_layernorm(x, axis=-1), L1_ffn_gate_w, L1_ffn_w1, L1_ffn_b1, L1_ffn_w2, L1_ffn_b2)
    return x

_drawn_inputs = setup_inputs


def setup_inputs(seed=0):
    import zlib

    import numpy as np

    out = dict(_drawn_inputs(seed))
    spreads = {'L0_attn_b_out': (0.0, 0.1),
     'L0_ffn_norm_gamma': (1.0, 0.2),
     'L0_ffn_slot_norm_gamma': (1.0, 0.2),
     'L0_ffn_b1': (0.0, 0.404),
     'L0_ffn_b2': (0.0, 0.1)}
    factors = {'L1_attn_w_q': 8.0, 'L1_ffn_b1': 2.834, 'L1_ffn_b2': 3.461}
    for name, (base, spread) in spreads.items():
        noise = np.random.default_rng([zlib.crc32(name.encode()), seed]).standard_normal(out[name].shape)
        drawn = base * np.exp(spread * noise) if base else spread * noise
        out[name] = jnp.asarray(drawn.astype(out[name].dtype))
    for name, factor in factors.items():
        out[name] = (out[name] * factor).astype(out[name].dtype)
    return out
```

```python
from contextlib import ExitStack

import numpy as np

import concourse.bass as bass
from concourse import mybir

P = 128
B, T, D = 8, 512, 128
TT = T // P
NT = B * TT
H, DH = 16, 64
PAIRS = B * H // 2
E_SLOT, S_SLOT = 8, 64
SLOTS = E_SLOT * S_SLOT
E_MOE, TOPK = 8, 2
HID = 512
HB = HID // P
EPS = 1e-5
MASKED = -3.0e38

ALU = mybir.AluOpType
ACT = mybir.ActivationFunctionType
F32 = mybir.dt.float32
F32R = mybir.dt.float32r
U32 = mybir.dt.uint32
AX = mybir.AxisListType.X

PROB_AT = {3: 0, 2: 512, 0: 896, 1: 1024}
PROBT_AT = {0: 0, 1: 512, 3: 896, 2: 1024}
CAUSAL = TT * (TT + 1) // 2 * P


def alibi_slopes():
    start = 2.0 ** (-8.0 / H)
    return np.array([start ** (i + 1) for i in range(H)], np.float32)


class Core:

    def __init__(self, nc, ctx):
        self.nc, self.ctx, self.in_use = nc, ctx, []
        self.x = self.sb("x_tokens", [P, NT, D])
        self.ident = self.sb("ident", [P, P])
        self.bank = [ctx.enter_context(nc.psum_tensor(f"bank{i}", [P, 512], F32)) for i in range(8)]

    def sb(self, name, shape, dt=F32, ctx=None):
        return (ctx or self.ctx).enter_context(self.nc.sbuf_tensor(name, shape, dt))

    def sem(self, name):
        self.in_use.append(self.nc.alloc_semaphore(name=name))
        return self.in_use[-1]

    def end_phase(self):
        self.nc.clear_and_free_semaphores(self.in_use)
        self.nc.all_engine_barrier()
        self.in_use = []


def start_at_one(engine, *semaphores):
    for s in semaphores:
        engine.sem_inc(s, 1)


def layer_norm_stats_on_vector(nc, dve, x, st, s_stat, s_chain, s_var, s_root):
    with dve.Fori(0, NT // 8) as i:
        for u in range(8):
            nc.vector.bn_stats(st["bn"][:, 8 * i + u], x[:, 8 * i + u]).then_inc(s_stat, 1)
    dve.wait_ge(s_stat, NT)
    bn = st["bn"]
    links = [0]

    def link(ins):
        links[0] += 1
        ins.then_inc(s_chain, 1)
        dve.wait_ge(s_chain, links[0])

    even, odd = bn[:, :, 1], bn[:, :, 4]
    link(nc.vector.tensor_tensor(st["mean"][:], even, odd, ALU.add))
    link(nc.vector.tensor_scalar(st["mean"][:], st["mean"][:], 0.5, None, ALU.mult))
    link(nc.vector.tensor_tensor(st["a"][:], even, odd, ALU.subtract))
    link(nc.vector.tensor_tensor(st["a"][:], st["a"][:], st["a"][:], ALU.mult))
    link(nc.vector.tensor_tensor(st["var"][:], bn[:, :, 2], bn[:, :, 5], ALU.add))
    link(nc.vector.tensor_scalar(st["var"][:], st["var"][:], 1.0 / D, None, ALU.mult))
    link(nc.vector.scalar_tensor_tensor(out=st["var"][:], in0=st["a"][:], scalar=0.25, in1=st["var"][:],
                                        op0=ALU.mult, op1=ALU.add))
    nc.vector.tensor_scalar(st["ve"][:], st["var"][:], EPS, None, ALU.add).then_inc(s_var, 1)
    dve.wait_ge(s_root, 1)
    link(nc.vector.reciprocal(st["rstd"][:], st["root"][:]))
    link(nc.vector.tensor_tensor(st["a"][:], st["rstd"][:], st["rstd"][:], ALU.mult))
    link(nc.vector.tensor_tensor(st["a"][:], st["a"][:], st["ve"][:], ALU.mult))
    link(nc.vector.tensor_scalar(st["a"][:], st["a"][:], -0.5, 1.5, ALU.mult, ALU.add))
    link(nc.vector.tensor_tensor(st["rstd"][:], st["rstd"][:], st["a"][:], ALU.mult))
    return link


def stats_buffers(core, ctx, pre):
    st = {k: core.sb(f"{pre}_{k}", [P, NT], ctx=ctx) for k in ("mean", "var", "ve", "a", "rstd", "root")}
    st["bn"] = core.sb(f"{pre}_bn", [P, NT, 6], ctx=ctx)
    return st


def attention(core, pre, w, alibi):
    nc, x, ident, bank = core.nc, core.x, core.ident, core.bank
    with ExitStack() as ctx:
        def sb(name, shape, dt=F32):
            return core.sb(f"{pre}_{name}", shape, dt, ctx)

        def sem(name):
            return core.sem(f"{pre}_{name}")

        xt_full = sb("xt_full", [P, B, T])
        xt_hi = sb("xt_hi", [P, B, T], F32R)
        xt_lo = sb("xt_lo", [P, B, T], F32R)
        m_split = sb("m_split", [P, H, 2, P], F32R)
        wv = sb("wv", [P, H * DH])
        wo2 = sb("wo2", [P, H, D])
        rel = sb("rel", [P, T])
        slopes = sb("slopes", [P, H])

        prepare(core, pre, w, alibi, xt_full, xt_hi, xt_lo, m_split, wv, wo2, rel, slopes)
        core.end_phase()
        attend(core, pre, alibi, xt_full, xt_hi, xt_lo, m_split, wv, wo2, rel, slopes)
        core.end_phase()


def prepare(core, pre, w, alibi, xt_full, xt_hi, xt_lo, m_split, wv, wo2, rel, slopes):
    nc, x, ident, bank = core.nc, core.x, core.ident, core.bank
    with ExitStack() as ctx:
        def sb(name, shape, dt=F32):
            return core.sb(f"{pre}_{name}", shape, dt, ctx)

        def sem(name):
            return core.sem(f"{pre}p_{name}")

        st = stats_buffers(core, ctx, pre + "_st")
        xn = sb("xn", [P, 2, TT, D])
        wq = sb("wq", [P, H * DH])
        wk = sb("wk", [P, H * DH])
        if not alibi:
            wkv_v = sb("wkv_v", [P, H * DH])
            wkd = sb("wkd", [P, P])
            wkd_t = sb("wkd_t", [P, P])
        else:
            bout = sb("bout", [P, D])
        qk_t = sb("qk_t", [P, 2, 2, P])

        s_w = sem("weights_in")
        s_stat, s_chain, s_var, s_root = sem("stats"), sem("chain"), sem("var"), sem("root")
        s_xn = sem("xn_ready")
        s_turned = sem("turned")
        s_xf, s_xh, s_xl = sem("xt_full"), sem("xt_hi"), sem("xt_lo")
        s_bias = sem("bias_added")
        s_qkm, s_qkt = sem("qk_turned"), sem("qk_copied")
        s_turn, s_mh, s_ml = sem("m_ready"), sem("m_hi"), sem("m_lo")
        s_kd, s_kdt, s_vm, s_vc = sem("kd_turned"), sem("kd_copied"), sem("v_ready"), sem("v_copied")

        n_w = [0]
        with nc.Block() as block:
            @block.sync
            def _(sp):
                def load(dst, src):
                    n_w[0] += 1
                    sp.dma_start(dst, src).then_inc(s_w, 16)

                if alibi:
                    load(wq[:], w["qkv"][:, 0:H * DH])
                    load(wk[:], w["qkv"][:, H * DH:2 * H * DH])
                    load(wv[:], w["qkv"][:, 2 * H * DH:3 * H * DH])
                    load(bout[:], w["b_out"].rearrange("(o d) -> o d", o=1).broadcast_to([P, D]))
                    load(slopes[:], w["slopes"])
                else:
                    load(wq[:], w["q"])
                    load(wk[:], w["kv_up"][:, 0:H * DH])
                    load(wkv_v[:], w["kv_up"][:, H * DH:2 * H * DH])
                    load(wkd[:], w["kv_down"])
                for half in range(2):
                    load(wo2[64 * half:64 * half + 64], w["out"].rearrange("(h d) c -> d h c", d=DH))
                load(rel[:], w["rel"])
                sp.wait_ge(s_w, 16 * n_w[0])

            n_loads = 8 if alibi else 7

            @block.gpsimd
            def _(pool):
                if alibi:
                    pool.wait_ge(s_w, 16 * n_loads)
                    with pool.Fori(0, B) as b:
                        pool.wait_ge(s_xn, b + 1)
                        tiles = x[:, bass.ts(b, TT)]
                        nc.gpsimd.tensor_tensor(tiles, tiles, bout[:, None, :].broadcast_to([P, TT, D]),
                                                ALU.add).then_inc(s_bias, 1)

            @block.vector
            def _(dve):
                start_at_one(dve, s_xl)
                link = layer_norm_stats_on_vector(nc, dve, x, st, s_stat, s_chain, s_var, s_root)

                def m_low(p):
                    dve.wait_ge(s_mh, p + 1)
                    nc.vector.scalar_tensor_tensor(
                        out=m_split[:, 2 * p:2 * p + 2, 1, :],
                        in0=bank[2 + p % 2][:, 0:2 * P].rearrange("p (u c) -> p u c", u=2), scalar=DH ** -0.5,
                        in1=m_split[:, 2 * p:2 * p + 2, 0, :].bitcast(F32), op0=ALU.mult,
                        op1=ALU.subtract).then_inc(s_ml, 1)

                with dve.Fori(0, B // 2) as i:
                    for u in range(2):
                        b = 2 * i + u
                        dve.wait_ge(s_turned, b + 1)
                        for t in range(TT):
                            k = TT * b + t
                            ins = nc.vector.tensor_scalar(xn[:, u, t], x[:, k], st["mean"][:, k, None],
                                                          st["rstd"][:, k, None], ALU.subtract, ALU.mult)
                        ins.then_inc(s_xn, 1)
                        dve.wait_ge(s_xh, b + 1)
                        nc.vector.tensor_tensor(xt_lo[:, b], bank[4 + u][:], xt_hi[:, b].bitcast(F32),
                                                ALU.subtract).then_inc(s_xl, 1)
                for p in range(H // 2):
                    m_low(p)

            @block.scalar
            def _(act):
                act.wait_ge(s_var, 1)
                nc.scalar.activation(st["root"][:], st["ve"][:], ACT.Sqrt).then_inc(s_root, 1)
                with act.Fori(0, B // 2) as i:
                    for u in range(2):
                        b = 2 * i + u
                        act.wait_ge(s_turned, b + 3)
                        nc.scalar.copy(xt_full[:, b], bank[4 + u][:]).then_inc(s_xf, 1)
                        nc.scalar.copy(xt_hi[:, b], bank[4 + u][:]).then_inc(s_xh, 1)
                if not alibi:
                    act.wait_ge(s_kd, 1)
                    nc.scalar.copy(wkd_t[:], bank[7][:, 0:P]).then_inc(s_kdt, 1)
                    for c in range(2):
                        act.wait_ge(s_vm, c + 1)
                        nc.scalar.copy(wv[:, 512 * c:512 * c + 512], bank[6][:]).then_inc(s_vc, 1)
                for p in range(H // 2):
                    act.wait_ge(s_qkm, p + 1)
                    nc.scalar.copy(qk_t[:, p % 2].rearrange("p a c -> p (a c)"),
                                   bank[p % 2][:, 0:2 * P]).then_inc(s_qkt, 1)
                    act.wait_ge(s_turn, 2 * p + 2)
                    nc.scalar.mul(m_split[:, 2 * p:2 * p + 2, 0, :],
                                  bank[2 + p % 2][:, 0:2 * P].rearrange("p (u c) -> p u c", u=2),
                                  DH ** -0.5).then_inc(s_mh, 1)

            @block.tensor
            def _(pe):
                pe.sem_inc(s_turned, 2)
                with pe.Fori(0, B // 2) as i:
                    for u in range(2):
                        b = 2 * i + u
                        pe.wait_ge(s_xn, b + 1)
                        pe.wait_ge(s_xl, 1 + 2 * i)
                        for t in range(TT):
                            ins = pe.transpose(bank[4 + u][:, P * t:P * t + P], xn[:, u, t], ident[:])
                        ins.then_inc(s_turned, 1)
                pe.wait_ge(s_w, 16 * n_loads)
                if not alibi:
                    pe.transpose(bank[7][:, 0:P], wkd[:], ident[:]).then_inc(s_kd, 1)
                    pe.wait_ge(s_kdt, 1)
                    for c in range(2):
                        pe.wait_ge(s_vc, c)
                        pe.matmul(bank[6][:], wkd_t[:], wkv_v[:, 512 * c:512 * c + 512], start=True,
                                  stop=True).then_inc(s_vm, 1)
                for p in range(H // 2):
                    cols = slice(P * p, P * p + P)
                    if p >= 2:
                        pe.wait_ge(s_qkt, p - 1)
                    pe.transpose(bank[p % 2][:, 0:P], wq[:, cols], ident[:])
                    if alibi:
                        pe.transpose(bank[p % 2][:, P:2 * P], wk[:, cols], ident[:]).then_inc(s_qkm, 1)
                    else:
                        pe.matmul(bank[p % 2][:, P:2 * P], wk[:, cols], wkd_t[:], start=True,
                                  stop=True).then_inc(s_qkm, 1)
                    pe.wait_ge(s_qkt, p + 1)
                    if p >= 2:
                        pe.wait_ge(s_ml, p - 1)
                    for u in range(2):
                        rows = slice(DH * u, DH * u + DH)
                        pe.wait_ge(s_turn, 2 * p + u)
                        pe.matmul(bank[2 + p % 2][:, P * u:P * u + P], qk_t[rows, p % 2, 0],
                                  qk_t[rows, p % 2, 1], start=True, stop=True).then_inc(s_turn, 1)


def attend(core, pre, alibi, xt_full, xt_hi, xt_lo, m_split, wv, wo2, rel, slopes):
    nc, x, ident, bank = core.nc, core.x, core.ident, core.bank
    proj, s3, s20, s1, turn0, turn1, av, outp = bank
    score_at = {3: s3[:, 0:512], 2: s20[:, 0:384], 0: s20[:, 384:512], 1: s1[:, 0:256]}
    ORDER = (3, 2, 0, 1)
    groups = ((turn0, (0,), 0, 512), (turn1, (1, 3), 512, 512), (turn0, (2,), 1024, 256))
    with ExitStack() as ctx:
        def sb(name, shape, dt=F32):
            return core.sb(f"{pre}_{name}", shape, dt, ctx)

        def sem(name):
            return core.sem(f"{pre}a_{name}")

        m_head = sb("m_head", [P, 2, 2, P], F32R)
        wo_head = sb("wo_head", [P, 2, D])
        wv_pair = sb("wv_pair", [P, P])
        xt_seq = sb("xt_seq", [P, T])
        bias = sb("bias", [P, 2, T]) if alibi else None
        q_hi = sb("q_hi", [P, 2, T], F32R)
        q_lo = sb("q_lo", [P, 2, T], F32R)
        v2 = sb("v2", [P, TT, 2, 2, DH], F32R)
        prob = sb("prob", [P, 2, CAUSAL])
        neg_max = sb("neg_max", [P, 2, TT])
        total = sb("total", [P, 2, TT])
        inv = sb("inv", [P, 2, TT])
        pt_hi = sb("pt_hi", [P, CAUSAL], F32R)
        pt_lo = sb("pt_lo", [P, CAUSAL], F32R)
        av_t = sb("av_t", [P, T])

        s_m, s_wo = [sem("m0_in"), sem("m1_in")], [sem("wo0_in"), sem("wo1_in")]
        s_wv = sem("wv_xt_in")
        s_bias = sem("bias_made")
        s_q, s_qh, s_ql = sem("q_ready"), sem("q_hi"), sem("q_lo")
        s_v, s_vh, s_vl = sem("v_ready"), sem("v_hi"), sem("v_lo")
        s_s, s_st, s_exp = sem("scores_ready"), sem("scores_shifted"), sem("probs_ready")
        s_t, s_th, s_tl = sem("probs_turned"), sem("pt_hi"), sem("pt_lo")
        s_av, s_avc, s_out, s_x = sem("av_ready"), sem("av_copied"), sem("out_ready"), sem("x_added")
        s_inv, s_go = sem("inv_ready"), sem("scores_seen")

        def seq(n):
            return n // (H // 2)

        def head(n, u):
            return (n % (H // 2)) * 2 + u

        with nc.Block() as block:
            @block.sync
            def _(sp):
                def m_of(n, u):
                    if not isinstance(n, int) or n > 0:
                        sp.wait_ge(s_q, 2 * n + u - 1)
                    sp.dma_start(m_head[:, u].bitcast(F32), m_split[:, head(n, u)].bitcast(F32)).then_inc(s_m[u], 16)

                def wo_of(n, u, first=False):
                    if not first:
                        sp.wait_ge(s_out, 2 * n + u - 1)
                    sp.dma_start(wo_head[:, u], wo2[:, head(n, u)]).then_inc(s_wo[u], 16)

                def values_of(n, first=False):
                    if not first:
                        sp.wait_ge(s_v, n)
                    sp.dma_start(wv_pair[:], wv[:, bass.ts(n % (H // 2), P)]).then_inc(s_wv, 16)
                    sp.dma_start(xt_seq[:], xt_full[:, seq(n)]).then_inc(s_wv, 16)

                m_of(0, 0)
                m_of(0, 1)
                values_of(0, True)
                m_of(1, 0)
                m_of(1, 1)
                wo_of(0, 0, True)
                wo_of(0, 1, True)
                values_of(1)
                with sp.Fori(2, PAIRS) as n:
                    m_of(n, 0)
                    m_of(n, 1)
                    wo_of(n - 1, 0)
                    wo_of(n - 1, 1)
                    values_of(n)
                wo_of(PAIRS - 1, 0)
                wo_of(PAIRS - 1, 1)

            @block.gpsimd
            def _(pool):
                if not alibi:
                    return

                def bias_of(n, u, first=False):
                    if not first:
                        pool.wait_ge(s_st, TT * (2 * n + u - 1))
                    nc.gpsimd.tensor_tensor(bias[:, u], rel[:], slopes[:, head(n, u), None].broadcast_to([P, T]),
                                            ALU.mult).then_inc(s_bias, 1)

                bias_of(0, 0, True)
                bias_of(0, 1, True)
                with pool.Fori(1, PAIRS) as n:
                    bias_of(n, 0)
                    bias_of(n, 1)

            @block.tensor
            def _(pe):
                def project(n, u):
                    g = 2 * n + u
                    pe.wait_ge(s_m[u], 16 * (n + 1))
                    xh, xl = xt_hi[:, seq(n)], xt_lo[:, seq(n)]
                    pe.matmul(proj[:], m_head[:, u, 0], xh, start=True, stop=False)
                    pe.matmul(proj[:], m_head[:, u, 0], xl, start=False, stop=False)
                    pe.matmul(proj[:], m_head[:, u, 1], xh, start=False, stop=True).then_inc(s_q, 1)

                def values(n):
                    pe.wait_ge(s_ql, 2 * n + 2)
                    pe.wait_ge(s_wv, 32 * (n + 1))
                    for j in range(TT):
                        ins = pe.matmul(proj[:, P * j:P * j + P], xt_seq[:, P * j:P * j + P], wv_pair[:],
                                        start=True, stop=True)
                    ins.then_inc(s_v, 1)

                def scores(n, u, first=False):
                    g = 2 * n + u
                    pe.wait_ge(s_ql, g + 1)
                    for k, i in enumerate(ORDER):
                        if not first and k in (0, 1, 3):
                            pe.wait_ge(s_st, TT * (g - 1) + (1, 3, 0, 4)[k])
                        keys = slice(0, P * (i + 1))
                        rows = slice(P * i, P * i + P)
                        at = score_at[i]
                        pe.matmul(at, q_hi[:, u, rows], xt_hi[:, seq(n), keys], start=True, stop=False)
                        pe.matmul(at, q_hi[:, u, rows], xt_lo[:, seq(n), keys], start=False, stop=False)
                        pe.matmul(at, q_lo[:, u, rows], xt_hi[:, seq(n), keys], start=False,
                                  stop=True).then_inc(s_s, 1)

                def turn(n, u, c, first=False):
                    g = 2 * n + u
                    to, tiles, at, _ = groups[c]
                    if c == 0:
                        pe.wait_ge(s_exp, TT * (g + 1))
                    if c == 2:
                        pe.wait_ge(s_tl, 3 * g + 1)
                    elif not first:
                        pe.wait_ge(s_tl, 3 * g - c)
                    for j in tiles:
                        for i in range(j, TT):
                            col = PROBT_AT[j] - at + P * (i - j)
                            src = PROB_AT[i] + P * j
                            ins = pe.transpose(to[:, col:col + P], prob[:, u, src:src + P], ident[:])
                    ins.then_inc(s_t, 1)

                def sum_values(n, u, first=False):
                    g = 2 * n + u
                    if not first:
                        pe.wait_ge(s_avc, g)
                    if u == 0:
                        pe.wait_ge(s_vl, n + 1)
                    for c, (_, tiles, _, _) in enumerate(groups):
                        pe.wait_ge(s_tl, 3 * g + c + 1)
                        for j in tiles:
                            at = PROBT_AT[j]
                            cols = slice(at, at + T - P * j)
                            lhs = v2[:, j, u].rearrange("p a d -> p (a d)")
                            pe.matmul(av[:, P * j:T], lhs, pt_hi[:, cols], start=j == 0, stop=False)
                            ins = pe.matmul(av[:, P * j:T], lhs, pt_lo[:, cols], start=False, stop=j == 2)
                    ins.then_inc(s_av, 1)

                def output(n, u, first=False):
                    g = 2 * n + u
                    pe.wait_ge(s_avc, g + 1)
                    pe.wait_ge(s_wo[u], 16 * (n + 1))
                    if not first:
                        pe.wait_ge(s_x, 1 + TT * g)
                    for i in range(TT):
                        ins = pe.matmul(outp[:, P * i:P * i + P], av_t[:, P * i:P * i + P], wo_head[:, u],
                                        start=True, stop=True)
                    ins.then_inc(s_out, 1)

                def pair(n, first=False, last=False):
                    scores(n, 0, first)
                    if not first:
                        output(n - 1, 0)
                        turn(n - 1, 1, 0)
                        turn(n - 1, 1, 1)
                    pe.wait_ge(s_ql, 2 * n + 1)
                    project(n, 1)
                    if not first:
                        turn(n - 1, 1, 2)
                        sum_values(n - 1, 1)
                    scores(n, 1)
                    values(n)
                    if not first:
                        output(n - 1, 1)
                    turn(n, 0, 0, first)
                    turn(n, 0, 1, first)
                    if not last:
                        pe.wait_ge(s_vl, n + 1)
                        project(n + 1, 0)
                    turn(n, 0, 2)
                    sum_values(n, 0, first)

                project(0, 0)
                pair(0, first=True)
                with pe.Fori(1, PAIRS - 1) as n:
                    pair(n)
                pair(PAIRS - 1, last=True)
                output(PAIRS - 1, 0)
                for c in range(3):
                    turn(PAIRS - 1, 1, c)
                sum_values(PAIRS - 1, 1)
                output(PAIRS - 1, 1)

            @block.scalar
            def _(act):
                def q_high(n, u):
                    act.wait_ge(s_q, 2 * n + u + 1)
                    nc.scalar.copy(q_hi[:, u], proj[:]).then_inc(s_qh, 1)

                def v_high(n):
                    act.wait_ge(s_v, n + 1)
                    nc.scalar.copy(v2[:, :, :, 0], proj[:].rearrange("p (j u d) -> p j u d", j=TT, u=2))\
                        .then_inc(s_vh, 1)

                def probs(n, u, k):
                    g = 2 * n + u
                    i = ORDER[k]
                    at = PROB_AT[i]
                    tile = prob[:, u, at:at + P * (i + 1)]
                    act.wait_ge(s_st, TT * g + k + 1)
                    nc.scalar.activation(tile, tile, ACT.Exp, bias=neg_max[:, u, i:i + 1], scale=-1.0,
                                         accum_out=total[:, u, i:i + 1]).then_inc(s_exp, 1)

                def pt_high(n, u, c):
                    to, _, at, size = groups[c]
                    act.wait_ge(s_t, 3 * (2 * n + u) + c + 1)
                    nc.scalar.copy(pt_hi[:, at:at + size], to[:, 0:size]).then_inc(s_th, 1)

                def av_copy(n, u):
                    act.wait_ge(s_av, 2 * n + u + 1)
                    nc.scalar.copy(av_t[:], av[:]).then_inc(s_avc, 1)

                def pair(n, first=False, last=False):
                    for u in range(2):
                        former = (n - 1, 1) if u == 0 else (n, 0)
                        turning = not (first and u == 0)
                        probs(n, u, 0)
                        probs(n, u, 1)
                        if u == 1:
                            v_high(n)
                        if turning:
                            pt_high(*former, 0)
                            pt_high(*former, 1)
                        if u == 0:
                            q_high(n, 1)
                        elif not last:
                            q_high(n + 1, 0)
                        if turning:
                            pt_high(*former, 2)
                        probs(n, u, 2)
                        probs(n, u, 3)
                        if turning:
                            av_copy(*former)

                q_high(0, 0)
                pair(0, first=True)
                with act.Fori(1, PAIRS - 1) as n:
                    pair(n)
                pair(PAIRS - 1, last=True)
                for c in range(3):
                    pt_high(PAIRS - 1, 1, c)
                av_copy(PAIRS - 1, 1)

            @block.vector
            def _(dve):
                start_at_one(dve, s_x)
                def q_low(n, u):
                    dve.wait_ge(s_qh, 2 * n + u + 1)
                    nc.vector.tensor_tensor(q_lo[:, u], proj[:], q_hi[:, u].bitcast(F32),
                                            ALU.subtract).then_inc(s_ql, 1)

                def v_low(n):
                    dve.wait_ge(s_vh, n + 1)
                    nc.vector.tensor_tensor(v2[:, :, :, 1], proj[:].rearrange("p (j u d) -> p j u d", j=TT, u=2),
                                            v2[:, :, :, 0].bitcast(F32), ALU.subtract).then_inc(s_vl, 1)

                def shift(n, u, first=False):
                    g = 2 * n + u
                    if not first:
                        dve.wait_ge(s_t, 3 * (g - 1))
                    if alibi:
                        dve.wait_ge(s_bias, g + 1)
                    for k, i in enumerate(ORDER):
                        dve.wait_ge(s_s, TT * g + (1, 3, 3, 4)[k])
                        dve.sem_inc(s_go, 1)
                        at = PROB_AT[i]
                        size = P * (i + 1)
                        table = bias[:, u] if alibi else rel
                        nc.vector.tensor_tensor_reduce(
                            out=prob[:, u, at:at + size], in0=score_at[i], in1=table[:, T - size:T],
                            scale=-1.0, scalar=-MASKED, op0=ALU.add, op1=ALU.min,
                            accum_out=neg_max[:, u, i:i + 1]).then_inc(s_st, 1)

                def pt_low(n, u, c):
                    to, _, at, size = groups[c]
                    dve.wait_ge(s_th, 3 * (2 * n + u) + c + 1)
                    nc.vector.tensor_tensor(pt_lo[:, at:at + size], to[:, 0:size], pt_hi[:, at:at + size].bitcast(F32),
                                            ALU.subtract).then_inc(s_tl, 1)

                def invert(n, u, first=False):
                    g = 2 * n + u
                    dve.wait_ge(s_exp, TT * (g + 1))
                    if not first:
                        dve.wait_ge(s_x, 1 + TT * (g - 1))
                    nc.vector.reciprocal(inv[:, u], total[:, u]).then_inc(s_inv, 1)

                def add_output(n, u):
                    g = 2 * n + u
                    dve.wait_ge(s_out, g + 1)
                    dve.wait_ge(s_inv, g + 1)
                    dve.wait_ge(s_x, 1 + TT * g)
                    for i in range(TT):
                        tile = x[:, seq(n) * TT + i]
                        nc.vector.scalar_tensor_tensor(out=tile, in0=outp[:, P * i:P * i + P], scalar=inv[:, u, i:i + 1],
                                                       in1=tile, op0=ALU.mult, op1=ALU.add).then_inc(s_x, 1)

                def pair(n, first=False, last=False):
                    for u in range(2):
                        former = (n - 1, 1) if u == 0 else (n, 0)
                        turning = not (first and u == 0)
                        shift(n, u, first)
                        if u == 1:
                            v_low(n)
                        if turning:
                            invert(*former, first)
                        if not first:
                            add_output(n - 1, u)
                        if turning:
                            pt_low(*former, 0)
                            pt_low(*former, 1)
                        if u == 0:
                            q_low(n, 1)
                        elif not last:
                            q_low(n + 1, 0)
                        if turning:
                            pt_low(*former, 2)

                q_low(0, 0)
                pair(0, first=True)
                with dve.Fori(1, PAIRS - 1) as n:
                    pair(n)
                pair(PAIRS - 1, last=True)
                invert(PAIRS - 1, 1)
                add_output(PAIRS - 1, 0)
                for c in range(3):
                    pt_low(PAIRS - 1, 1, c)
                add_output(PAIRS - 1, 1)


def refine_root(nc, link, y, v, a):
    link(nc.vector.tensor_tensor(a, y, y, ALU.mult))
    link(nc.vector.tensor_tensor(a, a, v, ALU.mult))
    link(nc.vector.tensor_scalar(a, a, -0.5, 1.5, ALU.mult, ALU.add))
    link(nc.vector.tensor_tensor(y, y, a, ALU.mult))


def soft_moe(core, pre, w):
    nc, x = core.nc, core.x
    with ExitStack() as ctx:
        def sb(name, shape, dt=F32):
            return core.sb(f"{pre}_{name}", shape, dt, ctx)

        combine_t = sb("combine_t", [P, B, TT, T])
        slots = sb("slots", [P, E_SLOT, B, S_SLOT])
        expert_out = sb("expert_out", [P, E_SLOT, B, S_SLOT])
        half_inv = sb("half_inv", [P, NT])
        b1_t = sb("b1_t", [P, E_SLOT * HB])
        b2_t = sb("b2_t", [P, E_SLOT])
        dispatch(core, pre, w, combine_t, slots, half_inv, b1_t, b2_t)
        core.end_phase()
        slot_experts(core, pre, w, slots, expert_out, b1_t, b2_t)
        core.end_phase()
        combine(core, pre, combine_t, expert_out, half_inv)
        core.end_phase()


def dispatch(core, pre, w, combine_t, slots, half_inv, b1_t, b2_t):
    nc, x, ident, bank = core.nc, core.x, core.ident, core.bank
    ST = SLOTS // P
    with ExitStack() as ctx:
        def sb(name, shape, dt=F32):
            return core.sb(f"{pre}_{name}", shape, dt, ctx)

        def sem(name):
            return core.sem(f"{pre}d_{name}")

        st = stats_buffers(core, ctx, pre + "_st")
        emb = sb("emb", [P, ST, D])
        square = sb("square", [P, D])
        norm2 = sb("norm2", [P, NT + ST])
        norm = sb("norm", [P, NT + ST])
        scale = sb("scale", [P, NT + ST])
        scratch = sb("scratch", [P, NT + ST])
        gammas = sb("gammas", [P, 2])
        gamma2 = sb("gamma2", [P, 1])
        emb_t = sb("emb_t", [P, SLOTS])
        b1_rows = sb("b1_rows", [E_SLOT * HB, P])
        b2_rows = sb("b2_rows", [E_SLOT, D])
        z = sb("z", [P, 2, TT, D])
        z_t = sb("z_t", [P, 2, T])
        neg_max = sb("neg_max", [P, 2, 2 * TT])
        total = sb("total", [P, 2, 2 * TT])
        inv = sb("inv", [P, 2, 2 * TT])
        prob = sb("prob", [P, 2, 2 * TT, T])
        disp = sb("disp", [P, TT, SLOTS])

        s_in = sem("inputs_in")
        s_stat, s_chain, s_var, s_root = sem("stats"), sem("chain"), sem("var"), sem("root")
        s_norm2, s_norm = sem("norm2"), sem("norm")
        s_emb, s_embm, s_embt = sem("slots_normed"), sem("slots_turned"), sem("slots_copied")
        s_z, s_zm, s_zt = sem("z_ready"), sem("z_turned"), sem("z_copied")
        s_l, s_max, s_exp = sem("logits"), sem("max"), sem("probs")
        s_inv, s_nrm = sem("inv_ready"), sem("dispatch_normed")
        s_t, s_dc, s_cc = sem("probs_turned"), sem("dispatch_copied"), sem("combine_copied")
        s_sl, s_slc = sem("slots_ready"), sem("slots_copied_out")
        s_bt, s_btc = sem("biases_turned"), sem("biases_copied")

        with nc.Block() as block:
            @block.sync
            def _(sp):
                sp.dma_start(emb[:], w["slot_embeds"].rearrange("e s d -> (e s) d")
                             .rearrange("(k p) d -> p k d", p=P)).then_inc(s_in, 16)
                sp.dma_start(gammas[:, 0:1], w["norm_gamma"].rearrange("(d o) -> d o", o=1)).then_inc(s_in, 16)
                sp.dma_start(gammas[:, 1:2], w["slot_norm_gamma"].rearrange("(d o) -> d o", o=1)).then_inc(s_in, 16)
                sp.dma_start(b1_rows[:], w["b1"].rearrange("e (k p) -> (e k) p", p=P)).then_inc(s_in, 16)
                sp.dma_start(b2_rows[:], w["b2"]).then_inc(s_in, 16)

            @block.vector
            def _(dve):
                start_at_one(dve, s_nrm, s_cc, s_slc)
                link = layer_norm_stats_on_vector(nc, dve, x, st, s_stat, s_chain, s_var, s_root)
                n2 = norm2[:, 0:NT]
                link(nc.vector.tensor_tensor(n2, st["rstd"][:], st["rstd"][:], ALU.mult))
                link(nc.vector.tensor_tensor(n2, n2, st["var"][:], ALU.mult))
                link(nc.vector.tensor_scalar(n2, n2, float(D), None, ALU.mult))
                dve.wait_ge(s_in, 16 * 5)
                for k in range(ST):
                    link(nc.vector.tensor_tensor_reduce(out=square[:], in0=emb[:, k], in1=emb[:, k], scale=1.0,
                                                        scalar=0.0, op0=ALU.mult, op1=ALU.add,
                                                        accum_out=norm2[:, NT + k:NT + k + 1]))
                nc.vector.tensor_scalar(norm2[:], norm2[:], 1e-24, None, ALU.max).then_inc(s_norm2, 1)
                dve.wait_ge(s_norm2, 1)
                dve.wait_ge(s_norm, 1)
                link(nc.vector.reciprocal(scale[:], norm[:]))
                refine_root(nc, link, scale[:], norm2[:], scratch[:])
                link(nc.vector.tensor_scalar(scale[:], scale[:], float(D) ** 0.5, None, ALU.mult))
                link(nc.vector.tensor_tensor(scale[:, 0:NT], scale[:, 0:NT], st["rstd"][:], ALU.mult))
                for k in range(ST):
                    ins = nc.vector.tensor_scalar(emb[:, k], emb[:, k], scale[:, NT + k:NT + k + 1], None, ALU.mult)
                ins.then_inc(s_emb, 1)
                link(nc.vector.tensor_tensor(gamma2[:], gammas[:, 0:1], gammas[:, 1:2], ALU.mult))
                dve.wait_ge(s_embm, 1)
                nc.vector.tensor_scalar(emb_t[:], bank[0][:], gamma2[:, 0:1], None, ALU.mult).then_inc(s_embt, 1)
                dve.wait_ge(s_bt, 1)
                nc.vector.tensor_copy(b1_t[:], bank[7][:, 0:E_SLOT * HB]).then_inc(s_btc, 1)
                nc.vector.tensor_copy(b2_t[:], bank[7][:, P:P + E_SLOT]).then_inc(s_btc, 1)

                def normed(b, u, i):
                    dve.wait_ge(s_sl, 1 + 2 * i)
                    for t in range(TT):
                        k = TT * b + t
                        ins = nc.vector.tensor_scalar(z[:, u, t], x[:, k], st["mean"][:, k, None], scale[:, k, None],
                                                      ALU.subtract, ALU.mult)
                    ins.then_inc(s_z, 1)

                def maxima(b, u, i):
                    dve.wait_ge(s_exp, 1 + 16 * i)
                    for k in range(2 * TT):
                        dve.wait_ge(s_l, 8 * b + k + 1)
                        nc.vector.tensor_reduce(neg_max[:, u, k:k + 1], bank[1 + k % 4][:], AX, ALU.max,
                                                negate=True).then_inc(s_max, 1)

                def norm_dispatch(b, u):
                    dve.wait_ge(s_exp, 1 + 8 * (b + 1))
                    dve.wait_ge(s_nrm, 1 + 5 * b)
                    nc.vector.reciprocal(inv[:, u], total[:, u]).then_inc(s_inv, 1)
                    dve.wait_ge(s_inv, b + 1)
                    for k in range(TT):
                        nc.vector.tensor_scalar(prob[:, u, k], prob[:, u, k], inv[:, u, k:k + 1], None,
                                                ALU.mult).then_inc(s_nrm, 1)
                    nc.vector.tensor_scalar(half_inv[:, bass.ts(b, TT)], inv[:, u, TT:2 * TT], 0.5, None,
                                            ALU.mult).then_inc(s_nrm, 1)

                def copy_combine(b):
                    for k in range(ST):
                        dve.wait_ge(s_t, 1 + 8 * b + TT + k + 1)
                        nc.vector.tensor_copy(combine_t[:, b, k], bank[5 + k % 2][:]).then_inc(s_cc, 1)

                def copy_slots(b):
                    dve.wait_ge(s_sl, 1 + b + 1)
                    nc.vector.tensor_scalar(slots[:, :, b], bank[7][:].rearrange("p (e s) -> p e s", e=E_SLOT),
                                            gammas[:, 0:1], None, ALU.mult).then_inc(s_slc, 1)

                with dve.Fori(0, B // 2) as i:
                    for u in range(2):
                        normed(2 * i + u, u, i)
                    for u in range(2):
                        maxima(2 * i + u, u, i)
                        norm_dispatch(2 * i + u, u)
                    for u in range(2):
                        copy_combine(2 * i + u)
                        copy_slots(2 * i + u)

            @block.scalar
            def _(act):
                start_at_one(act, s_exp, s_zt)
                act.wait_ge(s_var, 1)
                nc.scalar.activation(st["root"][:], st["ve"][:], ACT.Sqrt).then_inc(s_root, 1)
                act.wait_ge(s_norm2, 1)
                nc.scalar.activation(norm[:], norm2[:], ACT.Sqrt).then_inc(s_norm, 1)
                with act.Fori(0, B // 2) as i:
                    for u in range(2):
                        b = 2 * i + u
                        act.wait_ge(s_zm, b + 1)
                        nc.scalar.copy(z_t[:, u], bank[0][:]).then_inc(s_zt, 1)
                    for u in range(2):
                        b = 2 * i + u
                        act.wait_ge(s_t, 1 + 16 * i)
                        for k in range(2 * TT):
                            act.wait_ge(s_max, 8 * b + k + 1)
                            nc.scalar.activation(prob[:, u, k], bank[1 + k % 4][:], ACT.Exp,
                                                 bias=neg_max[:, u, k:k + 1], scale=1.0,
                                                 accum_out=total[:, u, k:k + 1]).then_inc(s_exp, 1)
                    for u in range(2):
                        b = 2 * i + u
                        act.wait_ge(s_sl, 1 + b)
                        for t in range(TT):
                            act.wait_ge(s_t, 1 + 8 * b + t + 1)
                            nc.scalar.copy(disp[:, t], bank[5 + t % 2][:]).then_inc(s_dc, 1)

            @block.tensor
            def _(pe):
                start_at_one(pe, s_sl, s_t)
                pe.wait_ge(s_in, 16 * 5)
                pe.wait_ge(s_emb, 1)
                for k in range(ST):
                    ins = pe.transpose(bank[0][:, P * k:P * k + P], emb[:, k], ident[:])
                ins.then_inc(s_embm, 1)
                pe.transpose(bank[7][:, 0:E_SLOT * HB], b1_rows[:], ident[0:E_SLOT * HB, 0:E_SLOT * HB])
                pe.transpose(bank[7][:, P:P + E_SLOT], b2_rows[:], ident[0:E_SLOT, 0:E_SLOT]).then_inc(s_bt, 1)
                pe.wait_ge(s_embt, 1)
                pe.wait_ge(s_btc, 2)

                def turn_tokens(b, u):
                    pe.wait_ge(s_z, b + 1)
                    pe.wait_ge(s_zt, 1 + b)
                    for t in range(TT):
                        ins = pe.transpose(bank[0][:, P * t:P * t + P], z[:, u, t], ident[:])
                    ins.then_inc(s_zm, 1)

                def logits(b, u):
                    pe.wait_ge(s_zt, 1 + b + 1)
                    for k in range(2 * TT):
                        if k >= 4:
                            pe.wait_ge(s_exp, 1 + 8 * b + k - 3)
                        else:
                            pe.wait_ge(s_exp, 1 + 8 * b)
                        to = bank[1 + k % 4][:]
                        if k < TT:
                            ins = pe.matmul(to, emb_t[:, P * k:P * k + P], z_t[:, u], start=True, stop=True)
                        else:
                            ins = pe.matmul(to, z_t[:, u, P * (k - TT):P * (k - TT) + P], emb_t[:],
                                            start=True, stop=True)
                        ins.then_inc(s_l, 1)

                def turn_probs(b, u):
                    pe.wait_ge(s_nrm, 1 + 5 * (b + 1))
                    for r in range(2 * TT):
                        if r < 2:
                            pe.wait_ge(s_cc, 1 + TT * b)
                        elif r < 6:
                            pe.wait_ge(s_dc, TT * b + r - 1)
                        else:
                            pe.wait_ge(s_cc, 1 + TT * b + r - 5)
                        rows = 0 if r < TT else TT
                        col = P * (r % TT)
                        for k in range(TT):
                            ins = pe.transpose(bank[5 + r % 2][:, P * k:P * k + P],
                                               prob[:, u, rows + k, col:col + P], ident[:])
                        ins.then_inc(s_t, 1)

                def slot_sums(b, u):
                    pe.wait_ge(s_dc, TT * (b + 1))
                    pe.wait_ge(s_slc, 1 + b)
                    for t in range(TT):
                        ins = pe.matmul(bank[7][:], z[:, u, t], disp[:, t], start=t == 0, stop=t == TT - 1)
                    ins.then_inc(s_sl, 1)

                with pe.Fori(0, B // 2) as i:
                    for u in range(2):
                        turn_tokens(2 * i + u, u)
                    for u in range(2):
                        logits(2 * i + u, u)
                    for u in range(2):
                        turn_probs(2 * i + u, u)
                        slot_sums(2 * i + u, u)


def slot_experts(core, pre, w, slots, expert_out, b1_t, b2_t):
    nc, bank = core.nc, core.bank
    N = B * S_SLOT
    with ExitStack() as ctx:
        def sb(name, shape, dt=F32):
            return core.sb(f"{pre}_{name}", shape, dt, ctx)

        def sem(name):
            return core.sem(f"{pre}e_{name}")

        w1 = sb("w1", [P, 2, HID])
        w2 = sb("w2", [P, 2, HB, D])
        hid = sb("hid", [P, 2, HB, N])
        s_w = [sem("w0_in"), sem("w1_in")]
        s_h, s_g, s_o, s_oc = sem("hidden"), sem("gelu"), sem("out"), sem("out_copied")

        with nc.Block() as block:
            @block.sync
            def _(sp):
                def load(e, u):
                    sp.dma_start(w1[:, u], w["w1"][e]).then_inc(s_w[u], 16)
                    sp.dma_start(w2[:, u], w["w2"][e].rearrange("(k p) d -> p k d", p=P)).then_inc(s_w[u], 16)

                load(0, 0)
                load(1, 1)
                with sp.Fori(1, E_SLOT // 2) as i:
                    for u in range(2):
                        sp.wait_ge(s_o, 1 + 2 * i + u - 1)
                        load(2 * i + u, u)

            @block.tensor
            def _(pe):
                start_at_one(pe, s_o)
                def first(e, u, i):
                    pe.wait_ge(s_w[u], 32 * (i + 1))
                    for k in range(HB):
                        if k == 0:
                            pe.wait_ge(s_g, 1 + HB * e)
                        pe.matmul(bank[k][:], w1[:, u, P * k:P * k + P], slots[:, e].rearrange("p b s -> p (b s)"),
                                  start=True, stop=True).then_inc(s_h, 1)

                def second(e, u):
                    pe.wait_ge(s_oc, 1 + e)
                    for k in range(HB):
                        pe.wait_ge(s_g, 1 + HB * e + k + 1)
                        ins = pe.matmul(bank[4 + u][:], w2[:, u, k], hid[:, u, k], start=k == 0, stop=k == HB - 1)
                    ins.then_inc(s_o, 1)

                with pe.Fori(0, E_SLOT // 2) as i:
                    first(2 * i, 0, i)
                    first(2 * i + 1, 1, i)
                    second(2 * i, 0)
                    second(2 * i + 1, 1)

            @block.scalar
            def _(act):
                start_at_one(act, s_g)
                with act.Fori(0, E_SLOT // 2) as i:
                    for u in range(2):
                        e = 2 * i + u
                        act.wait_ge(s_o, 1 + 2 * i)
                        for k in range(HB):
                            act.wait_ge(s_h, HB * e + k + 1)
                            nc.scalar.activation(hid[:, u, k], bank[k][:], ACT.Gelu,
                                                 bias=b1_t[:, HB * e + k, None], scale=1.0).then_inc(s_g, 1)

            @block.vector
            def _(dve):
                start_at_one(dve, s_oc)
                with dve.Fori(0, E_SLOT // 2) as i:
                    for u in range(2):
                        e = 2 * i + u
                        dve.wait_ge(s_o, 1 + e + 1)
                        nc.vector.tensor_scalar(expert_out[:, e].rearrange("p b s -> p (b s)"), bank[4 + u][:],
                                                b2_t[:, e, None], None, ALU.add).then_inc(s_oc, 1)


def combine(core, pre, combine_t, expert_out, half_inv):
    nc, x, ident, bank = core.nc, core.x, core.ident, core.bank
    ST = SLOTS // P
    with ExitStack() as ctx:
        def sb(name, shape, dt=F32):
            return core.sb(f"{pre}_{name}", shape, dt, ctx)

        def sem(name):
            return core.sem(f"{pre}c_{name}")

        out_seq = sb("out_seq", [P, 2, E_SLOT, S_SLOT])
        out_rows = sb("out_rows", [P, 2, ST, D])
        mixed_t = sb("mixed_t", [P, 2, T])
        s_seq, s_t, s_tc = sem("seq_picked"), sem("outs_turned"), sem("outs_copied")
        s_mix, s_mixc, s_back, s_x = sem("mixed"), sem("mixed_copied"), sem("turned_back"), sem("x_added")

        with nc.Block() as block:
            @block.gpsimd
            def _(pool):
                with pool.Fori(0, B // 2) as i:
                    for u in range(2):
                        b = 2 * i + u
                        pool.wait_ge(s_t, 1 + 2 * i)
                        nc.gpsimd.tensor_copy(out_seq[:, u], expert_out[:, :, b]).then_inc(s_seq, 1)

            @block.tensor
            def _(pe):
                start_at_one(pe, s_t, s_mix, s_back)
                with pe.Fori(0, B // 2) as i:
                    for u in range(2):
                        b = 2 * i + u
                        pe.wait_ge(s_seq, b + 1)
                        pe.wait_ge(s_tc, 1 + 2 * i)
                        flat = out_seq[:, u].rearrange("p e s -> p (e s)")
                        for k in range(ST):
                            ins = pe.transpose(bank[u][:, P * k:P * k + P], flat[:, P * k:P * k + P], ident[:])
                        ins.then_inc(s_t, 1)
                    for u in range(2):
                        b = 2 * i + u
                        pe.wait_ge(s_tc, 1 + b + 1)
                        pe.wait_ge(s_mixc, 1 + 2 * i)
                        for k in range(ST):
                            ins = pe.matmul(bank[2 + u][:], out_rows[:, u, k], combine_t[:, b, k],
                                            start=k == 0, stop=k == ST - 1)
                        ins.then_inc(s_mix, 1)
                    for u in range(2):
                        b = 2 * i + u
                        pe.wait_ge(s_mixc, 1 + b + 1)
                        pe.wait_ge(s_x, 1 + TT * 2 * i)
                        for t in range(TT):
                            ins = pe.transpose(bank[4 + u][:, P * t:P * t + P], mixed_t[:, u, P * t:P * t + P],
                                               ident[:])
                        ins.then_inc(s_back, 1)

            @block.scalar
            def _(act):
                start_at_one(act, s_tc, s_mixc)
                with act.Fori(0, B // 2) as i:
                    for u in range(2):
                        b = 2 * i + u
                        act.wait_ge(s_t, 1 + b + 1)
                        act.wait_ge(s_mix, 1 + 2 * i)
                        nc.scalar.copy(out_rows[:, u].rearrange("p k d -> p (k d)"), bank[u][:]).then_inc(s_tc, 1)
                    for u in range(2):
                        b = 2 * i + u
                        act.wait_ge(s_mix, 1 + b + 1)
                        act.wait_ge(s_back, 1 + 2 * i)
                        nc.scalar.copy(mixed_t[:, u], bank[2 + u][:]).then_inc(s_mixc, 1)

            @block.vector
            def _(dve):
                start_at_one(dve, s_x)
                with dve.Fori(0, B // 2) as i:
                    for u in range(2):
                        b = 2 * i + u
                        dve.wait_ge(s_back, 1 + b + 1)
                        for t in range(TT):
                            k = TT * b + t
                            nc.vector.scalar_tensor_tensor(out=x[:, k], in0=bank[4 + u][:, P * t:P * t + P],
                                                           scalar=half_inv[:, k, None], in1=x[:, k],
                                                           op0=ALU.mult, op1=ALU.add).then_inc(s_x, 1)


def top_moe(core, pre, w):
    nc, x, ident, bank = core.nc, core.x, core.ident, core.bank
    with ExitStack() as ctx:
        def sb(name, shape, dt=F32):
            return core.sb(f"{pre}_{name}", shape, dt, ctx)

        xt = sb("xt", [P, B, T])
        b1_t = sb("b1_t", [P, E_MOE, HB])
        mix = sb("mix", [P, TOPK * B])
        choice = sb("choice", [1, B * 8], U32)
        ones = sb("ones", [P, P])
        route(core, pre, w, xt, b1_t, mix, choice, ones)
        core.end_phase()
        chosen_experts(core, pre, w, xt, b1_t, mix, choice, ones)
        core.end_phase()


def route(core, pre, w, xt, b1_t, mix, choice, ones):
    nc, x, ident, bank = core.nc, core.x, core.ident, core.bank
    with ExitStack() as ctx:
        def sb(name, shape, dt=F32):
            return core.sb(f"{pre}_{name}", shape, dt, ctx)

        def sem(name):
            return core.sem(f"{pre}r_{name}")

        st = stats_buffers(core, ctx, pre + "_st")
        xn = sb("xn", [P, 2, TT, D])
        sums = sb("sums", [P, B])
        gate = sb("gate", [P, E_MOE])
        b1_rows = sb("b1_rows", [E_MOE * HB, P])
        logit = sb("logit", [B, E_MOE])
        neg = sb("neg", [B, 1])
        prob = sb("prob", [B, E_MOE])
        total = sb("total", [B, 1])
        inv = sb("inv", [B, 1])
        best = sb("best", [B, 8])
        index = sb("index", [B, 8], U32)
        pair_sum = sb("pair_sum", [B, 1])
        diag = sb("diag", [B, TOPK, B])

        s_in = sem("inputs_in")
        s_stat, s_chain, s_var, s_root = sem("stats"), sem("chain"), sem("var"), sem("root")
        s_xn, s_t, s_tc, s_ones = sem("xn_ready"), sem("turned"), sem("copied"), sem("ones")
        s_lg, s_neg, s_exp = sem("logits"), sem("neg_max"), sem("exp")
        s_dg, s_mix, s_ch = sem("diag"), sem("mix"), sem("choice_in")

        with nc.Block() as block:
            @block.sync
            def _(sp):
                sp.dma_start(gate[:], w["gate_w"]).then_inc(s_in, 16)
                sp.dma_start(b1_rows[:], w["b1"].rearrange("e (k p) -> (e k) p", p=P)).then_inc(s_in, 16)
                sp.wait_ge(s_dg, 1)
                sp.dma_start(choice[0:1, :].rearrange("o (b k) -> o b k", b=B), index[:]).then_inc(s_ch, 16)
                sp.wait_ge(s_ch, 16)

            @block.vector
            def _(dve):
                nc.vector.memset(ones[:], 1.0).then_inc(s_ones, 1)
                link = layer_norm_stats_on_vector(nc, dve, x, st, s_stat, s_chain, s_var, s_root)
                with dve.Fori(0, B // 2) as i:
                    for u in range(2):
                        b = 2 * i + u
                        dve.wait_ge(s_t, 1 + 2 * i)
                        for t in range(TT):
                            k = TT * b + t
                            ins = nc.vector.tensor_scalar(xn[:, u, t], x[:, k], st["mean"][:, k, None],
                                                          st["rstd"][:, k, None], ALU.subtract, ALU.mult)
                        ins.then_inc(s_xn, 1)
                dve.wait_ge(s_lg, 1)
                link(nc.vector.tensor_scalar(logit[:], bank[2][0:B, 0:E_MOE], 1.0 / T, None, ALU.mult))
                nc.vector.tensor_reduce(neg[:], logit[:], AX, ALU.max, negate=True).then_inc(s_neg, 1)
                dve.wait_ge(s_exp, 1)
                link(nc.vector.reciprocal(inv[:], total[:]))
                link(nc.vector.tensor_scalar(prob[:], prob[:], inv[:, 0:1], None, ALU.mult))
                link(nc.vector.max(best[:], prob[:]))
                link(nc.vector.max_index(index[:], best[:], prob[:]))
                link(nc.vector.tensor_tensor(pair_sum[:], best[:, 0:1], best[:, 1:2], ALU.add))
                link(nc.vector.reciprocal(pair_sum[:], pair_sum[:]))
                link(nc.vector.tensor_scalar(best[:], best[:], pair_sum[:, 0:1], 0.5, ALU.mult, ALU.mult))
                for k in range(TOPK):
                    link(nc.vector.tensor_scalar(diag[:, k], ident[0:B, 0:B], best[:, k:k + 1], None, ALU.mult))
                dve.sem_inc(s_dg, 1)
                dve.wait_ge(s_mix, 1)
                link(nc.vector.tensor_copy(mix[:], bank[3][:, 0:TOPK * B]))
                link(nc.vector.tensor_copy(b1_t[:].rearrange("p e k -> p (e k)"), bank[4][:, 0:E_MOE * HB]))

            @block.scalar
            def _(act):
                start_at_one(act, s_tc)
                act.wait_ge(s_var, 1)
                nc.scalar.activation(st["root"][:], st["ve"][:], ACT.Sqrt).then_inc(s_root, 1)
                with act.Fori(0, B // 2) as i:
                    for u in range(2):
                        b = 2 * i + u
                        act.wait_ge(s_t, 1 + b + 1)
                        nc.scalar.activation(xt[:, b], bank[u][:], ACT.Copy,
                                             accum_out=sums[:, b, None]).then_inc(s_tc, 1)
                act.wait_ge(s_neg, 1)
                nc.scalar.activation(prob[:], logit[:], ACT.Exp, bias=neg[:, 0:1], scale=1.0,
                                     accum_out=total[:, 0:1]).then_inc(s_exp, 1)

            @block.tensor
            def _(pe):
                start_at_one(pe, s_t)
                with pe.Fori(0, B // 2) as i:
                    for u in range(2):
                        b = 2 * i + u
                        pe.wait_ge(s_xn, b + 1)
                        pe.wait_ge(s_tc, 1 + 2 * i)
                        for t in range(TT):
                            ins = pe.transpose(bank[u][:, P * t:P * t + P], xn[:, u, t], ident[:])
                        ins.then_inc(s_t, 1)
                pe.wait_ge(s_in, 32)
                pe.transpose(bank[4][:, 0:E_MOE * HB], b1_rows[:], ident[0:E_MOE * HB, 0:E_MOE * HB])
                pe.wait_ge(s_tc, 1 + B)
                pe.matmul(bank[2][0:B, 0:E_MOE], sums[:], gate[:], start=True, stop=True).then_inc(s_lg, 1)
                pe.wait_ge(s_ones, 1)
                pe.wait_ge(s_dg, 1)
                pe.matmul(bank[3][:, 0:TOPK * B], ones[0:B, :], diag[:].rearrange("p k b -> p (k b)"),
                          start=True, stop=True).then_inc(s_mix, 1)


def chosen_experts(core, pre, w, xt, b1_t, mix, choice, ones):
    nc, x, bank = core.nc, core.x, core.bank
    with ExitStack() as ctx:
        def sb(name, shape, dt=F32):
            return core.sb(f"{pre}_{name}", shape, dt, ctx)

        def sem(name):
            return core.sem(f"{pre}x_{name}")

        w1 = sb("w1", [P, TOPK, HID])
        w2 = sb("w2", [P, TOPK, HB, D])
        b1 = sb("b1", [P, TOPK, HB])
        b2 = sb("b2", [1, TOPK, D])
        hid = sb("hid", [P, TOPK, HB, T])
        s_w = [sem("w0_in"), sem("w1_in")]
        s_h, s_g, s_y, s_x = sem("hidden"), sem("gelu"), sem("out"), sem("x_added")

        with nc.Block() as block:
            @block.sync
            def _(sp):
                def load(b, k):
                    e = sp.value_load(choice[0:1, bass.ds(8 * b + k, 1)], min_val=0, max_val=E_MOE - 1)
                    sp.dma_start(w1[:, k], w["w1"][e]).then_inc(s_w[k], 16)
                    sp.dma_start(w2[:, k], w["w2"][e].rearrange("(k p) d -> p k d", p=P)).then_inc(s_w[k], 16)
                    sp.dma_start(b1[:, k], b1_t[:, e]).then_inc(s_w[k], 16)
                    sp.dma_start(b2[:, k], w["b2"][e, None]).then_inc(s_w[k], 16)

                load(0, 0)
                load(0, 1)
                with sp.Fori(1, B) as b:
                    for k in range(TOPK):
                        sp.wait_ge(s_y, TOPK * (b - 1) + k + 1)
                        load(b, k)

            @block.tensor
            def _(pe):
                def first(b, k):
                    j = TOPK * b + k
                    pe.wait_ge(s_w[k], 64 * (b + 1))
                    for c in range(HB):
                        pe.wait_ge(s_g, HB * j if isinstance(j, int) and j == 0 else HB * (j - 1) + c + 1)
                        pe.matmul(bank[c][:], w1[:, k, P * c:P * c + P], xt[:, b], start=True,
                                  stop=True).then_inc(s_h, 1)

                def second(b, k):
                    j = TOPK * b + k
                    pe.wait_ge(s_g, HB * (j + 1))
                    if not isinstance(b, int) or b > 0:
                        pe.wait_ge(s_x, 1 + j - 1)
                    for t in range(TT):
                        at = bank[4 + k][:, P * t:P * t + P]
                        pe.matmul(at, ones[0:1, :], b2[0:1, k], start=True, stop=False)
                        for c in range(HB):
                            ins = pe.matmul(at, hid[:, k, c, P * t:P * t + P], w2[:, k, c], start=False,
                                            stop=c == HB - 1)
                    ins.then_inc(s_y, 1)

                first(0, 0)
                first(0, 1)
                second(0, 0)
                with pe.Fori(1, B) as b:
                    first(b, 0)
                    second(b - 1, 1)
                    first(b, 1)
                    second(b, 0)
                second(B - 1, 1)

            @block.scalar
            def _(act):
                def job(b, k, first=False):
                    j = TOPK * b + k
                    if not first:
                        act.wait_ge(s_y, j - 1)
                    for c in range(HB):
                        act.wait_ge(s_h, HB * j + c + 1)
                        nc.scalar.activation(hid[:, k, c], bank[c][:], ACT.Gelu, bias=b1[:, k, c:c + 1],
                                             scale=1.0).then_inc(s_g, 1)

                job(0, 0, True)
                job(0, 1, True)
                with act.Fori(1, B) as b:
                    job(b, 0)
                    job(b, 1)

            @block.vector
            def _(dve):
                start_at_one(dve, s_x)
                with dve.Fori(0, B) as b:
                    for k in range(TOPK):
                        j = TOPK * b + k
                        dve.wait_ge(s_y, j + 1)
                        dve.wait_ge(s_x, 1 + j)
                        rows = x[:, bass.ts(b, TT)].rearrange("p t d -> p (t d)")
                        nc.vector.scalar_tensor_tensor(out=rows, in0=bank[4 + k][:], scalar=mix[:, B * k + b, None],
                                                       in1=rows, op0=ALU.mult, op1=ALU.add).then_inc(s_x, 1)


def build(nc, a, out):
    with ExitStack() as ctx:
        core = Core(nc, ctx)
        s_in, s_out = core.sem("x_in"), core.sem("x_out")
        as_tiles = "b (i p) d -> p (b i) d"

        with nc.Block() as block:
            @block.sync
            def _(sp):
                sp.dma_start(core.x[:], a["L0_attn_x"].rearrange(as_tiles, p=P)).then_inc(s_in, 16)
                sp.dma_start(core.ident[:], a["identity"]).then_inc(s_in, 16)
                sp.wait_ge(s_in, 32)

        soft = {k: a["L0_ffn_" + k] for k in
                ("norm_gamma", "slot_norm_gamma", "slot_embeds", "w1", "b1", "w2", "b2")}
        top = {k: a["L1_ffn_" + k] for k in ("gate_w", "w1", "b1", "w2", "b2")}
        soft_moe(core, "s1", soft)
        attention(core, "a1", {"qkv": a["L0_attn_w_qkv"], "out": a["L0_attn_w_out"], "b_out": a["L0_attn_b_out"],
                               "rel": a["distance"], "slopes": a["slopes"]}, True)
        soft_moe(core, "s2", soft)
        top_moe(core, "t1", top)
        attention(core, "a2", {"q": a["L1_attn_w_q"], "kv_up": a["L1_attn_w_kv_up"],
                               "kv_down": a["L1_attn_w_kv_down"], "out": a["L1_attn_w_out"],
                               "rel": a["causal"]}, False)
        top_moe(core, "t2", top)

        with nc.Block() as block:
            @block.sync
            def _(sp):
                sp.dma_start(out.rearrange(as_tiles, p=P), core.x[:]).then_inc(s_out, 16)
                sp.wait_ge(s_out, 16)


def constants():
    gap = np.arange(T)[None, :] - (T - P) - np.arange(P)[:, None]
    return {
        "distance": np.where(gap <= 0, gap, MASKED).astype(np.float32),
        "causal": np.where(gap <= 0, 0.0, MASKED).astype(np.float32),
        "slopes": np.tile(alibi_slopes(), (P, 1)),
        "identity": np.eye(P, dtype=np.float32),
    }


def kernel(**inputs):
    import concourse.bacc as bacc
    from concourse.bass_utils import run_bass_kernel_spmd

    nc = bacc.Bacc("TRN2", target_bir_lowering=False, num_devices=1)
    arrays, args = {}, {}
    for name, value in {**inputs, **constants()}.items():
        value = np.ascontiguousarray(value)
        arrays[f"in_{name}"] = value
        args[name] = nc.dram_tensor(f"in_{name}", value.shape, mybir.dt.from_np(value.dtype),
                                    kind="ExternalInput").ap()
    out = nc.dram_tensor("out", (B, T, D), F32, kind="ExternalOutput").ap()
    build(nc, args, out)
    result = run_bass_kernel_spmd(nc, [arrays], core_ids=[0])
    return result.results[0]["out"]
```

```python
from contextlib import ExitStack

import numpy as np

import concourse.bass as bass
from concourse import mybir

P = 128
B, T, D = 8, 512, 128
TT = T // P
NT = B * TT
H, DH = 16, 64
PAIRS = B * H // 2
E_SLOT, S_SLOT = 8, 64
SLOTS = E_SLOT * S_SLOT
E_MOE, TOPK = 8, 2
HID = 512
HB = HID // P
EPS = 1e-5
MASKED = -3.0e38

ALU = mybir.AluOpType
ACT = mybir.ActivationFunctionType
F32 = mybir.dt.float32
F32R = mybir.dt.float32r
U32 = mybir.dt.uint32
AX = mybir.AxisListType.X

PROB_AT = {3: 0, 2: 512, 0: 896, 1: 1024}
PROBT_AT = {0: 0, 1: 512, 3: 896, 2: 1024}
CAUSAL = TT * (TT + 1) // 2 * P


def alibi_slopes():
    start = 2.0 ** (-8.0 / H)
    return np.array([start ** (i + 1) for i in range(H)], np.float32)


class Core:

    def __init__(self, nc, ctx):
        self.nc, self.ctx, self.in_use = nc, ctx, []
        self.x = self.sb("x_tokens", [P, NT, D])
        self.ident = self.sb("ident", [P, P])
        self.bank = [ctx.enter_context(nc.psum_tensor(f"bank{i}", [P, 512], F32)) for i in range(8)]

    def sb(self, name, shape, dt=F32, ctx=None):
        return (ctx or self.ctx).enter_context(self.nc.sbuf_tensor(name, shape, dt))

    def sem(self, name):
        self.in_use.append(self.nc.alloc_semaphore(name=name))
        return self.in_use[-1]

    def end_phase(self):
        self.nc.clear_and_free_semaphores(self.in_use)
        self.nc.all_engine_barrier()
        self.in_use = []


def start_at_one(engine, *semaphores):
    for s in semaphores:
        engine.sem_inc(s, 1)


def layer_norm_stats_on_vector(nc, dve, x, st, s_stat, s_chain, s_var, s_root):
    with dve.Fori(0, NT // 8) as i:
        for u in range(8):
            nc.vector.bn_stats(st["bn"][:, 8 * i + u], x[:, 8 * i + u]).then_inc(s_stat, 1)
    dve.wait_ge(s_stat, NT)
    bn = st["bn"]
    links = [0]

    def link(ins):
        links[0] += 1
        ins.then_inc(s_chain, 1)
        dve.wait_ge(s_chain, links[0])

    even, odd = bn[:, :, 1], bn[:, :, 4]
    link(nc.vector.tensor_tensor(st["mean"][:], even, odd, ALU.add))
    link(nc.vector.tensor_scalar(st["mean"][:], st["mean"][:], 0.5, None, ALU.mult))
    link(nc.vector.tensor_tensor(st["a"][:], even, odd, ALU.subtract))
    link(nc.vector.tensor_tensor(st["a"][:], st["a"][:], st["a"][:], ALU.mult))
    link(nc.vector.tensor_tensor(st["var"][:], bn[:, :, 2], bn[:, :, 5], ALU.add))
    link(nc.vector.tensor_scalar(st["var"][:], st["var"][:], 1.0 / D, None, ALU.mult))
    link(nc.vector.scalar_tensor_tensor(out=st["var"][:], in0=st["a"][:], scalar=0.25, in1=st["var"][:],
                                        op0=ALU.mult, op1=ALU.add))
    nc.vector.tensor_scalar(st["ve"][:], st["var"][:], EPS, None, ALU.add).then_inc(s_var, 1)
    dve.wait_ge(s_root, 1)
    link(nc.vector.reciprocal(st["rstd"][:], st["root"][:]))
    link(nc.vector.tensor_tensor(st["a"][:], st["rstd"][:], st["rstd"][:], ALU.mult))
    link(nc.vector.tensor_tensor(st["a"][:], st["a"][:], st["ve"][:], ALU.mult))
    link(nc.vector.tensor_scalar(st["a"][:], st["a"][:], -0.5, 1.5, ALU.mult, ALU.add))
    link(nc.vector.tensor_tensor(st["rstd"][:], st["rstd"][:], st["a"][:], ALU.mult))
    return link


def stats_buffers(core, ctx, pre):
    st = {k: core.sb(f"{pre}_{k}", [P, NT], ctx=ctx) for k in ("mean", "var", "ve", "a", "rstd", "root")}
    st["bn"] = core.sb(f"{pre}_bn", [P, NT, 6], ctx=ctx)
    return st


def attention(core, pre, w, alibi):
    nc, x, ident, bank = core.nc, core.x, core.ident, core.bank
    with ExitStack() as ctx:
        def sb(name, shape, dt=F32):
            return core.sb(f"{pre}_{name}", shape, dt, ctx)

        def sem(name):
            return core.sem(f"{pre}_{name}")

        xt_full = sb("xt_full", [P, B, T])
        xt_hi = sb("xt_hi", [P, B, T], F32R)
        xt_lo = sb("xt_lo", [P, B, T], F32R)
        m_split = sb("m_split", [P, H, 2, P], F32R)
        wv = sb("wv", [P, H * DH])
        wo2 = sb("wo2", [P, H, D])
        rel = sb("rel", [P, T])
        slopes = sb("slopes", [P, H])

        prepare(core, pre, w, alibi, xt_full, xt_hi, xt_lo, m_split, wv, wo2, rel, slopes)
        core.end_phase()
        attend(core, pre, alibi, xt_full, xt_hi, xt_lo, m_split, wv, wo2, rel, slopes)
        core.end_phase()


def prepare(core, pre, w, alibi, xt_full, xt_hi, xt_lo, m_split, wv, wo2, rel, slopes):
    nc, x, ident, bank = core.nc, core.x, core.ident, core.bank
    with ExitStack() as ctx:
        def sb(name, shape, dt=F32):
            return core.sb(f"{pre}_{name}", shape, dt, ctx)

        def sem(name):
            return core.sem(f"{pre}p_{name}")

        st = stats_buffers(core, ctx, pre + "_st")
        xn = sb("xn", [P, 2, TT, D])
        wq = sb("wq", [P, H * DH])
        wk = sb("wk", [P, H * DH])
        if not alibi:
            wkv_v = sb("wkv_v", [P, H * DH])
            wkd = sb("wkd", [P, P])
            wkd_t = sb("wkd_t", [P, P])
        else:
            bout = sb("bout", [P, D])
        qk_t = sb("qk_t", [P, 2, 2, P])

        s_w = sem("weights_in")
        s_stat, s_chain, s_var, s_root = sem("stats"), sem("chain"), sem("var"), sem("root")
        s_xn = sem("xn_ready")
        s_turned = sem("turned")
        s_xf, s_xh, s_xl = sem("xt_full"), sem("xt_hi"), sem("xt_lo")
        s_bias = sem("bias_added")
        s_qkm, s_qkt = sem("qk_turned"), sem("qk_copied")
        s_turn, s_mh, s_ml = sem("m_ready"), sem("m_hi"), sem("m_lo")
        s_kd, s_kdt, s_vm, s_vc = sem("kd_turned"), sem("kd_copied"), sem("v_ready"), sem("v_copied")

        n_w = [0]
        with nc.Block() as block:
            @block.sync
            def _(sp):
                def load(dst, src):
                    n_w[0] += 1
                    sp.dma_start(dst, src).then_inc(s_w, 16)

                if alibi:
                    load(wq[:], w["qkv"][:, 0:H * DH])
                    load(wk[:], w["qkv"][:, H * DH:2 * H * DH])
                    load(wv[:], w["qkv"][:, 2 * H * DH:3 * H * DH])
                    load(bout[:], w["b_out"].rearrange("(o d) -> o d", o=1).broadcast_to([P, D]))
                    load(slopes[:], w["slopes"])
                else:
                    load(wq[:], w["q"])
                    load(wk[:], w["kv_up"][:, 0:H * DH])
                    load(wkv_v[:], w["kv_up"][:, H * DH:2 * H * DH])
                    load(wkd[:], w["kv_down"])
                for half in range(2):
                    load(wo2[64 * half:64 * half + 64], w["out"].rearrange("(h d) c -> d h c", d=DH))
                load(rel[:], w["rel"])
                sp.wait_ge(s_w, 16 * n_w[0])

            n_loads = 8 if alibi else 7

            @block.gpsimd
            def _(pool):
                if alibi:
                    pool.wait_ge(s_w, 16 * n_loads)
                    with pool.Fori(0, B) as b:
                        pool.wait_ge(s_xn, b + 1)
                        tiles = x[:, bass.ts(b, TT)]
                        nc.gpsimd.tensor_tensor(tiles, tiles, bout[:, None, :].broadcast_to([P, TT, D]),
                                                ALU.add).then_inc(s_bias, 1)

            @block.vector
            def _(dve):
                start_at_one(dve, s_xl)
                link = layer_norm_stats_on_vector(nc, dve, x, st, s_stat, s_chain, s_var, s_root)

                def m_low(p):
                    dve.wait_ge(s_mh, p + 1)
                    nc.vector.scalar_tensor_tensor(
                        out=m_split[:, 2 * p:2 * p + 2, 1, :],
                        in0=bank[2 + p % 2][:, 0:2 * P].rearrange("p (u c) -> p u c", u=2), scalar=DH ** -0.5,
                        in1=m_split[:, 2 * p:2 * p + 2, 0, :].bitcast(F32), op0=ALU.mult,
                        op1=ALU.subtract).then_inc(s_ml, 1)

                with dve.Fori(0, B // 2) as i:
                    for u in range(2):
                        b = 2 * i + u
                        dve.wait_ge(s_turned, b + 1)
                        for t in range(TT):
                            k = TT * b + t
                            ins = nc.vector.tensor_scalar(xn[:, u, t], x[:, k], st["mean"][:, k, None],
                                                          st["rstd"][:, k, None], ALU.subtract, ALU.mult)
                        ins.then_inc(s_xn, 1)
                        dve.wait_ge(s_xh, b + 1)
                        nc.vector.tensor_tensor(xt_lo[:, b], bank[4 + u][:], xt_hi[:, b].bitcast(F32),
                                                ALU.subtract).then_inc(s_xl, 1)
                for p in range(H // 2):
                    m_low(p)

            @block.scalar
            def _(act):
                act.wait_ge(s_var, 1)
                nc.scalar.activation(st["root"][:], st["ve"][:], ACT.Sqrt).then_inc(s_root, 1)
                with act.Fori(0, B // 2) as i:
                    for u in range(2):
                        b = 2 * i + u
                        act.wait_ge(s_turned, b + 3)
                        nc.scalar.copy(xt_full[:, b], bank[4 + u][:]).then_inc(s_xf, 1)
                        nc.scalar.copy(xt_hi[:, b], bank[4 + u][:]).then_inc(s_xh, 1)
                if not alibi:
                    act.wait_ge(s_kd, 1)
                    nc.scalar.copy(wkd_t[:], bank[7][:, 0:P]).then_inc(s_kdt, 1)
                    for c in range(2):
                        act.wait_ge(s_vm, c + 1)
                        nc.scalar.copy(wv[:, 512 * c:512 * c + 512], bank[6][:]).then_inc(s_vc, 1)
                for p in range(H // 2):
                    act.wait_ge(s_qkm, p + 1)
                    nc.scalar.copy(qk_t[:, p % 2].rearrange("p a c -> p (a c)"),
                                   bank[p % 2][:, 0:2 * P]).then_inc(s_qkt, 1)
                    act.wait_ge(s_turn, 2 * p + 2)
                    nc.scalar.mul(m_split[:, 2 * p:2 * p + 2, 0, :],
                                  bank[2 + p % 2][:, 0:2 * P].rearrange("p (u c) -> p u c", u=2),
                                  DH ** -0.5).then_inc(s_mh, 1)

            @block.tensor
            def _(pe):
                pe.sem_inc(s_turned, 2)
                with pe.Fori(0, B // 2) as i:
                    for u in range(2):
                        b = 2 * i + u
                        pe.wait_ge(s_xn, b + 1)
                        pe.wait_ge(s_xl, 1 + 2 * i)
                        for t in range(TT):
                            ins = pe.transpose(bank[4 + u][:, P * t:P * t + P], xn[:, u, t], ident[:])
                        ins.then_inc(s_turned, 1)
                pe.wait_ge(s_w, 16 * n_loads)
                if not alibi:
                    pe.transpose(bank[7][:, 0:P], wkd[:], ident[:]).then_inc(s_kd, 1)
                    pe.wait_ge(s_kdt, 1)
                    for c in range(2):
                        pe.wait_ge(s_vc, c)
                        pe.matmul(bank[6][:], wkd_t[:], wkv_v[:, 512 * c:512 * c + 512], start=True,
                                  stop=True).then_inc(s_vm, 1)
                for p in range(H // 2):
                    cols = slice(P * p, P * p + P)
                    if p >= 2:
                        pe.wait_ge(s_qkt, p - 1)
                    pe.transpose(bank[p % 2][:, 0:P], wq[:, cols], ident[:])
                    if alibi:
                        pe.transpose(bank[p % 2][:, P:2 * P], wk[:, cols], ident[:]).then_inc(s_qkm, 1)
                    else:
                        pe.matmul(bank[p % 2][:, P:2 * P], wk[:, cols], wkd_t[:], start=True,
                                  stop=True).then_inc(s_qkm, 1)
                    pe.wait_ge(s_qkt, p + 1)
                    if p >= 2:
                        pe.wait_ge(s_ml, p - 1)
                    for u in range(2):
                        rows = slice(DH * u, DH * u + DH)
                        pe.wait_ge(s_turn, 2 * p + u)
                        pe.matmul(bank[2 + p % 2][:, P * u:P * u + P], qk_t[rows, p % 2, 0],
                                  qk_t[rows, p % 2, 1], start=True, stop=True).then_inc(s_turn, 1)


def attend(core, pre, alibi, xt_full, xt_hi, xt_lo, m_split, wv, wo2, rel, slopes):
    nc, x, ident, bank = core.nc, core.x, core.ident, core.bank
    proj, s3, s20, s1, turn0, turn1, av, outp = bank
    score_at = {3: s3[:, 0:512], 2: s20[:, 0:384], 0: s20[:, 384:512], 1: s1[:, 0:256]}
    ORDER = (3, 2, 0, 1)
    groups = ((turn0, (0,), 0, 512), (turn1, (1, 3), 512, 512), (turn0, (2,), 1024, 256))
    with ExitStack() as ctx:
        def sb(name, shape, dt=F32):
            return core.sb(f"{pre}_{name}", shape, dt, ctx)

        def sem(name):
            return core.sem(f"{pre}a_{name}")

        m_head = sb("m_head", [P, 2, 2, P], F32R)
        wo_head = sb("wo_head", [P, 2, D])
        wv_pair = sb("wv_pair", [P, P])
        xt_seq = sb("xt_seq", [P, T])
        bias = sb("bias", [P, 2, T]) if alibi else None
        q_hi = sb("q_hi", [P, 2, T], F32R)
        q_lo = sb("q_lo", [P, 2, T], F32R)
        v2 = sb("v2", [P, TT, 2, 2, DH], F32R)
        prob = sb("prob", [P, 2, CAUSAL])
        neg_max = sb("neg_max", [P, 2, TT])
        total = sb("total", [P, 2, TT])
        inv = sb("inv", [P, 2, TT])
        pt_hi = sb("pt_hi", [P, 2, CAUSAL], F32R)
        pt_lo = sb("pt_lo", [P, 2, CAUSAL], F32R)
        av_t = sb("av_t", [P, T])

        s_m, s_wo = [sem("m0_in"), sem("m1_in")], [sem("wo0_in"), sem("wo1_in")]
        s_wv = sem("wv_xt_in")
        s_bias = sem("bias_made")
        s_q, s_qh, s_ql = sem("q_ready"), sem("q_hi"), sem("q_lo")
        s_v, s_vh, s_vl = sem("v_ready"), sem("v_hi"), sem("v_lo")
        s_s, s_st, s_exp = sem("scores_ready"), sem("scores_shifted"), sem("probs_ready")
        s_t, s_th, s_tl = sem("probs_turned"), sem("pt_hi"), sem("pt_lo")
        s_av, s_avc, s_out, s_x = sem("av_ready"), sem("av_copied"), sem("out_ready"), sem("x_added")
        s_inv, s_go = sem("inv_ready"), sem("scores_seen")

        def slots(slot, loop):
            slot(0, 0, "PS")
            slot(0, 1, "PSTV")
            slot(1, 0, "PSTA")
            slot(1, 1, "PSTAOV")
            with loop(2, PAIRS - 1) as n:
                slot(n, 0, "PSTAO")
                slot(n, 1, "PSTAOV")
            slot(PAIRS - 1, 0, "STAO")
            slot(PAIRS - 1, 1, "STAOV")
            slot(PAIRS, 0, "TAO")
            slot(PAIRS, 1, "AO")
            slot(PAIRS + 1, 0, "O")

        def before(n, u):
            return (n - 1, 1) if u == 0 else (n, 0)

        def seq(n):
            return n // (H // 2)

        def head(n, u):
            return (n % (H // 2)) * 2 + u

        with nc.Block() as block:
            @block.sync
            def _(sp):
                def m_of(n, u):
                    if not isinstance(n, int) or n > 0:
                        sp.wait_ge(s_q, 2 * n + u - 1)
                    sp.dma_start(m_head[:, u].bitcast(F32), m_split[:, head(n, u)].bitcast(F32)).then_inc(s_m[u], 16)

                def wo_of(n, u, first=False):
                    if not first:
                        sp.wait_ge(s_out, 2 * n + u - 1)
                    sp.dma_start(wo_head[:, u], wo2[:, head(n, u)]).then_inc(s_wo[u], 16)

                def values_of(n, first=False):
                    if not first:
                        sp.wait_ge(s_v, n)
                    sp.dma_start(wv_pair[:], wv[:, bass.ts(n % (H // 2), P)]).then_inc(s_wv, 16)
                    sp.dma_start(xt_seq[:], xt_full[:, seq(n)]).then_inc(s_wv, 16)

                m_of(0, 0)
                m_of(0, 1)
                values_of(0, True)
                wo_of(0, 0, True)
                wo_of(0, 1, True)
                m_of(1, 0)
                m_of(1, 1)
                m_of(2, 0)
                m_of(2, 1)
                values_of(1)
                with sp.Fori(2, PAIRS - 1) as n:
                    m_of(n + 1, 0)
                    m_of(n + 1, 1)
                    values_of(n)
                    wo_of(n - 1, 0)
                    wo_of(n - 1, 1)
                values_of(PAIRS - 1)
                wo_of(PAIRS - 2, 0)
                wo_of(PAIRS - 2, 1)
                wo_of(PAIRS - 1, 0)
                wo_of(PAIRS - 1, 1)

            @block.gpsimd
            def _(pool):
                if not alibi:
                    return

                def bias_of(n, u, first=False):
                    if not first:
                        pool.wait_ge(s_st, TT * (2 * n + u - 1))
                    nc.gpsimd.tensor_tensor(bias[:, u], rel[:], slopes[:, head(n, u), None].broadcast_to([P, T]),
                                            ALU.mult).then_inc(s_bias, 1)

                bias_of(0, 0, True)
                bias_of(0, 1, True)
                with pool.Fori(1, PAIRS) as n:
                    bias_of(n, 0)
                    bias_of(n, 1)

            @block.tensor
            def _(pe):
                def project(n, u):
                    g = 2 * n + u
                    pe.wait_ge(s_m[u], 16 * (n + 1))
                    xh, xl = xt_hi[:, seq(n)], xt_lo[:, seq(n)]
                    pe.matmul(proj[:], m_head[:, u, 0], xh, start=True, stop=False)
                    pe.matmul(proj[:], m_head[:, u, 0], xl, start=False, stop=False)
                    pe.matmul(proj[:], m_head[:, u, 1], xh, start=False, stop=True).then_inc(s_q, 1)

                def values(n, full):
                    if full:
                        pe.wait_ge(s_x, 1 + TT * (2 * n - 1))
                    pe.wait_ge(s_wv, 32 * (n + 1))
                    for j in range(TT):
                        ins = pe.matmul(outp[:, P * j:P * j + P], xt_seq[:, P * j:P * j + P], wv_pair[:],
                                        start=True, stop=True)
                    ins.then_inc(s_v, 1)

                def scores(n, u, k, first=False):
                    g, i = 2 * n + u, ORDER[k]
                    if k == 0:
                        pe.wait_ge(s_ql, g + 1)
                    if not first and k in (0, 1, 3):
                        pe.wait_ge(s_st, TT * (g - 1) + (1, 3, 0, 4)[k])
                    keys = slice(0, P * (i + 1))
                    rows = slice(P * i, P * i + P)
                    at = score_at[i]
                    pe.matmul(at, q_hi[:, u, rows], xt_hi[:, seq(n), keys], start=True, stop=False)
                    pe.matmul(at, q_hi[:, u, rows], xt_lo[:, seq(n), keys], start=False, stop=False)
                    pe.matmul(at, q_lo[:, u, rows], xt_hi[:, seq(n), keys], start=False,
                              stop=True).then_inc(s_s, 1)

                def turn(n, u, c):
                    g = 2 * n + u
                    to, tiles, at, _ = groups[c]
                    if c == 0:
                        pe.wait_ge(s_exp, TT * (g + 1))
                    if c == 2:
                        pe.wait_ge(s_tl, 3 * g + 1)
                    elif not (isinstance(g, int) and g == 0):
                        pe.wait_ge(s_tl, 3 * g - c)
                    for j in tiles:
                        for i in range(j, TT):
                            col = PROBT_AT[j] - at + P * (i - j)
                            src = PROB_AT[i] + P * j
                            ins = pe.transpose(to[:, col:col + P], prob[:, u, src:src + P], ident[:])
                    ins.then_inc(s_t, 1)

                def sum_values(n, u):
                    g = 2 * n + u
                    if not (isinstance(g, int) and g == 0):
                        pe.wait_ge(s_avc, g)
                    if u == 0:
                        pe.wait_ge(s_vl, n + 1)
                    for c, (_, tiles, _, _) in enumerate(groups):
                        pe.wait_ge(s_tl, 3 * g + c + 1)
                        for j in tiles:
                            at = PROBT_AT[j]
                            cols = slice(at, at + T - P * j)
                            lhs = v2[:, j, u].rearrange("p a d -> p (a d)")
                            pe.matmul(av[:, P * j:T], lhs, pt_hi[:, u, cols], start=j == 0, stop=False)
                            ins = pe.matmul(av[:, P * j:T], lhs, pt_lo[:, u, cols], start=False, stop=j == 2)
                    ins.then_inc(s_av, 1)

                def output(n, u):
                    g = 2 * n + u
                    pe.wait_ge(s_avc, g + 1)
                    pe.wait_ge(s_wo[u], 16 * (n + 1))
                    if not (isinstance(g, int) and g == 0):
                        pe.wait_ge(s_x, 1 + TT * g)
                    if u == 1 and not (isinstance(n, int) and n == PAIRS - 1):
                        pe.wait_ge(s_vl, n + 2)
                    for i in range(TT):
                        ins = pe.matmul(outp[:, P * i:P * i + P], av_t[:, P * i:P * i + P], wo_head[:, u],
                                        start=True, stop=True)
                    ins.then_inc(s_out, 1)

                def slot(n, u, work):
                    if "S" in work:
                        for k in range(TT):
                            scores(n, u, k, isinstance(n, int) and n == 0 and u == 0)
                    if "O" in work:
                        output(*before(n - 1, u))
                    if "T" in work:
                        turn(*before(n, u), 0)
                        turn(*before(n, u), 1)
                    if "P" in work:
                        pe.wait_ge(s_ql, 2 * n + u + 2)
                        project(n + 1, u)
                    if "A" in work:
                        sum_values(n - 1, u)
                    if "T" in work:
                        turn(*before(n, u), 2)
                    if "V" in work:
                        values(n, "O" in work)

                project(0, 0)
                pe.wait_ge(s_ql, 1)
                project(0, 1)
                slots(slot, pe.Fori)

            @block.scalar
            def _(act):
                def q_high(n, u):
                    act.wait_ge(s_q, 2 * n + u + 1)
                    nc.scalar.copy(q_hi[:, u], proj[:]).then_inc(s_qh, 1)

                def v_high(n):
                    act.wait_ge(s_v, n + 1)
                    nc.scalar.copy(v2[:, :, :, 0], outp[:].rearrange("p (j u d) -> p j u d", j=TT, u=2))\
                        .then_inc(s_vh, 1)

                def probs(n, u, k):
                    g = 2 * n + u
                    i = ORDER[k]
                    at = PROB_AT[i]
                    tile = prob[:, u, at:at + P * (i + 1)]
                    act.wait_ge(s_st, TT * g + k + 1)
                    nc.scalar.activation(tile, tile, ACT.Exp, bias=neg_max[:, u, i:i + 1], scale=-1.0,
                                         accum_out=total[:, u, i:i + 1]).then_inc(s_exp, 1)

                def pt_high(n, u, c):
                    to, _, at, size = groups[c]
                    act.wait_ge(s_t, 3 * (2 * n + u) + c + 1)
                    nc.scalar.copy(pt_hi[:, u, at:at + size], to[:, 0:size]).then_inc(s_th, 1)

                def av_copy(n, u):
                    act.wait_ge(s_av, 2 * n + u + 1)
                    nc.scalar.copy(av_t[:], av[:]).then_inc(s_avc, 1)

                def slot(n, u, work):
                    if "S" in work:
                        probs(n, u, 0)
                        probs(n, u, 1)
                    if "T" in work:
                        pt_high(*before(n, u), 0)
                        pt_high(*before(n, u), 1)
                    if "S" in work:
                        probs(n, u, 2)
                    if "P" in work:
                        q_high(n + 1, u)
                    if "S" in work:
                        probs(n, u, 3)
                    if "A" in work:
                        av_copy(n - 1, u)
                    if "T" in work:
                        pt_high(*before(n, u), 2)
                    if "V" in work:
                        v_high(n)

                q_high(0, 0)
                q_high(0, 1)
                slots(slot, act.Fori)

            @block.vector
            def _(dve):
                start_at_one(dve, s_x)
                def q_low(n, u):
                    dve.wait_ge(s_qh, 2 * n + u + 1)
                    nc.vector.tensor_tensor(q_lo[:, u], proj[:], q_hi[:, u].bitcast(F32),
                                            ALU.subtract).then_inc(s_ql, 1)

                def v_low(n):
                    dve.wait_ge(s_vh, n + 1)
                    nc.vector.tensor_tensor(v2[:, :, :, 1], outp[:].rearrange("p (j u d) -> p j u d", j=TT, u=2),
                                            v2[:, :, :, 0].bitcast(F32), ALU.subtract).then_inc(s_vl, 1)

                def shift(n, u, k, first=False):
                    g = 2 * n + u
                    if k == 0:
                        if not first:
                            dve.wait_ge(s_t, 3 * (g - 1))
                        if alibi:
                            dve.wait_ge(s_bias, g + 1)
                    for i in (ORDER[k],):
                        dve.wait_ge(s_s, TT * g + (1, 3, 3, 4)[k])
                        dve.sem_inc(s_go, 1)
                        at = PROB_AT[i]
                        size = P * (i + 1)
                        table = bias[:, u] if alibi else rel
                        nc.vector.tensor_tensor_reduce(
                            out=prob[:, u, at:at + size], in0=score_at[i], in1=table[:, T - size:T],
                            scale=-1.0, scalar=-MASKED, op0=ALU.add, op1=ALU.min,
                            accum_out=neg_max[:, u, i:i + 1]).then_inc(s_st, 1)

                def pt_low(n, u, c):
                    to, _, at, size = groups[c]
                    dve.wait_ge(s_th, 3 * (2 * n + u) + c + 1)
                    nc.vector.tensor_tensor(pt_lo[:, u, at:at + size], to[:, 0:size], pt_hi[:, u, at:at + size].bitcast(F32),
                                            ALU.subtract).then_inc(s_tl, 1)

                def invert(n, u, first=False):
                    g = 2 * n + u
                    dve.wait_ge(s_exp, TT * (g + 1))
                    if not first:
                        dve.wait_ge(s_x, 1 + TT * (g - 1))
                    nc.vector.reciprocal(inv[:, u], total[:, u]).then_inc(s_inv, 1)

                def add_output(n, u):
                    g = 2 * n + u
                    dve.wait_ge(s_out, g + 1)
                    dve.wait_ge(s_inv, g + 1)
                    dve.wait_ge(s_x, 1 + TT * g)
                    for i in range(TT):
                        tile = x[:, seq(n) * TT + i]
                        nc.vector.scalar_tensor_tensor(out=tile, in0=outp[:, P * i:P * i + P], scalar=inv[:, u, i:i + 1],
                                                       in1=tile, op0=ALU.mult, op1=ALU.add).then_inc(s_x, 1)

                def slot(n, u, work):
                    if "S" in work:
                        for k in range(TT):
                            shift(n, u, k, isinstance(n, int) and n == 0)
                    if "O" in work:
                        add_output(*before(n - 1, u))
                    if "T" in work:
                        pt_low(*before(n, u), 0)
                        pt_low(*before(n, u), 1)
                    if "P" in work:
                        q_low(n + 1, u)
                    if "T" in work:
                        invert(*before(n, u), "O" not in work)
                        pt_low(*before(n, u), 2)
                    if "V" in work:
                        v_low(n)

                q_low(0, 0)
                q_low(0, 1)
                slots(slot, dve.Fori)


def refine_root(nc, link, y, v, a):
    link(nc.vector.tensor_tensor(a, y, y, ALU.mult))
    link(nc.vector.tensor_tensor(a, a, v, ALU.mult))
    link(nc.vector.tensor_scalar(a, a, -0.5, 1.5, ALU.mult, ALU.add))
    link(nc.vector.tensor_tensor(y, y, a, ALU.mult))


def soft_moe(core, pre, w):
    nc, x = core.nc, core.x
    with ExitStack() as ctx:
        def sb(name, shape, dt=F32):
            return core.sb(f"{pre}_{name}", shape, dt, ctx)

        combine_t = sb("combine_t", [P, B, TT, T])
        slots = sb("slots", [P, E_SLOT, B, S_SLOT])
        expert_out = sb("expert_out", [P, E_SLOT, B, S_SLOT])
        half_inv = sb("half_inv", [P, NT])
        b1_t = sb("b1_t", [P, E_SLOT * HB])
        b2_t = sb("b2_t", [P, E_SLOT])
        dispatch(core, pre, w, combine_t, slots, half_inv, b1_t, b2_t)
        core.end_phase()
        slot_experts(core, pre, w, slots, expert_out, b1_t, b2_t)
        core.end_phase()
        combine(core, pre, combine_t, expert_out, half_inv)
        core.end_phase()


def dispatch(core, pre, w, combine_t, slots, half_inv, b1_t, b2_t):
    nc, x, ident, bank = core.nc, core.x, core.ident, core.bank
    ST = SLOTS // P
    with ExitStack() as ctx:
        def sb(name, shape, dt=F32):
            return core.sb(f"{pre}_{name}", shape, dt, ctx)

        def sem(name):
            return core.sem(f"{pre}d_{name}")

        st = stats_buffers(core, ctx, pre + "_st")
        emb = sb("emb", [P, ST, D])
        square = sb("square", [P, D])
        norm2 = sb("norm2", [P, NT + ST])
        norm = sb("norm", [P, NT + ST])
        scale = sb("scale", [P, NT + ST])
        scratch = sb("scratch", [P, NT + ST])
        gammas = sb("gammas", [P, 2])
        gamma2 = sb("gamma2", [P, 1])
        emb_t = sb("emb_t", [P, SLOTS])
        b1_rows = sb("b1_rows", [E_SLOT * HB, P])
        b2_rows = sb("b2_rows", [E_SLOT, D])
        z = sb("z", [P, 2, TT, D])
        z_t = sb("z_t", [P, 2, T])
        neg_max = sb("neg_max", [P, 2, 2 * TT])
        total = sb("total", [P, 2, 2 * TT])
        inv = sb("inv", [P, 2, 2 * TT])
        prob = sb("prob", [P, 2, 2 * TT, T])
        disp = sb("disp", [P, TT, SLOTS])

        s_in = sem("inputs_in")
        s_stat, s_chain, s_var, s_root = sem("stats"), sem("chain"), sem("var"), sem("root")
        s_norm2, s_norm = sem("norm2"), sem("norm")
        s_emb, s_embm, s_embt = sem("slots_normed"), sem("slots_turned"), sem("slots_copied")
        s_z, s_zm, s_zt = sem("z_ready"), sem("z_turned"), sem("z_copied")
        s_l, s_max, s_exp = sem("logits"), sem("max"), sem("probs")
        s_inv, s_nrm = sem("inv_ready"), sem("dispatch_normed")
        s_t, s_dc, s_cc = sem("probs_turned"), sem("dispatch_copied"), sem("combine_copied")
        s_sl, s_slc = sem("slots_ready"), sem("slots_copied_out")
        s_bt, s_btc = sem("biases_turned"), sem("biases_copied")

        with nc.Block() as block:
            @block.sync
            def _(sp):
                sp.dma_start(emb[:], w["slot_embeds"].rearrange("e s d -> (e s) d")
                             .rearrange("(k p) d -> p k d", p=P)).then_inc(s_in, 16)
                sp.dma_start(gammas[:, 0:1], w["norm_gamma"].rearrange("(d o) -> d o", o=1)).then_inc(s_in, 16)
                sp.dma_start(gammas[:, 1:2], w["slot_norm_gamma"].rearrange("(d o) -> d o", o=1)).then_inc(s_in, 16)
                sp.dma_start(b1_rows[:], w["b1"].rearrange("e (k p) -> (e k) p", p=P)).then_inc(s_in, 16)
                sp.dma_start(b2_rows[:], w["b2"]).then_inc(s_in, 16)

            @block.vector
            def _(dve):
                start_at_one(dve, s_nrm, s_cc, s_slc)
                link = layer_norm_stats_on_vector(nc, dve, x, st, s_stat, s_chain, s_var, s_root)
                n2 = norm2[:, 0:NT]
                link(nc.vector.tensor_tensor(n2, st["rstd"][:], st["rstd"][:], ALU.mult))
                link(nc.vector.tensor_tensor(n2, n2, st["var"][:], ALU.mult))
                link(nc.vector.tensor_scalar(n2, n2, float(D), None, ALU.mult))
                dve.wait_ge(s_in, 16 * 5)
                for k in range(ST):
                    link(nc.vector.tensor_tensor_reduce(out=square[:], in0=emb[:, k], in1=emb[:, k], scale=1.0,
                                                        scalar=0.0, op0=ALU.mult, op1=ALU.add,
                                                        accum_out=norm2[:, NT + k:NT + k + 1]))
                nc.vector.tensor_scalar(norm2[:], norm2[:], 1e-24, None, ALU.max).then_inc(s_norm2, 1)
                dve.wait_ge(s_norm2, 1)
                dve.wait_ge(s_norm, 1)
                link(nc.vector.reciprocal(scale[:], norm[:]))
                refine_root(nc, link, scale[:], norm2[:], scratch[:])
                link(nc.vector.tensor_scalar(scale[:], scale[:], float(D) ** 0.5, None, ALU.mult))
                link(nc.vector.tensor_tensor(scale[:, 0:NT], scale[:, 0:NT], st["rstd"][:], ALU.mult))
                for k in range(ST):
                    ins = nc.vector.tensor_scalar(emb[:, k], emb[:, k], scale[:, NT + k:NT + k + 1], None, ALU.mult)
                ins.then_inc(s_emb, 1)
                link(nc.vector.tensor_tensor(gamma2[:], gammas[:, 0:1], gammas[:, 1:2], ALU.mult))
                dve.wait_ge(s_embm, 1)
                nc.vector.tensor_scalar(emb_t[:], bank[0][:], gamma2[:, 0:1], None, ALU.mult).then_inc(s_embt, 1)
                dve.wait_ge(s_bt, 1)
                nc.vector.tensor_copy(b1_t[:], bank[7][:, 0:E_SLOT * HB]).then_inc(s_btc, 1)
                nc.vector.tensor_copy(b2_t[:], bank[7][:, P:P + E_SLOT]).then_inc(s_btc, 1)

                def normed(b, u, i):
                    dve.wait_ge(s_sl, 1 + 2 * i)
                    for t in range(TT):
                        k = TT * b + t
                        ins = nc.vector.tensor_scalar(z[:, u, t], x[:, k], st["mean"][:, k, None], scale[:, k, None],
                                                      ALU.subtract, ALU.mult)
                    ins.then_inc(s_z, 1)

                def maxima(b, u, i):
                    dve.wait_ge(s_exp, 1 + 16 * i)
                    for k in range(2 * TT):
                        dve.wait_ge(s_l, 8 * b + k + 1)
                        nc.vector.tensor_reduce(neg_max[:, u, k:k + 1], bank[1 + k % 4][:], AX, ALU.max,
                                                negate=True).then_inc(s_max, 1)

                def norm_dispatch(b, u):
                    dve.wait_ge(s_exp, 1 + 8 * (b + 1))
                    dve.wait_ge(s_nrm, 1 + 5 * b)
                    nc.vector.reciprocal(inv[:, u], total[:, u]).then_inc(s_inv, 1)
                    dve.wait_ge(s_inv, b + 1)
                    for k in range(TT):
                        nc.vector.tensor_scalar(prob[:, u, k], prob[:, u, k], inv[:, u, k:k + 1], None,
                                                ALU.mult).then_inc(s_nrm, 1)
                    nc.vector.tensor_scalar(half_inv[:, bass.ts(b, TT)], inv[:, u, TT:2 * TT], 0.5, None,
                                            ALU.mult).then_inc(s_nrm, 1)

                def copy_combine(b):
                    for k in range(ST):
                        dve.wait_ge(s_t, 1 + 8 * b + TT + k + 1)
                        nc.vector.tensor_copy(combine_t[:, b, k], bank[5 + k % 2][:]).then_inc(s_cc, 1)

                def copy_slots(b):
                    dve.wait_ge(s_sl, 1 + b + 1)
                    nc.vector.tensor_scalar(slots[:, :, b], bank[7][:].rearrange("p (e s) -> p e s", e=E_SLOT),
                                            gammas[:, 0:1], None, ALU.mult).then_inc(s_slc, 1)

                with dve.Fori(0, B // 2) as i:
                    for u in range(2):
                        normed(2 * i + u, u, i)
                    for u in range(2):
                        maxima(2 * i + u, u, i)
                        norm_dispatch(2 * i + u, u)
                    for u in range(2):
                        copy_combine(2 * i + u)
                        copy_slots(2 * i + u)

            @block.scalar
            def _(act):
                start_at_one(act, s_exp, s_zt)
                act.wait_ge(s_var, 1)
                nc.scalar.activation(st["root"][:], st["ve"][:], ACT.Sqrt).then_inc(s_root, 1)
                act.wait_ge(s_norm2, 1)
                nc.scalar.activation(norm[:], norm2[:], ACT.Sqrt).then_inc(s_norm, 1)
                with act.Fori(0, B // 2) as i:
                    for u in range(2):
                        b = 2 * i + u
                        act.wait_ge(s_zm, b + 1)
                        nc.scalar.copy(z_t[:, u], bank[0][:]).then_inc(s_zt, 1)
                    for u in range(2):
                        b = 2 * i + u
                        act.wait_ge(s_t, 1 + 16 * i)
                        for k in range(2 * TT):
                            act.wait_ge(s_max, 8 * b + k + 1)
                            nc.scalar.activation(prob[:, u, k], bank[1 + k % 4][:], ACT.Exp,
                                                 bias=neg_max[:, u, k:k + 1], scale=1.0,
                                                 accum_out=total[:, u, k:k + 1]).then_inc(s_exp, 1)
                    for u in range(2):
                        b = 2 * i + u
                        act.wait_ge(s_sl, 1 + b)
                        for t in range(TT):
                            act.wait_ge(s_t, 1 + 8 * b + t + 1)
                            nc.scalar.copy(disp[:, t], bank[5 + t % 2][:]).then_inc(s_dc, 1)

            @block.tensor
            def _(pe):
                start_at_one(pe, s_sl, s_t)
                pe.wait_ge(s_in, 16 * 5)
                pe.wait_ge(s_emb, 1)
                for k in range(ST):
                    ins = pe.transpose(bank[0][:, P * k:P * k + P], emb[:, k], ident[:])
                ins.then_inc(s_embm, 1)
                pe.transpose(bank[7][:, 0:E_SLOT * HB], b1_rows[:], ident[0:E_SLOT * HB, 0:E_SLOT * HB])
                pe.transpose(bank[7][:, P:P + E_SLOT], b2_rows[:], ident[0:E_SLOT, 0:E_SLOT]).then_inc(s_bt, 1)
                pe.wait_ge(s_embt, 1)
                pe.wait_ge(s_btc, 2)

                def turn_tokens(b, u):
                    pe.wait_ge(s_z, b + 1)
                    pe.wait_ge(s_zt, 1 + b)
                    for t in range(TT):
                        ins = pe.transpose(bank[0][:, P * t:P * t + P], z[:, u, t], ident[:])
                    ins.then_inc(s_zm, 1)

                def logits(b, u):
                    pe.wait_ge(s_zt, 1 + b + 1)
                    for k in range(2 * TT):
                        if k >= 4:
                            pe.wait_ge(s_exp, 1 + 8 * b + k - 3)
                        else:
                            pe.wait_ge(s_exp, 1 + 8 * b)
                        to = bank[1 + k % 4][:]
                        if k < TT:
                            ins = pe.matmul(to, emb_t[:, P * k:P * k + P], z_t[:, u], start=True, stop=True)
                        else:
                            ins = pe.matmul(to, z_t[:, u, P * (k - TT):P * (k - TT) + P], emb_t[:],
                                            start=True, stop=True)
                        ins.then_inc(s_l, 1)

                def turn_probs(b, u):
                    pe.wait_ge(s_nrm, 1 + 5 * (b + 1))
                    for r in range(2 * TT):
                        if r < 2:
                            pe.wait_ge(s_cc, 1 + TT * b)
                        elif r < 6:
                            pe.wait_ge(s_dc, TT * b + r - 1)
                        else:
                            pe.wait_ge(s_cc, 1 + TT * b + r - 5)
                        rows = 0 if r < TT else TT
                        col = P * (r % TT)
                        for k in range(TT):
                            ins = pe.transpose(bank[5 + r % 2][:, P * k:P * k + P],
                                               prob[:, u, rows + k, col:col + P], ident[:])
                        ins.then_inc(s_t, 1)

                def slot_sums(b, u):
                    pe.wait_ge(s_dc, TT * (b + 1))
                    pe.wait_ge(s_slc, 1 + b)
                    for t in range(TT):
                        ins = pe.matmul(bank[7][:], z[:, u, t], disp[:, t], start=t == 0, stop=t == TT - 1)
                    ins.then_inc(s_sl, 1)

                with pe.Fori(0, B // 2) as i:
                    for u in range(2):
                        turn_tokens(2 * i + u, u)
                    for u in range(2):
                        logits(2 * i + u, u)
                    for u in range(2):
                        turn_probs(2 * i + u, u)
                        slot_sums(2 * i + u, u)


def slot_experts(core, pre, w, slots, expert_out, b1_t, b2_t):
    nc, bank = core.nc, core.bank
    N = B * S_SLOT
    with ExitStack() as ctx:
        def sb(name, shape, dt=F32):
            return core.sb(f"{pre}_{name}", shape, dt, ctx)

        def sem(name):
            return core.sem(f"{pre}e_{name}")

        w1 = sb("w1", [P, 2, HID])
        w2 = sb("w2", [P, 2, HB, D])
        hid = sb("hid", [P, 2, HB, N])
        s_w = [sem("w0_in"), sem("w1_in")]
        s_h, s_g, s_o, s_oc = sem("hidden"), sem("gelu"), sem("out"), sem("out_copied")

        with nc.Block() as block:
            @block.sync
            def _(sp):
                def load(e, u):
                    sp.dma_start(w1[:, u], w["w1"][e]).then_inc(s_w[u], 16)
                    sp.dma_start(w2[:, u], w["w2"][e].rearrange("(k p) d -> p k d", p=P)).then_inc(s_w[u], 16)

                load(0, 0)
                load(1, 1)
                with sp.Fori(1, E_SLOT // 2) as i:
                    for u in range(2):
                        sp.wait_ge(s_o, 1 + 2 * i + u - 1)
                        load(2 * i + u, u)

            @block.tensor
            def _(pe):
                start_at_one(pe, s_o)
                def first(e, u, i):
                    pe.wait_ge(s_w[u], 32 * (i + 1))
                    for k in range(HB):
                        if k == 0:
                            pe.wait_ge(s_g, 1 + HB * e)
                        pe.matmul(bank[k][:], w1[:, u, P * k:P * k + P], slots[:, e].rearrange("p b s -> p (b s)"),
                                  start=True, stop=True).then_inc(s_h, 1)

                def second(e, u):
                    pe.wait_ge(s_oc, 1 + e)
                    for k in range(HB):
                        pe.wait_ge(s_g, 1 + HB * e + k + 1)
                        ins = pe.matmul(bank[4 + u][:], w2[:, u, k], hid[:, u, k], start=k == 0, stop=k == HB - 1)
                    ins.then_inc(s_o, 1)

                with pe.Fori(0, E_SLOT // 2) as i:
                    first(2 * i, 0, i)
                    first(2 * i + 1, 1, i)
                    second(2 * i, 0)
                    second(2 * i + 1, 1)

            @block.scalar
            def _(act):
                start_at_one(act, s_g)
                with act.Fori(0, E_SLOT // 2) as i:
                    for u in range(2):
                        e = 2 * i + u
                        act.wait_ge(s_o, 1 + 2 * i)
                        for k in range(HB):
                            act.wait_ge(s_h, HB * e + k + 1)
                            nc.scalar.activation(hid[:, u, k], bank[k][:], ACT.Gelu,
                                                 bias=b1_t[:, HB * e + k, None], scale=1.0).then_inc(s_g, 1)

            @block.vector
            def _(dve):
                start_at_one(dve, s_oc)
                with dve.Fori(0, E_SLOT // 2) as i:
                    for u in range(2):
                        e = 2 * i + u
                        dve.wait_ge(s_o, 1 + e + 1)
                        nc.vector.tensor_scalar(expert_out[:, e].rearrange("p b s -> p (b s)"), bank[4 + u][:],
                                                b2_t[:, e, None], None, ALU.add).then_inc(s_oc, 1)


def combine(core, pre, combine_t, expert_out, half_inv):
    nc, x, ident, bank = core.nc, core.x, core.ident, core.bank
    ST = SLOTS // P
    with ExitStack() as ctx:
        def sb(name, shape, dt=F32):
            return core.sb(f"{pre}_{name}", shape, dt, ctx)

        def sem(name):
            return core.sem(f"{pre}c_{name}")

        out_seq = sb("out_seq", [P, 2, E_SLOT, S_SLOT])
        out_rows = sb("out_rows", [P, 2, ST, D])
        mixed_t = sb("mixed_t", [P, 2, T])
        s_seq, s_t, s_tc = sem("seq_picked"), sem("outs_turned"), sem("outs_copied")
        s_mix, s_mixc, s_back, s_x = sem("mixed"), sem("mixed_copied"), sem("turned_back"), sem("x_added")

        with nc.Block() as block:
            @block.gpsimd
            def _(pool):
                with pool.Fori(0, B // 2) as i:
                    for u in range(2):
                        b = 2 * i + u
                        pool.wait_ge(s_t, 1 + 2 * i)
                        nc.gpsimd.tensor_copy(out_seq[:, u], expert_out[:, :, b]).then_inc(s_seq, 1)

            @block.tensor
            def _(pe):
                start_at_one(pe, s_t, s_mix, s_back)
                with pe.Fori(0, B // 2) as i:
                    for u in range(2):
                        b = 2 * i + u
                        pe.wait_ge(s_seq, b + 1)
                        pe.wait_ge(s_tc, 1 + 2 * i)
                        flat = out_seq[:, u].rearrange("p e s -> p (e s)")
                        for k in range(ST):
                            ins = pe.transpose(bank[u][:, P * k:P * k + P], flat[:, P * k:P * k + P], ident[:])
                        ins.then_inc(s_t, 1)
                    for u in range(2):
                        b = 2 * i + u
                        pe.wait_ge(s_tc, 1 + b + 1)
                        pe.wait_ge(s_mixc, 1 + 2 * i)
                        for k in range(ST):
                            ins = pe.matmul(bank[2 + u][:], out_rows[:, u, k], combine_t[:, b, k],
                                            start=k == 0, stop=k == ST - 1)
                        ins.then_inc(s_mix, 1)
                    for u in range(2):
                        b = 2 * i + u
                        pe.wait_ge(s_mixc, 1 + b + 1)
                        pe.wait_ge(s_x, 1 + TT * 2 * i)
                        for t in range(TT):
                            ins = pe.transpose(bank[4 + u][:, P * t:P * t + P], mixed_t[:, u, P * t:P * t + P],
                                               ident[:])
                        ins.then_inc(s_back, 1)

            @block.scalar
            def _(act):
                start_at_one(act, s_tc, s_mixc)
                with act.Fori(0, B // 2) as i:
                    for u in range(2):
                        b = 2 * i + u
                        act.wait_ge(s_t, 1 + b + 1)
                        act.wait_ge(s_mix, 1 + 2 * i)
                        nc.scalar.copy(out_rows[:, u].rearrange("p k d -> p (k d)"), bank[u][:]).then_inc(s_tc, 1)
                    for u in range(2):
                        b = 2 * i + u
                        act.wait_ge(s_mix, 1 + b + 1)
                        act.wait_ge(s_back, 1 + 2 * i)
                        nc.scalar.copy(mixed_t[:, u], bank[2 + u][:]).then_inc(s_mixc, 1)

            @block.vector
            def _(dve):
                start_at_one(dve, s_x)
                with dve.Fori(0, B // 2) as i:
                    for u in range(2):
                        b = 2 * i + u
                        dve.wait_ge(s_back, 1 + b + 1)
                        for t in range(TT):
                            k = TT * b + t
                            nc.vector.scalar_tensor_tensor(out=x[:, k], in0=bank[4 + u][:, P * t:P * t + P],
                                                           scalar=half_inv[:, k, None], in1=x[:, k],
                                                           op0=ALU.mult, op1=ALU.add).then_inc(s_x, 1)


def top_moe(core, pre, w):
    nc, x, ident, bank = core.nc, core.x, core.ident, core.bank
    with ExitStack() as ctx:
        def sb(name, shape, dt=F32):
            return core.sb(f"{pre}_{name}", shape, dt, ctx)

        xt_hi = sb("xt_hi", [P, B, T], F32R)
        xt_lo = sb("xt_lo", [P, B, T], F32R)
        biases = sb("biases", [P, E_MOE, HB + 1])
        mix = sb("mix", [P, TOPK * B])
        choice = sb("choice", [1, B * 8], U32)
        route(core, pre, w, xt_hi, xt_lo, biases, mix, choice)
        core.end_phase()
        chosen_experts(core, pre, w, xt_hi, xt_lo, biases, mix, choice)
        core.end_phase()


def route(core, pre, w, xt_hi, xt_lo, biases, mix, choice):
    nc, x, ident, bank = core.nc, core.x, core.ident, core.bank
    U = 4
    with ExitStack() as ctx:
        def sb(name, shape, dt=F32):
            return core.sb(f"{pre}_{name}", shape, dt, ctx)

        def sem(name):
            return core.sem(f"{pre}r_{name}")

        st = stats_buffers(core, ctx, pre + "_st")
        xn = sb("xn", [P, U, TT, D])
        xt_full = sb("xt_full", [P, U, T])
        sums = sb("sums", [P, B])
        gate = sb("gate", [P, E_MOE])
        b1_rows = sb("b1_rows", [E_MOE * HB, P])
        b2_rows = sb("b2_rows", [E_MOE, P])
        ones = sb("ones", [P, P])
        logit = sb("logit", [B, E_MOE])
        neg = sb("neg", [B, 1])
        prob = sb("prob", [B, E_MOE])
        total = sb("total", [B, 1])
        inv = sb("inv", [B, 1])
        best = sb("best", [B, 8])
        index = sb("index", [B, 8], U32)
        pair_sum = sb("pair_sum", [B, 1])
        diag = sb("diag", [B, TOPK, B])

        s_in = sem("inputs_in")
        s_stat, s_chain, s_var, s_root = sem("stats"), sem("chain"), sem("var"), sem("root")
        s_xn, s_t, s_ones = sem("xn_ready"), sem("turned"), sem("ones")
        s_sum, s_hi, s_lo = sem("summed"), sem("xt_hi"), sem("xt_lo")
        s_lg, s_neg, s_exp = sem("logits"), sem("neg_max"), sem("exp")
        s_bt, s_ix, s_dg, s_mix, s_ch = sem("biases_turned"), sem("index"), sem("diag"), sem("mix"), sem("choice_in")

        with nc.Block() as block:
            @block.sync
            def _(sp):
                sp.dma_start(gate[:], w["gate_w"]).then_inc(s_in, 16)
                sp.dma_start(b1_rows[:], w["b1"].rearrange("e (k p) -> (e k) p", p=P)).then_inc(s_in, 16)
                sp.dma_start(b2_rows[:], w["b2"]).then_inc(s_in, 16)
                sp.wait_ge(s_ix, 1)
                sp.dma_start(choice[0:1, :].rearrange("o (b k) -> o b k", b=B), index[:]).then_inc(s_ch, 16)
                sp.wait_ge(s_ch, 16)

            @block.vector
            def _(dve):
                start_at_one(dve, s_lo)
                nc.vector.memset(ones[:], 1.0).then_inc(s_ones, 1)
                link = layer_norm_stats_on_vector(nc, dve, x, st, s_stat, s_chain, s_var, s_root)
                with dve.Fori(0, B // U) as i:
                    for u in range(U):
                        b = U * i + u
                        dve.wait_ge(s_t, 1 + U * i)
                        for t in range(TT):
                            k = TT * b + t
                            ins = nc.vector.tensor_scalar(xn[:, u, t], x[:, k], st["mean"][:, k, None],
                                                          st["rstd"][:, k, None], ALU.subtract, ALU.mult)
                        ins.then_inc(s_xn, 1)
                    for u in range(U):
                        b = U * i + u
                        dve.wait_ge(s_sum, b + 1)
                        dve.wait_ge(s_hi, b + 1)
                        nc.vector.tensor_tensor(xt_lo[:, b], bank[u][:], xt_hi[:, b].bitcast(F32),
                                                ALU.subtract).then_inc(s_lo, 1)
                dve.wait_ge(s_lg, 1)
                link(nc.vector.tensor_scalar(logit[:], bank[5][0:B, 0:E_MOE], 1.0 / T, None, ALU.mult))
                nc.vector.tensor_reduce(neg[:], logit[:], AX, ALU.max, negate=True).then_inc(s_neg, 1)
                dve.wait_ge(s_bt, 1)
                link(nc.vector.tensor_copy(biases[:, :, 0:HB],
                                           bank[4][:, 0:E_MOE * HB].rearrange("p (e k) -> p e k", k=HB)))
                link(nc.vector.tensor_copy(biases[:, :, HB], bank[4][:, E_MOE * HB:E_MOE * (HB + 1)]))
                dve.wait_ge(s_exp, 1)
                link(nc.vector.reciprocal(inv[:], total[:]))
                link(nc.vector.tensor_scalar(prob[:], prob[:], inv[:, 0:1], None, ALU.mult))
                link(nc.vector.max(best[:], prob[:]))
                nc.vector.max_index(index[:], best[:], prob[:]).then_inc(s_ix, 1)
                link(nc.vector.tensor_tensor(pair_sum[:], best[:, 0:1], best[:, 1:2], ALU.add))
                link(nc.vector.reciprocal(pair_sum[:], pair_sum[:]))
                dve.wait_ge(s_ix, 1)
                link(nc.vector.tensor_scalar(best[:], best[:], pair_sum[:, 0:1], 0.5, ALU.mult, ALU.mult))
                for k in range(TOPK):
                    link(nc.vector.tensor_scalar(diag[:, k], ident[0:B, 0:B], best[:, k:k + 1], None, ALU.mult))
                dve.sem_inc(s_dg, 1)
                dve.wait_ge(s_mix, 1)
                link(nc.vector.tensor_copy(mix[:], bank[6][:, 0:TOPK * B]))

            @block.scalar
            def _(act):
                act.wait_ge(s_var, 1)
                nc.scalar.activation(st["root"][:], st["ve"][:], ACT.Sqrt).then_inc(s_root, 1)
                with act.Fori(0, B // U) as i:
                    for u in range(U):
                        b = U * i + u
                        act.wait_ge(s_t, 1 + b + 1)
                        nc.scalar.activation(xt_full[:, u], bank[u][:], ACT.Copy,
                                             accum_out=sums[:, b, None]).then_inc(s_sum, 1)
                        nc.scalar.copy(xt_hi[:, b], bank[u][:]).then_inc(s_hi, 1)
                act.wait_ge(s_neg, 1)
                nc.scalar.activation(prob[:], logit[:], ACT.Exp, bias=neg[:, 0:1], scale=1.0,
                                     accum_out=total[:, 0:1]).then_inc(s_exp, 1)

            @block.tensor
            def _(pe):
                start_at_one(pe, s_t)
                with pe.Fori(0, B // U) as i:
                    for u in range(U):
                        b = U * i + u
                        pe.wait_ge(s_xn, b + 1)
                        pe.wait_ge(s_lo, 1 + U * i)
                        for t in range(TT):
                            ins = pe.transpose(bank[u][:, P * t:P * t + P], xn[:, u, t], ident[:])
                        ins.then_inc(s_t, 1)
                pe.wait_ge(s_sum, B)
                pe.wait_ge(s_in, 48)
                pe.matmul(bank[5][0:B, 0:E_MOE], sums[:], gate[:], start=True, stop=True).then_inc(s_lg, 1)
                pe.transpose(bank[4][:, 0:E_MOE * HB], b1_rows[:], ident[0:E_MOE * HB, 0:E_MOE * HB])
                pe.transpose(bank[4][:, E_MOE * HB:E_MOE * (HB + 1)], b2_rows[:],
                             ident[0:E_MOE, 0:E_MOE]).then_inc(s_bt, 1)
                pe.wait_ge(s_ones, 1)
                pe.wait_ge(s_dg, 1)
                pe.matmul(bank[6][:, 0:TOPK * B], ones[0:B, :], diag[:].rearrange("p k b -> p (k b)"),
                          start=True, stop=True).then_inc(s_mix, 1)


def chosen_experts(core, pre, w, xt_hi, xt_lo, biases, mix, choice):
    nc, x, ident, bank = core.nc, core.x, core.ident, core.bank
    hidden, out_t, back = bank[0:4], bank[4:6], bank[6:8]
    with ExitStack() as ctx:
        def sb(name, shape, dt=F32):
            return core.sb(f"{pre}_{name}", shape, dt, ctx)

        def sem(name):
            return core.sem(f"{pre}x_{name}")

        w1 = sb("w1", [P, 2, TOPK, HID])
        w2 = sb("w2", [P, 2, TOPK, HB, D])
        bias = sb("bias", [P, 2, TOPK, HB + 1])
        w1_hi, w1_lo = sb("w1_hi", [P, TOPK, HID], F32R), sb("w1_lo", [P, TOPK, HID], F32R)
        w2_hi, w2_lo = sb("w2_hi", [P, TOPK, HB * D], F32R), sb("w2_lo", [P, TOPK, HB * D], F32R)
        b2_mix = sb("b2_mix", [P, 2, 2])
        hid = sb("hid", [P, TOPK, HB, T])
        hid_hi = sb("hid_hi", [P, TOPK, HB, T], F32R)
        hid_lo = sb("hid_lo", [P, TOPK, HB, T], F32R)
        y_t = sb("y_t", [P, 2, T])
        s_w = [[sem(f"seq{s}_expert{k}_in") for k in range(TOPK)] for s in range(2)]
        s_bias = [sem("biases0_in"), sem("biases1_in")]
        s_w1h, s_w1l, s_w2h, s_w2l = sem("w1_hi"), sem("w1_lo"), sem("w2_hi"), sem("w2_lo")
        s_seen = sem("w1_seen")
        s_b2p, s_b2 = sem("b2_part"), sem("b2_mixed")
        s_h, s_g, s_hh, s_hl = sem("hidden"), sem("gelu"), sem("hid_hi"), sem("hid_lo")
        s_y, s_yc, s_bk, s_x = sem("out_summed"), sem("out_copied"), sem("turned_back"), sem("x_added")

        def loaded(b, s):
            return 16 * (b - s) + 32

        def steps(first, step, last, loop):
            first()
            with loop(0, B // 2 - 1) as i:
                step(2 * i + 1, 1)
                step(2 * i + 2, 0)
            step(B - 1, 1)
            last()

        with nc.Block() as block:
            @block.sync
            def _(sp):
                def experts_of(b):
                    return [sp.value_load(choice[0:1, bass.ds(8 * b + k, 1)], min_val=0, max_val=E_MOE - 1)
                            for k in range(TOPK)]

                def load_weights(experts, s):
                    for k, e in enumerate(experts):
                        sp.dma_start(w1[:, s, k], w["w1"][e]).then_inc(s_w[s][k], 16)
                        sp.dma_start(w2[:, s, k], w["w2"][e].rearrange("(k p) d -> p k d", p=P)).then_inc(s_w[s][k], 16)

                def load_biases(experts, s):
                    for k, e in enumerate(experts):
                        sp.dma_start(bias[:, s, k], biases[:, e]).then_inc(s_bias[s], 16)

                for b in range(2):
                    experts = experts_of(b)
                    load_weights(experts, b)
                    load_biases(experts, b)
                with sp.Fori(1, B // 2) as i:
                    for s in range(2):
                        b = 2 * i + s
                        experts = experts_of(b)
                        sp.wait_ge(s_w1l, TOPK * (b - 1))
                        sp.wait_ge(s_w2l, TOPK * (b - 1))
                        load_weights(experts, s)
                        sp.wait_ge(s_yc, b)
                        load_biases(experts, s)

            @block.gpsimd
            def _(pool):
                def split_w1(b, s, k):
                    j = TOPK * b + k
                    pool.wait_ge(s_w[s][k], loaded(b, s))
                    if not isinstance(b, int) or b > 0:
                        pool.wait_ge(s_h, HB * (j - 1))
                    pool.sem_inc(s_seen, 1)
                    nc.gpsimd.tensor_copy(w1_hi[:, k], w1[:, s, k]).then_inc(s_w1h, 1)
                    pool.wait_ge(s_w1h, j + 1)
                    nc.gpsimd.tensor_tensor(w1_lo[:, k], w1[:, s, k], w1_hi[:, k].bitcast(F32),
                                            ALU.subtract).then_inc(s_w1l, 1)

                def step(b, s):
                    split_w1(b, s, 0)
                    split_w1(b, s, 1)

                steps(lambda: step(0, 0), step, lambda: None, pool.Fori)

            @block.tensor
            def _(pe):
                def first_layer(b, k):
                    j = TOPK * b + k
                    pe.wait_ge(s_w1l, j + 1)
                    for c in range(HB):
                        if not (isinstance(j, int) and j == 0):
                            pe.wait_ge(s_g, HB * (j - 1) + c + 1)
                        cols = slice(P * c, P * c + P)
                        pe.matmul(hidden[c][:], w1_hi[:, k, cols], xt_hi[:, b], start=True, stop=False)
                        pe.matmul(hidden[c][:], w1_hi[:, k, cols], xt_lo[:, b], start=False, stop=False)
                        pe.matmul(hidden[c][:], w1_lo[:, k, cols], xt_hi[:, b], start=False,
                                  stop=True).then_inc(s_h, 1)

                def second_layer(b, s, k):
                    j = TOPK * b + k
                    pe.wait_ge(s_w2l, j + 1)
                    if k == 0 and not (isinstance(b, int) and b == 0):
                        pe.wait_ge(s_yc, b)
                    for c in range(HB):
                        pe.wait_ge(s_hh, HB * j + c + 1)
                        cols = slice(P * c, P * c + P)
                        pe.matmul(out_t[s][:], w2_hi[:, k, cols], hid_hi[:, k, c], start=k == 0 and c == 0,
                                  stop=False)
                        pe.matmul(out_t[s][:], w2_lo[:, k, cols], hid_hi[:, k, c], start=False, stop=False)
                        pe.wait_ge(s_hl, HB * j + c + 1)
                        ins = pe.matmul(out_t[s][:], w2_hi[:, k, cols], hid_lo[:, k, c], start=False,
                                        stop=k == 1 and c == HB - 1)
                    ins.then_inc(s_y, 1)

                def turn_back(b, s):
                    pe.wait_ge(s_yc, 1 + b + 1)
                    pe.wait_ge(s_x, b + 1)
                    for t in range(TT):
                        ins = pe.transpose(back[s][:, P * t:P * t + P], y_t[:, s, P * t:P * t + P], ident[:])
                    ins.then_inc(s_bk, 1)

                def first():
                    first_layer(0, 0)
                    first_layer(0, 1)
                    second_layer(0, 0, 0)

                def step(b, s):
                    first_layer(b, 0)
                    second_layer(b - 1, 1 - s, 1)
                    first_layer(b, 1)
                    turn_back(b - 1, 1 - s)
                    second_layer(b, s, 0)

                def last():
                    second_layer(B - 1, 1, 1)
                    turn_back(B - 1, 1)

                pe.sem_inc(s_bk, 2)
                steps(first, step, last, pe.Fori)

            @block.scalar
            def _(act):
                def gelus(b, s, k):
                    j = TOPK * b + k
                    if not isinstance(b, int) or b > 0:
                        act.wait_ge(s_y, j - 1)
                    if k == 0:
                        act.wait_ge(s_bias[s], loaded(b, s))
                    for c in range(HB + 1):
                        if c < HB:
                            act.wait_ge(s_h, HB * j + c + 1)
                            nc.scalar.activation(hid[:, k, c], hidden[c][:], ACT.Gelu, bias=bias[:, s, k, c:c + 1],
                                                 scale=1.0).then_inc(s_g, 1)
                        if c > 0:
                            act.wait_ge(s_g, HB * j + c)
                            nc.scalar.copy(hid_hi[:, k, c - 1], hid[:, k, c - 1]).then_inc(s_hh, 1)

                def copy_out(b, s):
                    act.wait_ge(s_y, TOPK * (b + 1))
                    act.wait_ge(s_b2, b + 1)
                    act.wait_ge(s_bk, b + 1)
                    nc.scalar.activation(y_t[:, s], out_t[s][:], ACT.Identity, bias=b2_mix[:, s, 1:2],
                                         scale=1.0).then_inc(s_yc, 1)

                def first():
                    gelus(0, 0, 0)
                    gelus(0, 0, 1)

                def step(b, s):
                    gelus(b, s, 0)
                    copy_out(b - 1, 1 - s)
                    gelus(b, s, 1)

                start_at_one(act, s_yc)
                steps(first, step, lambda: copy_out(B - 1, 1), act.Fori)

            @block.vector
            def _(dve):
                def weight_of(b, k):
                    return mix[:, bass.ds(B * k + b, 1)]

                def split_w2(b, s, k):
                    j = TOPK * b + k
                    flat = w2[:, s, k].rearrange("p c d -> p (c d)")
                    dve.wait_ge(s_w[s][k], loaded(b, s))
                    if not isinstance(b, int) or b > 0:
                        dve.wait_ge(s_y, j - 1)
                    nc.vector.tensor_scalar(w2_hi[:, k], flat, weight_of(b, k), None, ALU.mult).then_inc(s_w2h, 1)
                    dve.wait_ge(s_w2h, j + 1)
                    nc.vector.scalar_tensor_tensor(out=w2_lo[:, k], in0=flat, scalar=weight_of(b, k),
                                                   in1=w2_hi[:, k].bitcast(F32), op0=ALU.mult,
                                                   op1=ALU.subtract).then_inc(s_w2l, 1)

                def mix_b2(b, s):
                    dve.wait_ge(s_bias[s], loaded(b, s))
                    if not isinstance(b, int) or b > 0:
                        dve.wait_ge(s_yc, b)
                    nc.vector.tensor_scalar(b2_mix[:, s, 0:1], bias[:, s, 0, HB:HB + 1], weight_of(b, 0), None,
                                            ALU.mult).then_inc(s_b2p, 1)
                    dve.wait_ge(s_b2p, b + 1)
                    nc.vector.scalar_tensor_tensor(out=b2_mix[:, s, 1:2], in0=bias[:, s, 1, HB:HB + 1],
                                                   scalar=weight_of(b, 1), in1=b2_mix[:, s, 0:1], op0=ALU.mult,
                                                   op1=ALU.add).then_inc(s_b2, 1)

                def remainders(b, k):
                    for c in range(HB):
                        dve.wait_ge(s_hh, HB * (TOPK * b + k) + c + 1)
                        nc.vector.tensor_tensor(hid_lo[:, k, c], hid[:, k, c], hid_hi[:, k, c].bitcast(F32),
                                                ALU.subtract).then_inc(s_hl, 1)

                def add_out(b, s):
                    dve.wait_ge(s_bk, 2 + b + 1)
                    rows = x[:, bass.ts(b, TT)].rearrange("p t d -> p (t d)")
                    nc.vector.tensor_tensor(rows, rows, back[s][:], ALU.add).then_inc(s_x, 1)

                def first():
                    split_w2(0, 0, 0)
                    remainders(0, 0)
                    split_w2(0, 0, 1)
                    mix_b2(0, 0)
                    remainders(0, 1)

                def step(b, s):
                    split_w2(b, s, 0)
                    remainders(b, 0)
                    split_w2(b, s, 1)
                    mix_b2(b, s)
                    remainders(b, 1)
                    add_out(b - 1, 1 - s)

                dve.sem_inc(s_x, 2)
                steps(first, step, lambda: add_out(B - 1, 1), dve.Fori)


def build(nc, a, out):
    with ExitStack() as ctx:
        core = Core(nc, ctx)
        s_in, s_out = core.sem("x_in"), core.sem("x_out")
        as_tiles = "b (i p) d -> p (b i) d"

        with nc.Block() as block:
            @block.sync
            def _(sp):
                sp.dma_start(core.x[:], a["L0_attn_x"].rearrange(as_tiles, p=P)).then_inc(s_in, 16)
                sp.dma_start(core.ident[:], a["identity"]).then_inc(s_in, 16)
                sp.wait_ge(s_in, 32)

        soft = {k: a["L0_ffn_" + k] for k in
                ("norm_gamma", "slot_norm_gamma", "slot_embeds", "w1", "b1", "w2", "b2")}
        top = {k: a["L1_ffn_" + k] for k in ("gate_w", "w1", "b1", "w2", "b2")}
        soft_moe(core, "s1", soft)
        attention(core, "a1", {"qkv": a["L0_attn_w_qkv"], "out": a["L0_attn_w_out"], "b_out": a["L0_attn_b_out"],
                               "rel": a["distance"], "slopes": a["slopes"]}, True)
        soft_moe(core, "s2", soft)
        top_moe(core, "t1", top)
        attention(core, "a2", {"q": a["L1_attn_w_q"], "kv_up": a["L1_attn_w_kv_up"],
                               "kv_down": a["L1_attn_w_kv_down"], "out": a["L1_attn_w_out"],
                               "rel": a["causal"]}, False)
        top_moe(core, "t2", top)

        with nc.Block() as block:
            @block.sync
            def _(sp):
                sp.dma_start(out.rearrange(as_tiles, p=P), core.x[:]).then_inc(s_out, 16)
                sp.wait_ge(s_out, 16)


def constants():
    gap = np.arange(T)[None, :] - (T - P) - np.arange(P)[:, None]
    return {
        "distance": np.where(gap <= 0, gap, MASKED).astype(np.float32),
        "causal": np.where(gap <= 0, 0.0, MASKED).astype(np.float32),
        "slopes": np.tile(alibi_slopes(), (P, 1)),
        "identity": np.eye(P, dtype=np.float32),
    }


def kernel(**inputs):
    import concourse.bacc as bacc
    from concourse.bass_utils import run_bass_kernel_spmd

    nc = bacc.Bacc("TRN2", target_bir_lowering=False, num_devices=1)
    arrays, args = {}, {}
    for name, value in {**inputs, **constants()}.items():
        value = np.ascontiguousarray(value)
        arrays[f"in_{name}"] = value
        args[name] = nc.dram_tensor(f"in_{name}", value.shape, mybir.dt.from_np(value.dtype),
                                    kind="ExternalInput").ap()
    out = nc.dram_tensor("out", (B, T, D), F32, kind="ExternalOutput").ap()
    build(nc, args, out)
    result = run_bass_kernel_spmd(nc, [arrays], core_ids=[0])
    return result.results[0]["out"]
```

```python
from contextlib import ExitStack

import numpy as np

import concourse.bass as bass
from concourse import mybir

P = 128
B, T, D = 8, 512, 128
TT = T // P
NT = B * TT
H, DH = 16, 64
PAIRS = B * H // 2
TURN = 2
E_SLOT, S_SLOT = 8, 64
SLOTS = E_SLOT * S_SLOT
E_MOE, TOPK = 8, 2
HID = 512
HB = HID // P
EPS = 1e-5
MASKED = -3.0e38

ALU = mybir.AluOpType
ACT = mybir.ActivationFunctionType
F32 = mybir.dt.float32
F32R = mybir.dt.float32r
U32 = mybir.dt.uint32
AX = mybir.AxisListType.X

PROB_AT = {3: 0, 2: 512, 0: 896, 1: 1024}
PROBT_AT = {0: 0, 1: 512, 3: 896, 2: 1024}
CAUSAL = TT * (TT + 1) // 2 * P


def alibi_slopes():
    start = 2.0 ** (-8.0 / H)
    return np.array([start ** (i + 1) for i in range(H)], np.float32)


class Core:

    def __init__(self, nc, ctx):
        self.nc, self.ctx, self.in_use = nc, ctx, []
        self.x = self.sb("x_tokens", [P, NT, D])
        self.ident = self.sb("ident", [P, P])
        self.tile_stats = self.sb("tile_stats", [P, NT, 6])
        self.stats_fresh = False
        self.early = self.sb("early", [P, 2, 2, HID])
        self.bank = [ctx.enter_context(nc.psum_tensor(f"bank{i}", [P, 512], F32)) for i in range(8)]

    def sb(self, name, shape, dt=F32, ctx=None):
        return (ctx or self.ctx).enter_context(self.nc.sbuf_tensor(name, shape, dt))

    def sem(self, name):
        self.in_use.append(self.nc.alloc_semaphore(name=name))
        return self.in_use[-1]

    def end_phase(self):
        self.nc.clear_and_free_semaphores(self.in_use)
        self.nc.all_engine_barrier()
        self.in_use = []


def start_at_one(engine, *semaphores):
    for s in semaphores:
        engine.sem_inc(s, 1)


def layer_norm_stats_on_vector(core, dve, st, s_stat, s_chain, s_var, s_root):
    nc, bn = core.nc, core.tile_stats
    if not core.stats_fresh:
        for k in range(NT):
            nc.vector.bn_stats(bn[:, k], core.x[:, k]).then_inc(s_stat, 1)
        dve.wait_ge(s_stat, NT)
    core.stats_fresh = False
    links = [0]

    def link(ins):
        links[0] += 1
        ins.then_inc(s_chain, 1)
        dve.wait_ge(s_chain, links[0])

    even, odd = bn[:, :, 1], bn[:, :, 4]
    link(nc.vector.tensor_tensor(st["mean"][:], even, odd, ALU.add))
    link(nc.vector.tensor_scalar(st["mean"][:], st["mean"][:], 0.5, None, ALU.mult))
    link(nc.vector.tensor_tensor(st["a"][:], even, odd, ALU.subtract))
    link(nc.vector.tensor_tensor(st["a"][:], st["a"][:], st["a"][:], ALU.mult))
    link(nc.vector.tensor_tensor(st["var"][:], bn[:, :, 2], bn[:, :, 5], ALU.add))
    link(nc.vector.tensor_scalar(st["var"][:], st["var"][:], 1.0 / D, None, ALU.mult))
    link(nc.vector.scalar_tensor_tensor(out=st["var"][:], in0=st["a"][:], scalar=0.25, in1=st["var"][:],
                                        op0=ALU.mult, op1=ALU.add))
    nc.vector.tensor_scalar(st["ve"][:], st["var"][:], EPS, None, ALU.add).then_inc(s_var, 1)
    dve.wait_ge(s_root, 1)
    link(nc.vector.reciprocal(st["rstd"][:], st["root"][:]))
    link(nc.vector.tensor_tensor(st["a"][:], st["rstd"][:], st["rstd"][:], ALU.mult))
    link(nc.vector.tensor_tensor(st["a"][:], st["a"][:], st["ve"][:], ALU.mult))
    link(nc.vector.tensor_scalar(st["a"][:], st["a"][:], -0.5, 1.5, ALU.mult, ALU.add))
    link(nc.vector.tensor_tensor(st["rstd"][:], st["rstd"][:], st["a"][:], ALU.mult))
    return link


def stats_buffers(core, ctx, pre):
    st = {k: core.sb(f"{pre}_{k}", [P, NT], ctx=ctx) for k in ("mean", "var", "ve", "a", "rstd", "root")}
    return st


def attention(core, pre, w, alibi):
    with ExitStack() as ctx:
        def sb(name, shape, dt=F32):
            return core.sb(f"{pre}_{name}", shape, dt, ctx)

        xt_full = sb("xt_full", [P, B, T])
        xt_hi = sb("xt_hi", [P, B, T], F32R)
        xt_lo = sb("xt_lo", [P, B, T], F32R)
        qk_split = sb("qk_split", [P, 2, 2, H * DH], F32R)
        wv = sb("wv", [P, H * DH])
        wo2 = sb("wo2", [P, H, D])
        rel = sb("rel", [P, T])
        slopes = sb("slopes", [P, H])
        qk_pair = sb("qk_pair", [P, 2, 2, P], F32R)

        prepare(core, pre, w, alibi, xt_full, xt_hi, xt_lo, qk_split, qk_pair, wv, wo2, rel, slopes)
        core.end_phase()
        attend(core, pre, alibi, xt_full, xt_hi, xt_lo, qk_split, qk_pair, wv, wo2, rel, slopes)
        core.end_phase()


def prepare(core, pre, w, alibi, xt_full, xt_hi, xt_lo, qk_split, qk_pair, wv, wo2, rel, slopes):
    nc, x, ident, bank = core.nc, core.x, core.ident, core.bank
    with ExitStack() as ctx:
        def sb(name, shape, dt=F32):
            return core.sb(f"{pre}_{name}", shape, dt, ctx)

        def sem(name):
            return core.sem(f"{pre}p_{name}")

        st = stats_buffers(core, ctx, pre + "_st")
        xn = sb("xn", [P, 4, TT, D])
        wq, wk = (core.early[:, i].rearrange("p a c -> p (a c)") for i in range(2))
        if not alibi:
            wkv_v = sb("wkv_v", [P, H * DH])
            wkd = sb("wkd", [P, P])
            wkd_t = sb("wkd_t", [P, P])
        else:
            bout = sb("bout", [P, D])

        s_w = sem("weights_in")
        s_stat, s_chain, s_var, s_root = sem("stats"), sem("chain"), sem("var"), sem("root")
        s_xn = sem("xn_ready")
        s_turned = sem("turned")
        s_xf, s_xh, s_xl = sem("xt_full"), sem("xt_hi"), sem("xt_lo")
        s_bias = sem("bias_added")
        s_kw, s_wh, s_wl = sem("w_k_ready"), sem("weights_hi"), sem("weights_lo")
        s_kd_in, s_first = sem("kv_down_in"), sem("first_heads_in")
        s_kd, s_kdt, s_vm, s_vc = sem("kd_turned"), sem("kd_copied"), sem("v_ready"), sem("v_copied")

        wk_parts = ((wk, slice(0, H * DH)),) if alibi else tuple(
            (bank[c][:], slice(512 * c, 512 * c + 512)) for c in range(2))
        n_splits = 1 + len(wk_parts)
        n_w = [0]
        with nc.Block() as block:
            @block.sync
            def _(sp):
                def load(dst, src):
                    n_w[0] += 1
                    sp.dma_start(dst, src).then_inc(s_w, 16)

                if alibi:
                    load(bout[:], w["b_out"].rearrange("(o d) -> o d", o=1).broadcast_to([P, D]))
                    load(slopes[:], w["slopes"])
                    load(wv[:], w["qkv"][:, 2 * H * DH:3 * H * DH])
                else:
                    sp.dma_start(wkd[:], w["kv_down"]).then_inc(s_kd_in, 16)
                    load(wkv_v[:], w["kv_up"][:, H * DH:2 * H * DH])
                for half in range(2):
                    load(wo2[64 * half:64 * half + 64], w["out"].rearrange("(h d) c -> d h c", d=DH))
                load(rel[:], w["rel"])
                sp.wait_ge(s_wl, n_splits)
                sp.dma_start(qk_pair[:].bitcast(F32), qk_split[:, :, :, 0:P].bitcast(F32)).then_inc(s_first, 16)
                sp.wait_ge(s_first, 16)
                sp.wait_ge(s_w, 16 * n_w[0])

            n_loads = 6 if alibi else 4

            @block.gpsimd
            def _(pool):
                if alibi:
                    pool.wait_ge(s_w, 16 * n_loads)
                    with pool.Fori(0, B) as b:
                        pool.wait_ge(s_xn, b + 1)
                        tiles = x[:, bass.ts(b, TT)]
                        nc.gpsimd.tensor_tensor(tiles, tiles, bout[:, None, :].broadcast_to([P, TT, D]),
                                                ALU.add).then_inc(s_bias, 1)

            @block.vector
            def _(dve):
                layer_norm_stats_on_vector(core, dve, st, s_stat, s_chain, s_var, s_root)

                def normed(b):
                    if b >= 4:
                        dve.wait_ge(s_turned, b - 3)
                    for k in range(TT * b, TT * (b + 1)):
                        ins = nc.vector.tensor_scalar(xn[:, b % 4, k % TT], x[:, k], st["mean"][:, k:k + 1],
                                                      st["rstd"][:, k:k + 1], ALU.subtract, ALU.mult)
                    ins.then_inc(s_xn, 1)

                normed(0)
                normed(1)
                dve.wait_ge(s_wh, 1)
                nc.vector.scalar_tensor_tensor(out=qk_split[:, 0, 1], in0=wq, scalar=DH ** -0.5,
                                               in1=qk_split[:, 0, 0].bitcast(F32), op0=ALU.mult,
                                               op1=ALU.subtract).then_inc(s_wl, 1)
                for i, (part, cols) in enumerate(wk_parts):
                    dve.wait_ge(s_wh, i + 2)
                    nc.vector.tensor_tensor(qk_split[:, 1, 1, cols], part, qk_split[:, 1, 0, cols].bitcast(F32),
                                            ALU.subtract).then_inc(s_wl, 1)
                for b in range(B):
                    if b + 2 < B:
                        normed(b + 2)
                    dve.wait_ge(s_xf, b + 1)
                    dve.wait_ge(s_xh, b + 1)
                    nc.vector.tensor_tensor(xt_lo[:, b], bank[4 + b % 3][:], xt_hi[:, b].bitcast(F32),
                                            ALU.subtract).then_inc(s_xl, 1)

            @block.scalar
            def _(act):
                if not alibi:
                    act.wait_ge(s_kd, 1)
                    nc.scalar.copy(wkd_t[:], bank[7][:, 0:P]).then_inc(s_kdt, 1)
                nc.scalar.mul(qk_split[:, 0, 0], wq, DH ** -0.5).then_inc(s_wh, 1)
                for i, (part, cols) in enumerate(wk_parts):
                    if not alibi:
                        act.wait_ge(s_kw, i + 1)
                    nc.scalar.copy(qk_split[:, 1, 0, cols], part).then_inc(s_wh, 1)
                act.wait_ge(s_var, 1)
                nc.scalar.activation(st["root"][:], st["ve"][:], ACT.Sqrt).then_inc(s_root, 1)
                for b in range(B):
                    act.wait_ge(s_turned, b + 1)
                    nc.scalar.copy(xt_hi[:, b], bank[4 + b % 3][:]).then_inc(s_xh, 1)
                    nc.scalar.copy(xt_full[:, b], bank[4 + b % 3][:]).then_inc(s_xf, 1)
                if not alibi:
                    for c in range(2):
                        act.wait_ge(s_vm, c + 1)
                        nc.scalar.copy(wv[:, 512 * c:512 * c + 512], bank[7][:]).then_inc(s_vc, 1)

            @block.tensor
            def _(pe):
                def turn_tokens(b):
                    pe.wait_ge(s_xn, b + 1)
                    if b >= 3:
                        pe.wait_ge(s_xl, b - 2)
                    for t in range(TT):
                        ins = pe.transpose(bank[4 + b % 3][:, P * t:P * t + P], xn[:, b % 4, t], ident[:])
                    ins.then_inc(s_turned, 1)

                if not alibi:
                    pe.wait_ge(s_kd_in, 16)
                    pe.transpose(bank[7][:, 0:P], wkd[:], ident[:]).then_inc(s_kd, 1)
                    pe.wait_ge(s_kdt, 1)
                    for c in range(2):
                        pe.matmul(bank[c][:], wkd_t[:], wk[:, 512 * c:512 * c + 512], start=True,
                                  stop=True).then_inc(s_kw, 1)
                for b in range(B):
                    turn_tokens(b)
                if not alibi:
                    pe.wait_ge(s_w, 16 * n_loads)
                    for c in range(2):
                        if c > 0:
                            pe.wait_ge(s_vc, c)
                        pe.matmul(bank[7][:], wkd_t[:], wkv_v[:, 512 * c:512 * c + 512], start=True,
                                  stop=True).then_inc(s_vm, 1)


def attend(core, pre, alibi, xt_full, xt_hi, xt_lo, qk_split, qk_pair, wv, wo2, rel, slopes):
    nc, x, ident, bank = core.nc, core.x, core.ident, core.bank
    proj, s3, s20, s1, turn0, turn1, av, outp = bank
    score_at = {3: s3[:, 0:512], 2: s20[:, 0:384], 0: s20[:, 384:512], 1: s1[:, 0:256]}
    ORDER = (3, 2, 0, 1)
    groups = ((turn0, (0,), 0, 512), (turn1, (1, 3), 512, 512), (turn0, (2,), 1024, 256))
    with ExitStack() as ctx:
        def sb(name, shape, dt=F32):
            return core.sb(f"{pre}_{name}", shape, dt, ctx)

        def sem(name):
            return core.sem(f"{pre}a_{name}")

        xt_seq = sb("xt_seq", [P, T])
        bias = sb("bias", [P, 2, T]) if alibi else None
        split = sb("split", [P, 2, 2, 2, T], F32R)
        q_head = sb("q_head", [P, 2, T], F32R)
        k_head = sb("k_head", [P, 2, 2, T], F32R)
        v2 = sb("v2", [P, TT, 2, 2, DH], F32R)
        prob = sb("prob", [P, 2, CAUSAL])
        neg_max = sb("neg_max", [P, 2, TT])
        total = sb("total", [P, 2, TT])
        inv = sb("inv", [P, 2, TT])
        pt_hi = sb("pt_hi", [P, 2, CAUSAL], F32R)
        pt_lo = sb("pt_lo", [P, 2, CAUSAL], F32R)
        av_t = sb("av_t", [P, T])

        s_wqk = [sem("wq_in"), sem("wk_in")]
        s_seen = sem("projections_seen")
        s_head = [sem("head0_in"), sem("head1_in")]
        s_xt = sem("xt_in")
        s_bias = sem("bias_made")
        s_p, s_ph, s_pl = sem("projected"), sem("projection_hi"), sem("projection_lo")
        s_v, s_vh, s_vl = sem("v_ready"), sem("v_hi"), sem("v_lo")
        s_s, s_st, s_exp = sem("scores_ready"), sem("scores_shifted"), sem("probs_ready")
        s_t, s_th, s_tl = sem("probs_turned"), sem("pt_hi"), sem("pt_lo")
        s_av, s_avc, s_out, s_x = sem("av_ready"), sem("av_copied"), sem("out_ready"), sem("x_added")
        s_inv, s_go, s_stat = sem("inv_ready"), sem("scores_seen"), sem("stats")

        def slots(slot, loop):
            slot(0, 0, "PS")
            slot(0, 1, "PSTV")
            slot(1, 0, "PSTA")
            slot(1, 1, "PSTAOV")
            with loop(0, (PAIRS - 4) // TURN) as i:
                for k in range(TURN):
                    slot(TURN * i + 2 + k, 0, "PSTAO")
                    slot(TURN * i + 2 + k, 1, "PSTAOV")
            slot(PAIRS - 2, 0, "PSTAO")
            slot(PAIRS - 2, 1, "STAOV")
            slot(PAIRS - 1, 0, "STAO")
            slot(PAIRS - 1, 1, "STAOV")
            slot(PAIRS, 0, "TAO")
            slot(PAIRS, 1, "AO")
            slot(PAIRS + 1, 0, "O")

        def before(n, u):
            return (n - 1, 1) if u == 0 else (n, 0)

        def seq(n):
            return n // (H // 2)

        def head(n, u):
            return (n % (H // 2)) * 2 + u

        with nc.Block() as block:
            @block.sync
            def _(sp):
                def weights_of(m, k):
                    sp.wait_ge(s_p, 2 * m - k)
                    sp.dma_start(qk_pair[:, k].bitcast(F32),
                                 qk_split[:, k, :, bass.ts(m % (H // 2), P)].bitcast(F32)).then_inc(s_wqk[k], 16)

                def head_of(m, u, first=False):
                    sp.wait_ge(s_pl, 2 * m + 2)
                    sp.sem_inc(s_seen, 1)
                    if not first:
                        sp.wait_ge(s_s, TT * (2 * m + u - 1))
                    rows = slice(DH * u, DH * u + DH)
                    q, k = split[rows, m % 2, 0].bitcast(F32), split[rows, m % 2, 1].bitcast(F32)
                    for half in range(2):
                        to = slice(DH * half, DH * half + DH)
                        sp.dma_start(q_head[to, u].bitcast(F32), q[:, half]).then_inc(s_head[u], 16)
                        sp.dma_start(k_head[to, u].bitcast(F32), k).then_inc(s_head[u], 16)

                def values_of(n, first=False):
                    if not first:
                        sp.wait_ge(s_v, n)
                    sp.dma_start(xt_seq[:], xt_full[:, seq(n)]).then_inc(s_xt, 16)

                def pair(n, wk=True, wq=True):
                    if not isinstance(n, int) or n > 0:
                        head_of(n, 1)
                        values_of(n)
                    if wq:
                        weights_of(n + 2, 0)
                    if not isinstance(n, int) or n < PAIRS - 1:
                        head_of(n + 1, 0)
                    if wk:
                        weights_of(n + 3, 1)

                weights_of(1, 1)
                head_of(0, 0, True)
                head_of(0, 1, True)
                weights_of(1, 0)
                weights_of(2, 1)
                values_of(0, True)
                pair(0)
                pair(1)
                with sp.Fori(2, PAIRS - 3) as n:
                    pair(n)
                pair(PAIRS - 3, wk=False)
                pair(PAIRS - 2, wk=False, wq=False)
                pair(PAIRS - 1, wk=False, wq=False)

            @block.gpsimd
            def _(pool):
                if not alibi:
                    return

                def bias_of(n, u, first=False):
                    if not first:
                        pool.wait_ge(s_st, TT * (2 * n + u - 1))
                    nc.gpsimd.tensor_tensor(bias[:, u], rel[:], slopes[:, head(n, u), None].broadcast_to([P, T]),
                                            ALU.mult).then_inc(s_bias, 1)

                bias_of(0, 0, True)
                bias_of(0, 1, True)
                with pool.Fori(1, PAIRS) as n:
                    bias_of(n, 0)
                    bias_of(n, 1)

            @block.tensor
            def _(pe):
                def project(m, k):
                    if not isinstance(m, int) or m > 0:
                        pe.wait_ge(s_wqk[k], 16 * m)
                    xh, xl = xt_hi[:, seq(m)], xt_lo[:, seq(m)]
                    pe.matmul(proj[:], qk_pair[:, k, 0], xh, start=True, stop=False)
                    pe.matmul(proj[:], qk_pair[:, k, 0], xl, start=False, stop=False)
                    pe.matmul(proj[:], qk_pair[:, k, 1], xh, start=False, stop=True).then_inc(s_p, 1)

                def values(n, full):
                    if full:
                        pe.wait_ge(s_x, 1 + TT * (2 * n - 1))
                    pe.wait_ge(s_xt, 16 * (n + 1))
                    for j in range(TT):
                        ins = pe.matmul(outp[:, P * j:P * j + P], xt_seq[:, P * j:P * j + P],
                                        wv[:, bass.ts(n % (H // 2), P)], start=True, stop=True)
                    ins.then_inc(s_v, 1)

                def scores(n, u, k, first=False):
                    g, i = 2 * n + u, ORDER[k]
                    if k == 0:
                        pe.wait_ge(s_head[u], 64 * (n + 1))
                    if not first and k in (0, 1, 3):
                        pe.wait_ge(s_st, TT * (g - 1) + (1, 3, 0, 4)[k])
                    keys = slice(0, P * (i + 1))
                    rows = slice(P * i, P * i + P)
                    at = score_at[i]
                    pe.matmul(at, q_head[:, u, rows], k_head[:, u, 0, keys], start=True, stop=False)
                    pe.matmul(at, q_head[:, u, rows], k_head[:, u, 1, keys], start=False,
                              stop=True).then_inc(s_s, 1)

                def turn(n, u, c):
                    g = 2 * n + u
                    to, tiles, at, _ = groups[c]
                    if c == 0:
                        pe.wait_ge(s_exp, TT * (g + 1))
                    if c == 2:
                        pe.wait_ge(s_tl, 3 * g + 1)
                    elif not (isinstance(g, int) and g == 0):
                        pe.wait_ge(s_tl, 3 * g - c)
                    for j in tiles:
                        for i in range(j, TT):
                            col = PROBT_AT[j] - at + P * (i - j)
                            src = PROB_AT[i] + P * j
                            ins = pe.transpose(to[:, col:col + P], prob[:, u, src:src + P], ident[:])
                    ins.then_inc(s_t, 1)

                def sum_values(n, u):
                    g = 2 * n + u
                    if not (isinstance(g, int) and g == 0):
                        pe.wait_ge(s_avc, g)
                    if u == 0:
                        pe.wait_ge(s_vl, n + 1)
                    for c, (_, tiles, _, _) in enumerate(groups):
                        pe.wait_ge(s_tl, 3 * g + c + 1)
                        for j in tiles:
                            at = PROBT_AT[j]
                            cols = slice(at, at + T - P * j)
                            lhs = v2[:, j, u].rearrange("p a d -> p (a d)")
                            pe.matmul(av[:, P * j:T], lhs, pt_hi[:, u, cols], start=j == 0, stop=False)
                            ins = pe.matmul(av[:, P * j:T], lhs, pt_lo[:, u, cols], start=False, stop=j == 2)
                    ins.then_inc(s_av, 1)

                def output(n, u):
                    g = 2 * n + u
                    pe.wait_ge(s_avc, g + 1)
                    if not (isinstance(g, int) and g == 0):
                        pe.wait_ge(s_x, 1 + TT * g)
                    if u == 1 and not (isinstance(n, int) and n == PAIRS - 1):
                        pe.wait_ge(s_vl, n + 2)
                    for i in range(TT):
                        ins = pe.matmul(outp[:, P * i:P * i + P], av_t[:, P * i:P * i + P], wo2[:, head(n, u)],
                                        start=True, stop=True)
                    ins.then_inc(s_out, 1)

                def slot(n, u, work):
                    if "S" in work:
                        for k in range(TT):
                            scores(n, u, k, isinstance(n, int) and n == 0 and u == 0)
                    if "O" in work:
                        output(*before(n - 1, u))
                    if "T" in work:
                        turn(*before(n, u), 0)
                        turn(*before(n, u), 1)
                    if "P" in work:
                        pe.wait_ge(s_pl, 2 * n + u + 3)
                        project(n + 1 + u, u)
                    if "A" in work:
                        sum_values(n - 1, u)
                    if "T" in work:
                        turn(*before(n, u), 2)
                    if "V" in work:
                        values(n, "O" in work)

                project(0, 1)
                pe.wait_ge(s_pl, 1)
                project(0, 0)
                pe.wait_ge(s_pl, 2)
                project(1, 1)
                slots(slot, pe.Fori)

            @block.scalar
            def _(act):
                def projection_high(m, k):
                    act.wait_ge(s_p, 2 * m + 2 - k)
                    if not isinstance(m, int) or m > 1:
                        for u in range(2):
                            act.wait_ge(s_head[u], 64 * (m - 1))
                    nc.scalar.copy(split[:, m % 2, k, 0], proj[:]).then_inc(s_ph, 1)

                def v_high(n):
                    act.wait_ge(s_v, n + 1)
                    nc.scalar.copy(v2[:, :, :, 0], outp[:].rearrange("p (j u d) -> p j u d", j=TT, u=2))\
                        .then_inc(s_vh, 1)

                def probs(n, u, k):
                    g = 2 * n + u
                    i = ORDER[k]
                    at = PROB_AT[i]
                    tile = prob[:, u, at:at + P * (i + 1)]
                    act.wait_ge(s_st, TT * g + k + 1)
                    nc.scalar.activation(tile, tile, ACT.Exp, bias=neg_max[:, u, i:i + 1], scale=-1.0,
                                         accum_out=total[:, u, i:i + 1]).then_inc(s_exp, 1)

                def pt_high(n, u, c):
                    to, _, at, size = groups[c]
                    act.wait_ge(s_t, 3 * (2 * n + u) + c + 1)
                    nc.scalar.copy(pt_hi[:, u, at:at + size], to[:, 0:size]).then_inc(s_th, 1)

                def av_copy(n, u):
                    act.wait_ge(s_av, 2 * n + u + 1)
                    nc.scalar.copy(av_t[:], av[:]).then_inc(s_avc, 1)

                def slot(n, u, work):
                    if "S" in work:
                        probs(n, u, 0)
                        probs(n, u, 1)
                    if "T" in work:
                        pt_high(*before(n, u), 0)
                        pt_high(*before(n, u), 1)
                    if "S" in work:
                        probs(n, u, 2)
                    if "P" in work:
                        projection_high(n + 1 + u, u)
                    if "A" in work:
                        av_copy(n - 1, u)
                    if "T" in work:
                        pt_high(*before(n, u), 2)
                    if "V" in work:
                        v_high(n)
                    if "S" in work:
                        probs(n, u, 3)

                projection_high(0, 1)
                projection_high(0, 0)
                projection_high(1, 1)
                slots(slot, act.Fori)

            @block.vector
            def _(dve):
                start_at_one(dve, s_x)
                def projection_low(m, k):
                    dve.wait_ge(s_ph, 2 * m + 2 - k)
                    nc.vector.tensor_tensor(split[:, m % 2, k, 1], proj[:], split[:, m % 2, k, 0].bitcast(F32),
                                            ALU.subtract).then_inc(s_pl, 1)

                def v_low(n):
                    dve.wait_ge(s_vh, n + 1)
                    nc.vector.tensor_tensor(v2[:, :, :, 1], outp[:].rearrange("p (j u d) -> p j u d", j=TT, u=2),
                                            v2[:, :, :, 0].bitcast(F32), ALU.subtract).then_inc(s_vl, 1)

                def shift(n, u, k, first=False):
                    g = 2 * n + u
                    if k == 0:
                        if not first:
                            dve.wait_ge(s_t, 3 * (g - 1))
                        if alibi:
                            dve.wait_ge(s_bias, g + 1)
                    for i in (ORDER[k],):
                        dve.wait_ge(s_s, TT * g + (1, 3, 3, 4)[k])
                        dve.sem_inc(s_go, 1)
                        at = PROB_AT[i]
                        size = P * (i + 1)
                        table = bias[:, u] if alibi else rel
                        nc.vector.tensor_tensor_reduce(
                            out=prob[:, u, at:at + size], in0=score_at[i], in1=table[:, T - size:T],
                            scale=-1.0, scalar=-MASKED, op0=ALU.add, op1=ALU.min,
                            accum_out=neg_max[:, u, i:i + 1]).then_inc(s_st, 1)

                def pt_low(n, u, c):
                    to, _, at, size = groups[c]
                    dve.wait_ge(s_th, 3 * (2 * n + u) + c + 1)
                    nc.vector.tensor_tensor(pt_lo[:, u, at:at + size], to[:, 0:size], pt_hi[:, u, at:at + size].bitcast(F32),
                                            ALU.subtract).then_inc(s_tl, 1)

                def invert(n, u, first=False):
                    g = 2 * n + u
                    dve.wait_ge(s_exp, TT * (g + 1))
                    if not first:
                        dve.wait_ge(s_x, 1 + TT * (g - 1))
                    nc.vector.reciprocal(inv[:, u], total[:, u]).then_inc(s_inv, 1)

                def add_output(n, u):
                    g = 2 * n + u
                    dve.wait_ge(s_out, g + 1)
                    dve.wait_ge(s_inv, g + 1)
                    dve.wait_ge(s_x, 1 + TT * g)
                    for i in range(TT):
                        tile = x[:, seq(n) * TT + i]
                        nc.vector.scalar_tensor_tensor(out=tile, in0=outp[:, P * i:P * i + P], scalar=inv[:, u, i:i + 1],
                                                       in1=tile, op0=ALU.mult, op1=ALU.add).then_inc(s_x, 1)

                def slot(n, u, work):
                    if "S" in work:
                        for k in range(TT):
                            shift(n, u, k, isinstance(n, int) and n == 0)
                    if "O" in work:
                        add_output(*before(n - 1, u))
                    if "T" in work:
                        pt_low(*before(n, u), 0)
                        pt_low(*before(n, u), 1)
                    if "P" in work:
                        projection_low(n + 1 + u, u)
                    if "T" in work:
                        invert(*before(n, u), "O" not in work)
                        pt_low(*before(n, u), 2)
                    if "V" in work:
                        v_low(n)
                    if isinstance(n, int) and n == PAIRS:
                        for k in range(u * TT * 4, min(u * TT * 4 + 16, NT - TT)):
                            nc.vector.bn_stats(core.tile_stats[:, k], x[:, k]).then_inc(s_stat, 1)

                projection_low(0, 1)
                projection_low(0, 0)
                projection_low(1, 1)
                slots(slot, dve.Fori)
                dve.wait_ge(s_x, 1 + TT * 2 * PAIRS)
                for k in range(NT - TT, NT):
                    nc.vector.bn_stats(core.tile_stats[:, k], x[:, k]).then_inc(s_stat, 1)
    core.stats_fresh = True


def refine_root(nc, link, y, v, a):
    link(nc.vector.tensor_tensor(a, y, y, ALU.mult))
    link(nc.vector.tensor_tensor(a, a, v, ALU.mult))
    link(nc.vector.tensor_scalar(a, a, -0.5, 1.5, ALU.mult, ALU.add))
    link(nc.vector.tensor_tensor(y, y, a, ALU.mult))


def soft_moe(core, pre, w, next_qk=()):
    with ExitStack() as ctx:
        def sb(name, shape, dt=F32):
            return core.sb(f"{pre}_{name}", shape, dt, ctx)

        combine_t = sb("combine_t", [P, B, TT, T])
        slots_hi = sb("slots_hi", [P, E_SLOT, B, S_SLOT], F32R)
        slots_lo = sb("slots_lo", [P, E_SLOT, B, S_SLOT], F32R)
        half_inv = sb("half_inv", [P, NT])
        b1_t = sb("b1_t", [P, E_SLOT * HB])
        b2_t = sb("b2_t", [P, E_SLOT])
        dispatch(core, pre, w, combine_t, slots_hi, slots_lo, half_inv, b1_t, b2_t)
        core.end_phase()
        expert_out = sb("expert_out", [P, B, E_SLOT, S_SLOT])
        slot_experts(core, pre, w, slots_hi, slots_lo, expert_out, b1_t, b2_t)
        core.end_phase()
        combine(core, pre, combine_t, expert_out, half_inv, next_qk)
        core.end_phase()


def load_expert(sp, core, w, e, u, done):
    sp.dma_start(core.early[:, u, 0], w["w1"][e]).then_inc(done, 16)
    sp.dma_start(core.early[:, u, 1].rearrange("p (k d) -> p k d", d=D),
                 w["w2"][e].rearrange("(k p) d -> p k d", p=P)).then_inc(done, 16)


def load_qk(sp, core, w, done):
    for i, cols in enumerate(w):
        sp.dma_start(core.early[:, i].rearrange("p a c -> p (a c)"), cols).then_inc(done, 16)


def dispatch(core, pre, w, combine_t, slots_hi, slots_lo, half_inv, b1_t, b2_t):
    nc, x, ident, bank = core.nc, core.x, core.ident, core.bank
    ST = SLOTS // P
    turned, ring, turn_ring, sums = bank[0], bank[1:5], bank[5:7], bank[7]
    with ExitStack() as ctx:
        def sb(name, shape, dt=F32):
            return core.sb(f"{pre}_{name}", shape, dt, ctx)

        def sem(name):
            return core.sem(f"{pre}d_{name}")

        st = stats_buffers(core, ctx, pre + "_st")
        emb = sb("emb", [P, ST, D])
        square = sb("square", [P, D])
        norm2 = sb("norm2", [P, NT + ST])
        norm = sb("norm", [P, NT + ST])
        scale = sb("scale", [P, NT + ST])
        scratch = sb("scratch", [P, NT + ST])
        gammas = sb("gammas", [P, 2])
        gamma2 = sb("gamma2", [P, 1])
        emb_hi = sb("emb_hi", [P, SLOTS], F32R)
        emb_lo = sb("emb_lo", [P, SLOTS], F32R)
        b1_rows = sb("b1_rows", [E_SLOT * HB, P])
        b2_rows = sb("b2_rows", [E_SLOT, D])
        z = sb("z", [P, 2, TT, D])
        z_kept = sb("z_kept", [P, 2, TT, D])
        zt_hi = sb("zt_hi", [P, 2, T], F32R)
        zt_lo = sb("zt_lo", [P, 2, T], F32R)
        neg_max = sb("neg_max", [P, 2, 2 * TT])
        total = sb("total", [P, 2, 2 * TT])
        inv = sb("inv", [P, 2, 2 * TT])
        prob = sb("prob", [P, 2, 2 * TT, T])
        disp = sb("disp", [P, TT, SLOTS])
        slot_rows = sb("slot_rows", [P, ST, D])

        s_in, s_early = sem("inputs_in"), sem("experts_in")
        s_stat, s_chain, s_var, s_root = sem("stats"), sem("chain"), sem("var"), sem("root")
        s_norm2, s_norm = sem("norm2"), sem("norm")
        s_emb, s_embm, s_embh, s_embt = sem("embeds_normed"), sem("embeds_turned"), sem("emb_hi"), sem("emb_lo")
        s_z, s_kept, s_zm, s_zh, s_zl = sem("z_ready"), sem("z_kept"), sem("z_turned"), sem("zt_hi"), sem("zt_lo")
        s_l, s_max, s_exp = sem("logits"), sem("max"), sem("probs")
        s_inv, s_half = sem("inv_ready"), sem("half_inv")
        s_t, s_dc, s_cc = sem("probs_turned"), sem("dispatch_copied"), sem("combine_copied")
        s_sl, s_rows, s_slt = sem("slots_summed"), sem("slot_rows"), sem("slots_turned")
        s_slh, s_slc = sem("slots_hi"), sem("slots_lo")
        s_bt, s_btc, s_seen = sem("biases_turned"), sem("biases_copied"), sem("z_seen")

        def steps(step, loop):
            step(0, 0, "NZL")
            step(1, 1, "NZLT")
            with loop(1, B // 2 - 1) as i:
                step(2 * i, 0, "NZLTS")
                step(2 * i + 1, 1, "NZLTS")
            step(B - 2, 0, "ZLTS")
            step(B - 1, 1, "LTS")
            step(B, 0, "TS")
            step(B + 1, 1, "S")

        with nc.Block() as block:
            @block.sync
            def _(sp):
                sp.dma_start(emb[:], w["slot_embeds"].rearrange("e s d -> (e s) d")
                             .rearrange("(k p) d -> p k d", p=P)).then_inc(s_in, 16)
                sp.dma_start(gammas[:, 0:1], w["norm_gamma"].rearrange("(d o) -> d o", o=1)).then_inc(s_in, 16)
                sp.dma_start(gammas[:, 1:2], w["slot_norm_gamma"].rearrange("(d o) -> d o", o=1)).then_inc(s_in, 16)
                sp.dma_start(b1_rows[:], w["b1"].rearrange("e (k p) -> (e k) p", p=P)).then_inc(s_in, 16)
                sp.dma_start(b2_rows[:], w["b2"]).then_inc(s_in, 16)
                for e in range(2):
                    load_expert(sp, core, w, e, e, s_early)
                sp.wait_ge(s_early, 16 * 4)

            @block.gpsimd
            def _(pool):
                def keep(b, s):
                    pool.wait_ge(s_z, b + 1)
                    if not isinstance(b, int) or b > 1:
                        pool.wait_ge(s_sl, b - 1)
                    pool.sem_inc(s_seen, 1)
                    nc.gpsimd.tensor_copy(z_kept[:, s], z[:, s]).then_inc(s_kept, 1)

                keep(0, 0)
                keep(1, 1)
                with pool.Fori(1, B // 2) as i:
                    keep(2 * i, 0)
                    keep(2 * i + 1, 1)

            @block.vector
            def _(dve):
                start_at_one(dve, s_slc)
                link = layer_norm_stats_on_vector(core, dve, st, s_stat, s_chain, s_var, s_root)
                n2 = norm2[:, 0:NT]
                link(nc.vector.tensor_tensor(n2, st["rstd"][:], st["rstd"][:], ALU.mult))
                link(nc.vector.tensor_tensor(n2, n2, st["var"][:], ALU.mult))
                link(nc.vector.tensor_scalar(n2, n2, float(D), None, ALU.mult))
                dve.wait_ge(s_in, 16 * 5)
                for k in range(ST):
                    link(nc.vector.tensor_tensor_reduce(out=square[:], in0=emb[:, k], in1=emb[:, k], scale=1.0,
                                                        scalar=0.0, op0=ALU.mult, op1=ALU.add,
                                                        accum_out=norm2[:, NT + k:NT + k + 1]))
                nc.vector.tensor_scalar(norm2[:], norm2[:], 1e-24, None, ALU.max).then_inc(s_norm2, 1)
                dve.wait_ge(s_norm2, 1)
                dve.wait_ge(s_norm, 1)
                link(nc.vector.reciprocal(scale[:], norm[:]))
                refine_root(nc, link, scale[:], norm2[:], scratch[:])
                link(nc.vector.tensor_scalar(scale[:], scale[:], float(D) ** 0.5, None, ALU.mult))
                link(nc.vector.tensor_tensor(scale[:, 0:NT], scale[:, 0:NT], st["rstd"][:], ALU.mult))
                for k in range(ST):
                    ins = nc.vector.tensor_scalar(emb[:, k], emb[:, k], scale[:, NT + k:NT + k + 1], None, ALU.mult)
                ins.then_inc(s_emb, 1)
                link(nc.vector.tensor_tensor(gamma2[:], gammas[:, 0:1], gammas[:, 1:2], ALU.mult))

                def normed(b, s):
                    if not isinstance(b, int) or b > 1:
                        dve.wait_ge(s_zm, b - 1)
                        dve.wait_ge(s_kept, b - 1)
                    for t in range(TT):
                        k = TT * b + t
                        ins = nc.vector.tensor_scalar(z[:, s, t], x[:, k], st["mean"][:, k, None], scale[:, k, None],
                                                      ALU.subtract, ALU.mult)
                    ins.then_inc(s_z, 1)

                def zt_low(b, s):
                    dve.wait_ge(s_zh, b + 1)
                    nc.vector.tensor_tensor(zt_lo[:, s], turned[:], zt_hi[:, s].bitcast(F32),
                                            ALU.subtract).then_inc(s_zl, 1)

                def maximum(b, s, k):
                    if k == 0 and (not isinstance(b, int) or b > 1):
                        dve.wait_ge(s_exp, 8 * (b - 1))
                    dve.wait_ge(s_l, 8 * b + k + 1)
                    nc.vector.tensor_reduce(neg_max[:, s, k:k + 1], ring[k % 4][:], AX, ALU.max,
                                            negate=True).then_inc(s_max, 1)

                def invert(b, s):
                    dve.wait_ge(s_exp, 8 * (b + 1))
                    nc.vector.reciprocal(inv[:, s], total[:, s]).then_inc(s_inv, 1)
                    dve.wait_ge(s_inv, b + 1)
                    nc.vector.tensor_scalar(half_inv[:, bass.ts(b, TT)], inv[:, s, TT:2 * TT], 0.5, None,
                                            ALU.mult).then_inc(s_half, 1)

                def combine_copy(b, r):
                    dve.wait_ge(s_t, 8 * b + r + 1)
                    nc.vector.tensor_copy(combine_t[:, b, r - TT], turn_ring[r % 2][:]).then_inc(s_cc, 1)

                def rows_of(b, s):
                    dve.wait_ge(s_sl, b + 1)
                    if not isinstance(b, int) or b > 0:
                        dve.wait_ge(s_slt, b)
                    for t in range(ST):
                        ins = nc.vector.tensor_scalar(slot_rows[:, t], sums[:, P * t:P * t + P], inv[:, s, t:t + 1],
                                                      None, ALU.mult)
                    ins.then_inc(s_rows, 1)

                def slots_of(b):
                    dve.wait_ge(s_slt, b + 1)
                    at = turned[:].rearrange("p (e s) -> p e s", e=E_SLOT)
                    nc.vector.tensor_scalar(slots_hi[:, :, b], at, gammas[:, 0:1], None, ALU.mult).then_inc(s_slh, 1)
                    dve.wait_ge(s_slh, b + 1)
                    nc.vector.scalar_tensor_tensor(out=slots_lo[:, :, b], in0=at, scalar=gammas[:, 0:1],
                                                   in1=slots_hi[:, :, b].bitcast(F32), op0=ALU.mult,
                                                   op1=ALU.subtract).then_inc(s_slc, 1)

                def step(b, s, work):
                    for k in range(2 * TT):
                        if "L" in work:
                            maximum(b, s, k)
                        if "S" in work and k == 0:
                            rows_of(b - 2, s)
                        if "Z" in work and k == 2:
                            zt_low(b + 1, 1 - s)
                        if "N" in work and k == 3:
                            normed(b + 2, s)
                        if "S" in work and k == 5:
                            slots_of(b - 2)
                        if "T" in work and k >= TT:
                            combine_copy(b - 1, k)
                    if "L" in work:
                        invert(b, s)

                normed(0, 0)
                dve.wait_ge(s_embm, 1)
                nc.vector.tensor_scalar(emb_hi[:], bank[1][:], gamma2[:, 0:1], None, ALU.mult).then_inc(s_embh, 1)
                dve.wait_ge(s_embh, 1)
                nc.vector.scalar_tensor_tensor(out=emb_lo[:], in0=bank[1][:], scalar=gamma2[:, 0:1],
                                               in1=emb_hi[:].bitcast(F32), op0=ALU.mult,
                                               op1=ALU.subtract).then_inc(s_embt, 1)
                zt_low(0, 0)
                normed(1, 1)
                dve.wait_ge(s_bt, 1)
                nc.vector.tensor_copy(b1_t[:], bank[7][:, 0:E_SLOT * HB]).then_inc(s_btc, 1)
                nc.vector.tensor_copy(b2_t[:], bank[7][:, P:P + E_SLOT]).then_inc(s_btc, 1)
                steps(step, dve.Fori)

            @block.scalar
            def _(act):
                act.wait_ge(s_var, 1)
                nc.scalar.activation(st["root"][:], st["ve"][:], ACT.Sqrt).then_inc(s_root, 1)
                act.wait_ge(s_norm2, 1)
                nc.scalar.activation(norm[:], norm2[:], ACT.Sqrt).then_inc(s_norm, 1)

                def zt_high(b, s):
                    act.wait_ge(s_zm, b + 1)
                    if not isinstance(b, int) or b > 1:
                        act.wait_ge(s_l, 8 * (b - 1))
                    nc.scalar.copy(zt_hi[:, s], turned[:]).then_inc(s_zh, 1)

                def exponentials(b, s, k):
                    if k == 0 and (not isinstance(b, int) or b > 1):
                        act.wait_ge(s_t, 8 * (b - 1))
                        act.wait_ge(s_inv, b - 1)
                    act.wait_ge(s_max, 8 * b + k + 1)
                    nc.scalar.activation(prob[:, s, k], ring[k % 4][:], ACT.Exp, bias=neg_max[:, s, k:k + 1],
                                         scale=1.0, accum_out=total[:, s, k:k + 1]).then_inc(s_exp, 1)

                def dispatch_copy(b, r):
                    if r == 0 and (not isinstance(b, int) or b > 0):
                        act.wait_ge(s_sl, b)
                    act.wait_ge(s_t, 8 * b + r + 1)
                    nc.scalar.copy(disp[:, r], turn_ring[r % 2][:]).then_inc(s_dc, 1)

                def step(b, s, work):
                    for k in range(2 * TT):
                        if "L" in work:
                            exponentials(b, s, k)
                        if "T" in work and k < TT:
                            dispatch_copy(b - 1, k)
                        if "Z" in work and k == 0:
                            zt_high(b + 1, 1 - s)

                zt_high(0, 0)
                steps(step, act.Fori)

            @block.tensor
            def _(pe):
                pe.wait_ge(s_in, 16 * 5)
                pe.transpose(sums[:, 0:E_SLOT * HB], b1_rows[:], ident[0:E_SLOT * HB, 0:E_SLOT * HB])
                pe.transpose(sums[:, P:P + E_SLOT], b2_rows[:], ident[0:E_SLOT, 0:E_SLOT]).then_inc(s_bt, 1)
                pe.wait_ge(s_emb, 1)
                for k in range(ST):
                    ins = pe.transpose(bank[1][:, P * k:P * k + P], emb[:, k], ident[:])
                ins.then_inc(s_embm, 1)

                def turn_tokens(b, s):
                    pe.wait_ge(s_z, b + 1)
                    if not isinstance(b, int) or b > 0:
                        pe.wait_ge(s_zl, b)
                    if not isinstance(b, int) or b > 2:
                        pe.wait_ge(s_slc, 1 + b - 3)
                    for t in range(TT):
                        ins = pe.transpose(turned[:, P * t:P * t + P], z[:, s, t], ident[:])
                    ins.then_inc(s_zm, 1)

                def logits(b, s, k):
                    if k == 0:
                        pe.wait_ge(s_zl, b + 1)
                    if not isinstance(b, int) or b > 0 or k >= 4:
                        pe.wait_ge(s_exp, 8 * b + k - 3)
                    to = ring[k % 4][:]
                    if k < TT:
                        cols = slice(P * k, P * k + P)
                        pe.matmul(to, emb_hi[:, cols], zt_hi[:, s], start=True, stop=False)
                        pe.matmul(to, emb_hi[:, cols], zt_lo[:, s], start=False, stop=False)
                        ins = pe.matmul(to, emb_lo[:, cols], zt_hi[:, s], start=False, stop=True)
                    else:
                        cols = slice(P * (k - TT), P * (k - TT) + P)
                        pe.matmul(to, zt_hi[:, s, cols], emb_hi[:], start=True, stop=False)
                        pe.matmul(to, zt_hi[:, s, cols], emb_lo[:], start=False, stop=False)
                        ins = pe.matmul(to, zt_lo[:, s, cols], emb_hi[:], start=False, stop=True)
                    ins.then_inc(s_l, 1)

                def turn_probs(b, s, r):
                    if r == 0:
                        pe.wait_ge(s_exp, 8 * b + TT)
                    if r == TT:
                        pe.wait_ge(s_exp, 8 * b + 2 * TT)
                    if r < 2:
                        if not isinstance(b, int) or b > 0:
                            pe.wait_ge(s_cc, TT * b + r - 1)
                    elif r < 6:
                        pe.wait_ge(s_dc, TT * b + r - 1)
                    else:
                        pe.wait_ge(s_cc, TT * b + r - 5)
                    rows = 0 if r < TT else TT
                    col = P * (r % TT)
                    for k in range(TT):
                        ins = pe.transpose(turn_ring[r % 2][:, P * k:P * k + P],
                                           prob[:, s, rows + k, col:col + P], ident[:])
                    ins.then_inc(s_t, 1)

                def slot_sums(b, s, k):
                    if k == 0:
                        pe.wait_ge(s_dc, TT * (b + 1))
                        pe.wait_ge(s_kept, b + 1)
                        if not isinstance(b, int) or b > 0:
                            pe.wait_ge(s_rows, b)
                    cols = slice(P * k, P * k + P)
                    for t in range(TT):
                        ins = pe.matmul(sums[:, cols], disp[:, t, cols], z_kept[:, s, t], start=t == 0,
                                        stop=t == TT - 1)
                    if k == ST - 1:
                        ins.then_inc(s_sl, 1)

                def turn_slots(b, after_tokens):
                    pe.wait_ge(s_rows, b + 1)
                    if after_tokens:
                        pe.wait_ge(s_zl, b + 4)
                    else:
                        pe.wait_ge(s_slc, 1 + b)
                    for k in range(ST):
                        ins = pe.transpose(turned[:, P * k:P * k + P], slot_rows[:, k], ident[:])
                    ins.then_inc(s_slt, 1)

                def step(b, s, work):
                    if "Z" in work:
                        turn_tokens(b + 1, 1 - s)
                    for k in range(2 * TT):
                        if "L" in work:
                            logits(b, s, k)
                        if "S" in work and k == TT:
                            turn_slots(b - 2, "Z" in work)
                        if "T" in work:
                            turn_probs(b - 1, 1 - s, k)
                        if "T" in work and k >= TT:
                            slot_sums(b - 1, 1 - s, k - TT)

                turn_tokens(0, 0)
                pe.wait_ge(s_embt, 1)
                pe.wait_ge(s_btc, 2)
                steps(step, pe.Fori)


def slot_experts(core, pre, w, slots_hi, slots_lo, expert_out, b1_t, b2_t):
    nc, bank = core.nc, core.bank
    hidden, out_t = bank[0:4], bank[4:6]
    N = B * S_SLOT
    with ExitStack() as ctx:
        def sb(name, shape, dt=F32):
            return core.sb(f"{pre}_{name}", shape, dt, ctx)

        def sem(name):
            return core.sem(f"{pre}e_{name}")

        w1, w2 = core.early[:, :, 0], core.early[:, :, 1]
        w1_hi, w1_lo = sb("w1_hi", [P, 2, HID], F32R), sb("w1_lo", [P, 2, HID], F32R)
        w2_hi, w2_lo = sb("w2_hi", [P, 2, HB * D], F32R), sb("w2_lo", [P, 2, HB * D], F32R)
        hid = sb("hid", [P, HB, N])
        hid_hi, hid_lo = sb("hid_hi", [P, 2, HB, N], F32R), sb("hid_lo", [P, 2, HB, N], F32R)
        s_w = [sem("expert0_in"), sem("expert1_in")]
        s_seen = sem("w1_seen")
        s_w1h, s_w1l, s_w2h, s_w2l = sem("w1_hi"), sem("w1_lo"), sem("w2_hi"), sem("w2_lo")
        s_h, s_g, s_hh, s_hl = sem("hidden"), sem("gelu"), sem("hid_hi"), sem("hid_lo")
        s_o, s_oc = sem("out_summed"), sem("out_copied")

        def steps(step, loop):
            step(0, 0, "F")
            step(1, 1, "FS")
            with loop(1, E_SLOT // 2) as i:
                step(2 * i, 0, "FS")
                step(2 * i + 1, 1, "FS")
            step(E_SLOT, 0, "S")

        with nc.Block() as block:
            @block.sync
            def _(sp):
                with sp.Fori(1, E_SLOT // 2) as i:
                    for u in range(2):
                        sp.wait_ge(s_w1l, 2 * i + u - 1)
                        sp.wait_ge(s_w2l, 2 * i + u - 1)
                        load_expert(sp, core, w, 2 * i + u, u, s_w[u])

            @block.gpsimd
            def _(pool):
                def step(e, u, work):
                    if "F" in work:
                        if not isinstance(e, int) or e > 1:
                            pool.wait_ge(s_w[u], 16 * (e - u))
                            pool.wait_ge(s_h, HB * (e - 1))
                        pool.sem_inc(s_seen, 1)
                        nc.gpsimd.tensor_copy(w1_hi[:, u], w1[:, u]).then_inc(s_w1h, 1)
                        pool.wait_ge(s_w1h, e + 1)
                        nc.gpsimd.tensor_tensor(w1_lo[:, u], w1[:, u], w1_hi[:, u].bitcast(F32),
                                                ALU.subtract).then_inc(s_w1l, 1)

                steps(step, pool.Fori)

            @block.tensor
            def _(pe):
                def first_layer(e, u):
                    pe.wait_ge(s_w1l, e + 1)
                    hi = slots_hi[:, e].rearrange("p b s -> p (b s)")
                    lo = slots_lo[:, e].rearrange("p b s -> p (b s)")
                    for c in range(HB):
                        if not isinstance(e, int) or e > 0:
                            pe.wait_ge(s_g, HB * (e - 1) + c + 1)
                        cols = slice(P * c, P * c + P)
                        pe.matmul(hidden[c][:], w1_hi[:, u, cols], hi, start=True, stop=False)
                        pe.matmul(hidden[c][:], w1_hi[:, u, cols], lo, start=False, stop=False)
                        pe.matmul(hidden[c][:], w1_lo[:, u, cols], hi, start=False, stop=True).then_inc(s_h, 1)

                def second_layer(e, u):
                    pe.wait_ge(s_w2l, e + 1)
                    if not isinstance(e, int) or e > 1:
                        pe.wait_ge(s_oc, e - 1)
                    for c in range(HB):
                        cols = slice(P * c, P * c + P)
                        pe.wait_ge(s_hh, HB * e + c + 1)
                        pe.matmul(out_t[u][:], w2_hi[:, u, cols], hid_hi[:, u, c], start=c == 0, stop=False)
                        pe.matmul(out_t[u][:], w2_lo[:, u, cols], hid_hi[:, u, c], start=False, stop=False)
                        pe.wait_ge(s_hl, HB * e + c + 1)
                        ins = pe.matmul(out_t[u][:], w2_hi[:, u, cols], hid_lo[:, u, c], start=False,
                                        stop=c == HB - 1)
                    ins.then_inc(s_o, 1)

                def step(e, u, work):
                    if "F" in work:
                        first_layer(e, u)
                    if "S" in work:
                        second_layer(e - 1, 1 - u)

                steps(step, pe.Fori)

            @block.scalar
            def _(act):
                def step(e, u, work):
                    if "F" not in work:
                        return
                    for c in range(HB + 1):
                        if c < HB:
                            act.wait_ge(s_h, HB * e + c + 1)
                            if not isinstance(e, int) or e > 0:
                                act.wait_ge(s_hl, HB * (e - 1) + c + 1)
                            nc.scalar.activation(hid[:, c], hidden[c][:], ACT.Gelu, bias=b1_t[:, HB * e + c, None],
                                                 scale=1.0).then_inc(s_g, 1)
                        if c == 1 and (not isinstance(e, int) or e > 1):
                            act.wait_ge(s_o, e - 1)
                        if c > 0:
                            act.wait_ge(s_g, HB * e + c)
                            nc.scalar.copy(hid_hi[:, u, c - 1], hid[:, c - 1]).then_inc(s_hh, 1)

                steps(step, act.Fori)

            @block.vector
            def _(dve):
                def split_w2(e, u):
                    flat = w2[:, u]
                    if not isinstance(e, int) or e > 1:
                        dve.wait_ge(s_w[u], 16 * (e - u))
                        dve.wait_ge(s_o, e - 1)
                    nc.vector.tensor_copy(w2_hi[:, u], flat).then_inc(s_w2h, 1)
                    dve.wait_ge(s_w2h, e + 1)
                    nc.vector.tensor_tensor(w2_lo[:, u], flat, w2_hi[:, u].bitcast(F32),
                                            ALU.subtract).then_inc(s_w2l, 1)

                def step(e, u, work):
                    if "F" in work:
                        split_w2(e, u)
                        for c in range(HB):
                            dve.wait_ge(s_hh, HB * e + c + 1)
                            nc.vector.tensor_tensor(hid_lo[:, u, c], hid[:, c], hid_hi[:, u, c].bitcast(F32),
                                                    ALU.subtract).then_inc(s_hl, 1)
                    if "S" in work:
                        dve.wait_ge(s_o, e)
                        nc.vector.tensor_scalar(expert_out[:, :, e - 1], out_t[1 - u][:].rearrange("p (b s) -> p b s", b=B),
                                                b2_t[:, e - 1, None], None, ALU.add).then_inc(s_oc, 1)

                steps(step, dve.Fori)


def combine(core, pre, combine_t, expert_out, half_inv, next_qk):
    nc, x, ident, bank = core.nc, core.x, core.ident, core.bank
    turned, out = bank[0:3], bank[3:6]
    ST = SLOTS // P
    with ExitStack() as ctx:
        def sb(name, shape, dt=F32):
            return core.sb(f"{pre}_{name}", shape, dt, ctx)

        def sem(name):
            return core.sem(f"{pre}c_{name}")

        out_rows = sb("out_rows", [P, 3, ST, D])
        s_t, s_tc, s_mix, s_x = sem("outs_turned"), sem("outs_copied"), sem("mixed"), sem("x_added")
        s_stat, s_qk = sem("stats"), sem("next_qk_in")

        with nc.Block() as block:
            @block.sync
            def _(sp):
                if next_qk:
                    load_qk(sp, core, next_qk, s_qk)
                    sp.wait_ge(s_qk, 32)

            @block.tensor
            def _(pe):
                def turn(b):
                    if b >= 3:
                        pe.wait_ge(s_tc, b - 2)
                    flat = expert_out[:, b].rearrange("p e s -> p (e s)")
                    for k in range(ST):
                        ins = pe.transpose(turned[b % 3][:, P * k:P * k + P], flat[:, P * k:P * k + P], ident[:])
                    ins.then_inc(s_t, 1)

                turn(0)
                turn(1)
                for b in range(B):
                    if b + 2 < B:
                        turn(b + 2)
                    pe.wait_ge(s_tc, b + 1)
                    if b >= 3:
                        pe.wait_ge(s_x, TT * (b - 2))
                    for t in range(TT):
                        cols = slice(P * t, P * t + P)
                        for k in range(ST):
                            ins = pe.matmul(out[b % 3][:, cols], combine_t[:, b, k, cols], out_rows[:, b % 3, k],
                                            start=k == 0, stop=k == ST - 1)
                    ins.then_inc(s_mix, 1)

            @block.scalar
            def _(act):
                for b in range(B):
                    act.wait_ge(s_t, b + 1)
                    if b >= 3:
                        act.wait_ge(s_mix, b - 2)
                    nc.scalar.copy(out_rows[:, b % 3].rearrange("p k d -> p (k d)"), turned[b % 3][:]).then_inc(s_tc, 1)

            @block.vector
            def _(dve):
                def stats(b):
                    dve.wait_ge(s_x, TT * (b + 1))
                    for k in range(TT * b, TT * (b + 1)):
                        nc.vector.bn_stats(core.tile_stats[:, k], x[:, k]).then_inc(s_stat, 1)

                for b in range(B):
                    dve.wait_ge(s_mix, b + 1)
                    for t in range(TT):
                        k = TT * b + t
                        nc.vector.scalar_tensor_tensor(out=x[:, k], in0=out[b % 3][:, P * t:P * t + P],
                                                       scalar=half_inv[:, k:k + 1], in1=x[:, k],
                                                       op0=ALU.mult, op1=ALU.add).then_inc(s_x, 1)
                    if b > 0:
                        stats(b - 1)
                stats(B - 1)
    core.stats_fresh = True


def top_moe(core, pre, w, next_qk=(), out=None):
    with ExitStack() as ctx:
        def sb(name, shape, dt=F32):
            return core.sb(f"{pre}_{name}", shape, dt, ctx)

        xt_hi = sb("xt_hi", [P, B, T], F32R)
        xt_lo = sb("xt_lo", [P, B, T], F32R)
        biases = sb("biases", [P, E_MOE, HB + 1])
        mix = sb("mix", [P, TOPK * B])
        choice = sb("choice", [1, B * 8], U32)
        route(core, pre, w, xt_hi, xt_lo, biases, mix, choice)
        core.end_phase()
        chosen_experts(core, pre, w, xt_hi, xt_lo, biases, mix, choice, next_qk, out)
        core.stats_fresh = out is None
        core.end_phase()


def route(core, pre, w, xt_hi, xt_lo, biases, mix, choice):
    nc, x, ident, bank = core.nc, core.x, core.ident, core.bank
    U = 4
    with ExitStack() as ctx:
        def sb(name, shape, dt=F32):
            return core.sb(f"{pre}_{name}", shape, dt, ctx)

        def sem(name):
            return core.sem(f"{pre}r_{name}")

        st = stats_buffers(core, ctx, pre + "_st")
        xn = sb("xn", [P, U, TT, D])
        xt_full = sb("xt_full", [P, U, T])
        sums = sb("sums", [P, B])
        gate = sb("gate", [P, E_MOE])
        b1_rows = sb("b1_rows", [E_MOE * HB, P])
        b2_rows = sb("b2_rows", [E_MOE, P])
        ones = sb("ones", [P, P])
        logit = sb("logit", [B, E_MOE])
        neg = sb("neg", [B, 1])
        prob = sb("prob", [B, E_MOE])
        total = sb("total", [B, 1])
        inv = sb("inv", [B, 1])
        best = sb("best", [B, 8])
        index = sb("index", [B, 8], U32)
        pair_sum = sb("pair_sum", [B, 1])
        diag = sb("diag", [B, TOPK, B])

        s_in = sem("inputs_in")
        s_stat, s_chain, s_var, s_root = sem("stats"), sem("chain"), sem("var"), sem("root")
        s_xn, s_t, s_ones = sem("xn_ready"), sem("turned"), sem("ones")
        s_sum, s_hi, s_lo = sem("summed"), sem("xt_hi"), sem("xt_lo")
        s_lg, s_neg, s_exp = sem("logits"), sem("neg_max"), sem("exp")
        s_bt, s_ix, s_dg, s_mix, s_ch = sem("biases_turned"), sem("index"), sem("diag"), sem("mix"), sem("choice_in")

        with nc.Block() as block:
            @block.sync
            def _(sp):
                sp.dma_start(gate[:], w["gate_w"]).then_inc(s_in, 16)
                sp.dma_start(b1_rows[:], w["b1"].rearrange("e (k p) -> (e k) p", p=P)).then_inc(s_in, 16)
                sp.dma_start(b2_rows[:], w["b2"]).then_inc(s_in, 16)
                sp.wait_ge(s_ix, 1)
                sp.dma_start(choice[0:1, :].rearrange("o (b k) -> o b k", b=B), index[:]).then_inc(s_ch, 16)
                sp.wait_ge(s_ch, 16)

            @block.vector
            def _(dve):
                nc.vector.memset(ones[:], 1.0).then_inc(s_ones, 1)
                link = layer_norm_stats_on_vector(core, dve, st, s_stat, s_chain, s_var, s_root)

                def normed(b):
                    if b >= U:
                        dve.wait_ge(s_t, b - U + 1)
                    for k in range(TT * b, TT * (b + 1)):
                        ins = nc.vector.tensor_scalar(xn[:, b % U, k % TT], x[:, k], st["mean"][:, k:k + 1],
                                                      st["rstd"][:, k:k + 1], ALU.subtract, ALU.mult)
                    ins.then_inc(s_xn, 1)

                normed(0)
                normed(1)
                for b in range(B):
                    if b + 2 < B:
                        normed(b + 2)
                    dve.wait_ge(s_sum, b + 1)
                    dve.wait_ge(s_hi, b + 1)
                    nc.vector.tensor_tensor(xt_lo[:, b], bank[b % U][:], xt_hi[:, b].bitcast(F32),
                                            ALU.subtract).then_inc(s_lo, 1)
                dve.wait_ge(s_lg, 1)
                link(nc.vector.tensor_scalar(logit[:], bank[5][0:B, 0:E_MOE], 1.0 / T, None, ALU.mult))
                nc.vector.tensor_reduce(neg[:], logit[:], AX, ALU.max, negate=True).then_inc(s_neg, 1)
                dve.wait_ge(s_bt, 1)
                link(nc.vector.tensor_copy(biases[:, :, 0:HB],
                                           bank[4][:, 0:E_MOE * HB].rearrange("p (e k) -> p e k", k=HB)))
                link(nc.vector.tensor_copy(biases[:, :, HB], bank[4][:, E_MOE * HB:E_MOE * (HB + 1)]))
                dve.wait_ge(s_exp, 1)
                link(nc.vector.reciprocal(inv[:], total[:]))
                link(nc.vector.tensor_scalar(prob[:], prob[:], inv[:, 0:1], None, ALU.mult))
                link(nc.vector.max(best[:], prob[:]))
                nc.vector.max_index(index[:], best[:], prob[:]).then_inc(s_ix, 1)
                link(nc.vector.tensor_tensor(pair_sum[:], best[:, 0:1], best[:, 1:2], ALU.add))
                link(nc.vector.reciprocal(pair_sum[:], pair_sum[:]))
                dve.wait_ge(s_ix, 1)
                link(nc.vector.tensor_scalar(best[:], best[:], pair_sum[:, 0:1], 0.5, ALU.mult, ALU.mult))
                for k in range(TOPK):
                    link(nc.vector.tensor_scalar(diag[:, k], ident[0:B, 0:B], best[:, k:k + 1], None, ALU.mult))
                dve.sem_inc(s_dg, 1)
                dve.wait_ge(s_mix, 1)
                link(nc.vector.tensor_copy(mix[:], bank[6][:, 0:TOPK * B]))

            @block.scalar
            def _(act):
                act.wait_ge(s_var, 1)
                nc.scalar.activation(st["root"][:], st["ve"][:], ACT.Sqrt).then_inc(s_root, 1)
                for b in range(B):
                    act.wait_ge(s_t, b + 1)
                    nc.scalar.copy(xt_hi[:, b], bank[b % U][:]).then_inc(s_hi, 1)
                    if b >= U:
                        act.wait_ge(s_sum, b - U + 1)
                    nc.scalar.activation(xt_full[:, b % U], bank[b % U][:], ACT.Copy,
                                         accum_out=sums[:, b:b + 1]).then_inc(s_sum, 1)
                act.wait_ge(s_neg, 1)
                nc.scalar.activation(prob[:], logit[:], ACT.Exp, bias=neg[:, 0:1], scale=1.0,
                                     accum_out=total[:, 0:1]).then_inc(s_exp, 1)

            @block.tensor
            def _(pe):
                for b in range(B):
                    pe.wait_ge(s_xn, b + 1)
                    if b >= U:
                        pe.wait_ge(s_lo, b - U + 1)
                    for t in range(TT):
                        ins = pe.transpose(bank[b % U][:, P * t:P * t + P], xn[:, b % U, t], ident[:])
                    ins.then_inc(s_t, 1)
                pe.wait_ge(s_sum, B)
                pe.wait_ge(s_in, 48)
                pe.matmul(bank[5][0:B, 0:E_MOE], sums[:], gate[:], start=True, stop=True).then_inc(s_lg, 1)
                pe.transpose(bank[4][:, 0:E_MOE * HB], b1_rows[:], ident[0:E_MOE * HB, 0:E_MOE * HB])
                pe.transpose(bank[4][:, E_MOE * HB:E_MOE * (HB + 1)], b2_rows[:],
                             ident[0:E_MOE, 0:E_MOE]).then_inc(s_bt, 1)
                pe.wait_ge(s_ones, 1)
                pe.wait_ge(s_dg, 1)
                pe.matmul(bank[6][:, 0:TOPK * B], ones[0:B, :], diag[:].rearrange("p k b -> p (k b)"),
                          start=True, stop=True).then_inc(s_mix, 1)


def chosen_experts(core, pre, w, xt_hi, xt_lo, biases, mix, choice, next_qk, out):
    nc, x, ident, bank = core.nc, core.x, core.ident, core.bank
    hidden, out_t, back = bank[0:4], bank[4:6], bank[6:8]
    with ExitStack() as ctx:
        def sb(name, shape, dt=F32):
            return core.sb(f"{pre}_{name}", shape, dt, ctx)

        def sem(name):
            return core.sem(f"{pre}x_{name}")

        w1 = sb("w1", [P, 2, TOPK, HID])
        w2 = sb("w2", [P, 2, TOPK, HB, D])
        bias = sb("bias", [P, 2, TOPK, HB + 1])
        w1_hi, w1_lo = sb("w1_hi", [P, TOPK, HID], F32R), sb("w1_lo", [P, TOPK, HID], F32R)
        w2_hi, w2_lo = sb("w2_hi", [P, TOPK, HB * D], F32R), sb("w2_lo", [P, TOPK, HB * D], F32R)
        b2_mix = sb("b2_mix", [P, 2, 2])
        hid = sb("hid", [P, TOPK, HB, T])
        hid_hi = sb("hid_hi", [P, TOPK, HB, T], F32R)
        hid_lo = sb("hid_lo", [P, TOPK, HB, T], F32R)
        y_t = sb("y_t", [P, 2, T])
        s_w = [[sem(f"seq{s}_expert{k}_in") for k in range(TOPK)] for s in range(2)]
        s_bias = [sem("biases0_in"), sem("biases1_in")]
        s_w1h, s_w1l, s_w2h, s_w2l = sem("w1_hi"), sem("w1_lo"), sem("w2_hi"), sem("w2_lo")
        s_seen, s_stat = sem("w1_seen"), sem("stats")
        s_qk, s_out = sem("next_qk_in"), sem("stored")
        s_b2p, s_b2 = sem("b2_part"), sem("b2_mixed")
        s_h, s_g, s_hh, s_hl = sem("hidden"), sem("gelu"), sem("hid_hi"), sem("hid_lo")
        s_y, s_yc, s_bk, s_x = sem("out_summed"), sem("out_copied"), sem("turned_back"), sem("x_added")

        def loaded(b, s):
            return 16 * (b - s) + 32

        def steps(first, step, last, loop):
            first()
            with loop(0, B // 2 - 1) as i:
                step(2 * i + 1, 1)
                step(2 * i + 2, 0)
            step(B - 1, 1)
            last()

        with nc.Block() as block:
            @block.sync
            def _(sp):
                def experts_of(b):
                    return [sp.value_load(choice[0:1, bass.ds(8 * b + k, 1)], min_val=0, max_val=E_MOE - 1)
                            for k in range(TOPK)]

                def load_weights(experts, s):
                    for k, e in enumerate(experts):
                        sp.dma_start(w1[:, s, k], w["w1"][e]).then_inc(s_w[s][k], 16)
                        sp.dma_start(w2[:, s, k], w["w2"][e].rearrange("(k p) d -> p k d", p=P)).then_inc(s_w[s][k], 16)

                def load_biases(experts, s):
                    for k, e in enumerate(experts):
                        sp.dma_start(bias[:, s, k], biases[:, e]).then_inc(s_bias[s], 16)

                for b in range(2):
                    experts = experts_of(b)
                    load_weights(experts, b)
                    load_biases(experts, b)
                if next_qk:
                    load_qk(sp, core, next_qk, s_qk)
                with sp.Fori(1, B // 2) as i:
                    for s in range(2):
                        b = 2 * i + s
                        experts = experts_of(b)
                        sp.wait_ge(s_w1l, TOPK * (b - 1))
                        sp.wait_ge(s_w2l, TOPK * (b - 1))
                        load_weights(experts, s)
                        sp.wait_ge(s_yc, b)
                        load_biases(experts, s)
                if next_qk:
                    sp.wait_ge(s_qk, 32)
                if out is not None:
                    with sp.Fori(0, B) as b:
                        sp.wait_ge(s_x, 2 + b + 1)
                        sp.dma_start(out[:, bass.ts(b, TT)], x[:, bass.ts(b, TT)]).then_inc(s_out, 16)
                    sp.wait_ge(s_out, 16 * B)

            @block.gpsimd
            def _(pool):
                def split_w1(b, s, k):
                    j = TOPK * b + k
                    pool.wait_ge(s_w[s][k], loaded(b, s))
                    if not isinstance(b, int) or b > 0:
                        pool.wait_ge(s_h, HB * (j - 1))
                    pool.sem_inc(s_seen, 1)
                    nc.gpsimd.tensor_copy(w1_hi[:, k], w1[:, s, k]).then_inc(s_w1h, 1)
                    pool.wait_ge(s_w1h, j + 1)
                    nc.gpsimd.tensor_tensor(w1_lo[:, k], w1[:, s, k], w1_hi[:, k].bitcast(F32),
                                            ALU.subtract).then_inc(s_w1l, 1)

                def step(b, s):
                    split_w1(b, s, 0)
                    split_w1(b, s, 1)

                steps(lambda: step(0, 0), step, lambda: None, pool.Fori)

            @block.tensor
            def _(pe):
                def first_layer(b, k):
                    j = TOPK * b + k
                    pe.wait_ge(s_w1l, j + 1)
                    for c in range(HB):
                        if not (isinstance(j, int) and j == 0):
                            pe.wait_ge(s_g, HB * (j - 1) + c + 1)
                        cols = slice(P * c, P * c + P)
                        pe.matmul(hidden[c][:], w1_hi[:, k, cols], xt_hi[:, b], start=True, stop=False)
                        pe.matmul(hidden[c][:], w1_hi[:, k, cols], xt_lo[:, b], start=False, stop=False)
                        pe.matmul(hidden[c][:], w1_lo[:, k, cols], xt_hi[:, b], start=False,
                                  stop=True).then_inc(s_h, 1)

                def second_layer(b, s, k):
                    j = TOPK * b + k
                    pe.wait_ge(s_w2l, j + 1)
                    if k == 0 and not (isinstance(b, int) and b == 0):
                        pe.wait_ge(s_yc, b)
                    for c in range(HB):
                        pe.wait_ge(s_hh, HB * j + c + 1)
                        cols = slice(P * c, P * c + P)
                        pe.matmul(out_t[s][:], w2_hi[:, k, cols], hid_hi[:, k, c], start=k == 0 and c == 0,
                                  stop=False)
                        pe.matmul(out_t[s][:], w2_lo[:, k, cols], hid_hi[:, k, c], start=False, stop=False)
                        pe.wait_ge(s_hl, HB * j + c + 1)
                        ins = pe.matmul(out_t[s][:], w2_hi[:, k, cols], hid_lo[:, k, c], start=False,
                                        stop=k == 1 and c == HB - 1)
                    ins.then_inc(s_y, 1)

                def turn_back(b, s):
                    pe.wait_ge(s_yc, 1 + b + 1)
                    pe.wait_ge(s_x, b + 1)
                    for t in range(TT):
                        ins = pe.transpose(back[s][:, P * t:P * t + P], y_t[:, s, P * t:P * t + P], ident[:])
                    ins.then_inc(s_bk, 1)

                def first():
                    first_layer(0, 0)
                    first_layer(0, 1)
                    second_layer(0, 0, 0)

                def step(b, s):
                    first_layer(b, 0)
                    second_layer(b - 1, 1 - s, 1)
                    first_layer(b, 1)
                    turn_back(b - 1, 1 - s)
                    second_layer(b, s, 0)

                def last():
                    second_layer(B - 1, 1, 1)
                    turn_back(B - 1, 1)

                pe.sem_inc(s_bk, 2)
                steps(first, step, last, pe.Fori)

            @block.scalar
            def _(act):
                def gelus(b, s, k):
                    j = TOPK * b + k
                    if not isinstance(b, int) or b > 0:
                        act.wait_ge(s_y, j - 1)
                    if k == 0:
                        act.wait_ge(s_bias[s], loaded(b, s))
                    for c in range(HB + 1):
                        if c < HB:
                            act.wait_ge(s_h, HB * j + c + 1)
                            nc.scalar.activation(hid[:, k, c], hidden[c][:], ACT.Gelu, bias=bias[:, s, k, c:c + 1],
                                                 scale=1.0).then_inc(s_g, 1)
                        if c > 0:
                            act.wait_ge(s_g, HB * j + c)
                            nc.scalar.copy(hid_hi[:, k, c - 1], hid[:, k, c - 1]).then_inc(s_hh, 1)

                def copy_out(b, s):
                    act.wait_ge(s_y, TOPK * (b + 1))
                    act.wait_ge(s_b2, b + 1)
                    act.wait_ge(s_bk, b + 1)
                    nc.scalar.activation(y_t[:, s], out_t[s][:], ACT.Identity, bias=b2_mix[:, s, 1:2],
                                         scale=1.0).then_inc(s_yc, 1)

                def first():
                    gelus(0, 0, 0)
                    gelus(0, 0, 1)

                def step(b, s):
                    gelus(b, s, 0)
                    copy_out(b - 1, 1 - s)
                    gelus(b, s, 1)

                start_at_one(act, s_yc)
                steps(first, step, lambda: copy_out(B - 1, 1), act.Fori)

            @block.vector
            def _(dve):
                def weight_of(b, k):
                    return mix[:, bass.ds(B * k + b, 1)]

                def split_w2(b, s, k):
                    j = TOPK * b + k
                    flat = w2[:, s, k].rearrange("p c d -> p (c d)")
                    dve.wait_ge(s_w[s][k], loaded(b, s))
                    if not isinstance(b, int) or b > 0:
                        dve.wait_ge(s_y, j - 1)
                    nc.vector.tensor_scalar(w2_hi[:, k], flat, weight_of(b, k), None, ALU.mult).then_inc(s_w2h, 1)
                    dve.wait_ge(s_w2h, j + 1)
                    nc.vector.scalar_tensor_tensor(out=w2_lo[:, k], in0=flat, scalar=weight_of(b, k),
                                                   in1=w2_hi[:, k].bitcast(F32), op0=ALU.mult,
                                                   op1=ALU.subtract).then_inc(s_w2l, 1)

                def mix_b2(b, s):
                    dve.wait_ge(s_bias[s], loaded(b, s))
                    if not isinstance(b, int) or b > 0:
                        dve.wait_ge(s_yc, b)
                    nc.vector.tensor_scalar(b2_mix[:, s, 0:1], bias[:, s, 0, HB:HB + 1], weight_of(b, 0), None,
                                            ALU.mult).then_inc(s_b2p, 1)
                    dve.wait_ge(s_b2p, b + 1)
                    nc.vector.scalar_tensor_tensor(out=b2_mix[:, s, 1:2], in0=bias[:, s, 1, HB:HB + 1],
                                                   scalar=weight_of(b, 1), in1=b2_mix[:, s, 0:1], op0=ALU.mult,
                                                   op1=ALU.add).then_inc(s_b2, 1)

                def remainders(b, k):
                    for c in range(HB):
                        dve.wait_ge(s_hh, HB * (TOPK * b + k) + c + 1)
                        nc.vector.tensor_tensor(hid_lo[:, k, c], hid[:, k, c], hid_hi[:, k, c].bitcast(F32),
                                                ALU.subtract).then_inc(s_hl, 1)

                def add_out(b, s):
                    dve.wait_ge(s_bk, 2 + b + 1)
                    rows = x[:, bass.ts(b, TT)].rearrange("p t d -> p (t d)")
                    nc.vector.tensor_tensor(rows, rows, back[s][:], ALU.add).then_inc(s_x, 1)
                    if out is None:
                        dve.wait_ge(s_x, 2 + b + 1)
                        for t in range(TT):
                            k = TT * b + t
                            nc.vector.bn_stats(core.tile_stats[:, k], x[:, k]).then_inc(s_stat, 1)

                def first():
                    split_w2(0, 0, 0)
                    remainders(0, 0)
                    split_w2(0, 0, 1)
                    mix_b2(0, 0)
                    remainders(0, 1)

                def step(b, s):
                    split_w2(b, s, 0)
                    remainders(b, 0)
                    split_w2(b, s, 1)
                    mix_b2(b, s)
                    remainders(b, 1)
                    add_out(b - 1, 1 - s)

                dve.sem_inc(s_x, 2)
                steps(first, step, lambda: add_out(B - 1, 1), dve.Fori)


def load_stream(core, tokens, identity):
    PARTS = 4
    part = NT // PARTS
    s_part = [core.sem(f"x{i}_in") for i in range(PARTS)]
    s_ident, s_stat = core.sem("identity_in"), core.sem("x_stats")
    with core.nc.Block() as block:
        @block.sync
        def _(sp):
            for i in range(PARTS):
                tiles = slice(part * i, part * (i + 1))
                sp.dma_start(core.x[:, tiles], tokens[:, tiles]).then_inc(s_part[i], 16)
            sp.dma_start(core.ident[:], identity).then_inc(s_ident, 16)
            sp.wait_ge(s_ident, 16)

        @block.vector
        def _(dve):
            for i in range(PARTS):
                dve.wait_ge(s_part[i], 16)
                for k in range(part * i, part * (i + 1)):
                    core.nc.vector.bn_stats(core.tile_stats[:, k], core.x[:, k]).then_inc(s_stat, 1)
    core.stats_fresh = True
    core.end_phase()


def build(nc, a, out):
    with ExitStack() as ctx:
        core = Core(nc, ctx)
        as_tiles = "b (i p) d -> p (b i) d"
        load_stream(core, a["L0_attn_x"].rearrange(as_tiles, p=P), a["identity"])

        soft = {k: a["L0_ffn_" + k] for k in
                ("norm_gamma", "slot_norm_gamma", "slot_embeds", "w1", "b1", "w2", "b2")}
        top = {k: a["L1_ffn_" + k] for k in ("gate_w", "w1", "b1", "w2", "b2")}
        qk = (a["L0_attn_w_qkv"][:, 0:H * DH], a["L0_attn_w_qkv"][:, H * DH:2 * H * DH])
        soft_moe(core, "s1", soft, qk)
        attention(core, "a1", {"qkv": a["L0_attn_w_qkv"], "out": a["L0_attn_w_out"], "b_out": a["L0_attn_b_out"],
                               "rel": a["distance"], "slopes": a["slopes"]}, True)
        soft_moe(core, "s2", soft)
        qk = (a["L1_attn_w_q"], a["L1_attn_w_kv_up"][:, 0:H * DH])
        top_moe(core, "t1", top, qk)
        attention(core, "a2", {"kv_up": a["L1_attn_w_kv_up"], "kv_down": a["L1_attn_w_kv_down"],
                               "out": a["L1_attn_w_out"], "rel": a["causal"]}, False)
        top_moe(core, "t2", top, out=out.rearrange(as_tiles, p=P))


def constants():
    gap = np.arange(T)[None, :] - (T - P) - np.arange(P)[:, None]
    return {
        "distance": np.where(gap <= 0, gap, MASKED).astype(np.float32),
        "causal": np.where(gap <= 0, 0.0, MASKED).astype(np.float32),
        "slopes": np.tile(alibi_slopes(), (P, 1)),
        "identity": np.eye(P, dtype=np.float32),
    }


def kernel(**inputs):
    import concourse.bacc as bacc
    from concourse.bass_utils import run_bass_kernel_spmd

    nc = bacc.Bacc("TRN2", target_bir_lowering=False, num_devices=1)
    arrays, args = {}, {}
    for name, value in {**inputs, **constants()}.items():
        value = np.ascontiguousarray(value)
        arrays[f"in_{name}"] = value
        args[name] = nc.dram_tensor(f"in_{name}", value.shape, mybir.dt.from_np(value.dtype),
                                    kind="ExternalInput").ap()
    out = nc.dram_tensor("out", (B, T, D), F32, kind="ExternalOutput").ap()
    build(nc, args, out)
    result = run_bass_kernel_spmd(nc, [arrays], core_ids=[0])
    return result.results[0]["out"]
```
